# Optimizing a Trainium2 kernel written in Bass

```python
import numpy as np
import jax
import jax.numpy as jnp

def _softmax(x, axis=-1):
    return jax.nn.softmax(x, axis=axis)

def _gelu(x):
    return jax.nn.gelu(x, approximate=True)

def _silu(x):
    return jax.nn.silu(x)

def _sigmoid(x):
    return jax.nn.sigmoid(x)

def _layernorm(x, axis=-1, eps=1e-05):
    m = jnp.mean(x, axis=axis, keepdims=True)
    v = jnp.var(x, axis=axis, keepdims=True)
    return (x - m) / jnp.sqrt(v + eps)

def _scatter_add(tgt, idx, src, axis=0):
    return tgt.at[idx].add(src)

def _segment_sum(src, seg, n):
    return jax.ops.segment_sum(src, seg, n)
kernel_name = 'mk_vit_tower_postln_d4_tok_img768_r4_caa705'

def setup_inputs(seed: int=0):
    np.random.seed(seed)
    _w = jnp.asarray

    def _rec_inputs():
        import jax
        import jax.numpy as jnp
        _rk = jax.random.key(seed)
        x = -0.000222058 + 0.999998 * jax.random.normal(jax.random.fold_in(_rk, 1), (32, 3, 112, 112), jnp.float32)
        return x
    x = _rec_inputs()

    def _L0_tok_setup():
        import jax, jax.numpy as jnp
        import numpy as np
        from jax import lax
        HIDDEN = 192
        C_IN = 3
        PATCH = 16
        SIDE = 32
        NUM_PATCHES = SIDE * SIDE

        def _position_ids(nb_h, nb_w):
            boundaries = np.arange(1.0 / SIDE, 1.0, 1.0 / SIDE, dtype=np.float32)
            frac_h = np.arange(0.0, 1.0 - 1e-06, 1.0 / nb_h, dtype=np.float32)
            frac_w = np.arange(0.0, 1.0 - 1e-06, 1.0 / nb_w, dtype=np.float32)
            bh = np.searchsorted(boundaries, frac_h, side='right')
            bw = np.searchsorted(boundaries, frac_w, side='right')
            return jnp.asarray((bh[:, None] * SIDE + bw).reshape(-1), dtype=jnp.int32)
        key = jax.random.key(seed)
        k1, k2, k3 = jax.random.split(key, 3)
        pixel_values = jax.random.normal(k1, (32, C_IN, 128, 128), dtype=jnp.float32)
        conv_w = jax.random.normal(k2, (HIDDEN, C_IN, PATCH, PATCH), dtype=jnp.float32) * 0.02
        conv_b = jnp.zeros((HIDDEN,), dtype=jnp.float32)
        pos_table = jax.random.normal(k3, (NUM_PATCHES, HIDDEN), dtype=jnp.float32) * 0.02
        return {'pixel_values': pixel_values, 'conv_w': conv_w, 'conv_b': conv_b, 'pos_table': pos_table}
    _L0_tok_all = _L0_tok_setup()
    _L0_tok_in = {k: v for k, v in _L0_tok_all.items() if k in ('conv_w', 'conv_b', 'pos_table')}
    del _L0_tok_all

    def _L0_attn_setup():
        import jax, jax.numpy as jnp
        import numpy as np
        HIDDEN = 192
        KV_DIM = HIDDEN // 3
        BATCH, SEQ = (2, 2048)
        THETA = 10000.0

        def rope_table(seq_len, dim):
            pos = jnp.arange(seq_len, dtype=jnp.float32)
            freqs = THETA ** (-jnp.arange(0, dim, 2, dtype=jnp.float32) / dim)
            ang = pos[:, None] * freqs[None, :]
            return jnp.concatenate([jnp.sin(ang), jnp.cos(ang)], axis=-1)[None]
        key = jax.random.key(seed)
        kx, kq, kk, kv, ko = jax.random.split(key, 5)
        s = 1.0 / np.sqrt(HIDDEN)
        return {'x': jax.random.normal(kx, (BATCH, SEQ, HIDDEN), dtype=jnp.float32), 'Wq': jax.random.uniform(kq, (HIDDEN, HIDDEN), jnp.float32, -s, s), 'Wk': jax.random.uniform(kk, (KV_DIM, HIDDEN), jnp.float32, -s, s), 'Wv': jax.random.uniform(kv, (KV_DIM, HIDDEN), jnp.float32, -s, s), 'Wo': jax.random.uniform(ko, (HIDDEN, KV_DIM), jnp.float32, -s, s)}
    _L0_attn_all = _L0_attn_setup()
    _L0_attn_in = {k: v for k, v in _L0_attn_all.items() if k in ('Wq', 'Wk', 'Wv', 'Wo')}
    del _L0_attn_all

    def _L0_ffn_setup():
        import jax, jax.numpy as jnp
        import numpy as np
        E, TOPK = (32, 2)
        D, HID, BOT, OUT = (192, 512, 64, 192)
        B, S = (2, 128)
        key = jax.random.key(seed)
        ks = jax.random.split(key, 7)
        p = lambda k, shape: jax.random.normal(k, shape, dtype=jnp.float32) * 0.02
        return {'x': jax.random.normal(ks[0], (B, S, D), dtype=jnp.float32), 'gate_w': p(ks[1], (E, D)), 'W1': p(ks[2], (E, D, HID)), 'b1': jnp.zeros((E, HID), jnp.float32), 'W2': p(ks[3], (E, HID, HID)), 'b2': jnp.zeros((E, HID), jnp.float32), 'W3': p(ks[4], (E, HID, BOT)), 'b3': jnp.zeros((E, BOT), jnp.float32), 'Wl': p(ks[5], (E, BOT, OUT)), 'bl': jnp.zeros((E, OUT), jnp.float32)}
    _L0_ffn_all = _L0_ffn_setup()
    _L0_ffn_in = {k: v for k, v in _L0_ffn_all.items() if k in ('gate_w', 'W1', 'b1', 'W2', 'b2', 'W3', 'b3', 'Wl', 'bl')}
    del _L0_ffn_all

    def _L1_attn_setup():
        import jax, jax.numpy as jnp
        import numpy as np
        N_HEAD = 12
        key = jax.random.key(seed)
        ks = jax.random.split(key, 5)
        C = 192
        B, T = (2, 512)
        s = 0.02
        x = jax.random.normal(ks[0], (B, T, C), dtype=jnp.float32)
        W_attn = jax.random.normal(ks[1], (C, 3 * C), dtype=jnp.float32) * s
        b_attn = jnp.zeros((3 * C,), dtype=jnp.float32)
        W_proj = jax.random.normal(ks[2], (C, C), dtype=jnp.float32) * s
        b_proj = jnp.zeros((C,), dtype=jnp.float32)
        return {'x': x, 'W_attn': W_attn, 'b_attn': b_attn, 'W_proj': W_proj, 'b_proj': b_proj}
    _L1_attn_all = _L1_attn_setup()
    _L1_attn_in = {k: v for k, v in _L1_attn_all.items() if k in ('W_attn', 'b_attn', 'W_proj', 'b_proj')}
    del _L1_attn_all

    def _L1_ffn_setup():
        import jax, jax.numpy as jnp
        import numpy as np
        D_MODEL = 192
        D_FF = 768
        N_EXPERTS = 9
        key = jax.random.key(seed)
        ks = jax.random.split(key, 7)
        scale = 0.02
        return {'x': jax.random.normal(ks[0], (2, 256, D_MODEL), jnp.float32), 'Ws': jax.random.normal(ks[1], (D_MODEL, N_EXPERTS), jnp.float32) * scale, 'bs': jnp.zeros((N_EXPERTS,), jnp.float32), 'W1': jax.random.normal(ks[2], (N_EXPERTS, D_MODEL, D_FF), jnp.float32) * scale, 'b1': jnp.zeros((N_EXPERTS, D_FF), jnp.float32), 'W2': jax.random.normal(ks[3], (N_EXPERTS, D_FF, D_MODEL), jnp.float32) * scale, 'b2': jnp.zeros((N_EXPERTS, D_MODEL), jnp.float32)}
    _L1_ffn_all = _L1_ffn_setup()
    _L1_ffn_in = {k: v for k, v in _L1_ffn_all.items() if k in ('Ws', 'bs', 'W1', 'b1', 'W2', 'b2')}
    del _L1_ffn_all

    def _L2_attn_setup():
        import jax, jax.numpy as jnp
        import numpy as np
        B, N, C = (64, 80, 192)
        NUM_HEADS = 12
        LENS_Z = 64
        SCALE = (C // NUM_HEADS) ** (-0.5)
        key = jax.random.key(seed)
        k1, k2, k3 = jax.random.split(key, 3)
        x = jax.random.normal(k1, (B, N, C), dtype=jnp.float32)
        proj_w = jax.random.normal(k2, (C, C), dtype=jnp.float32) * 0.02
        proj_b = jax.random.normal(k3, (C,), dtype=jnp.float32) * 0.02
        return {'x': x, 'proj_w': proj_w, 'proj_b': proj_b}
    _L2_attn_all = _L2_attn_setup()
    _L2_attn_in = {k: v for k, v in _L2_attn_all.items() if k in ('proj_w', 'proj_b')}
    del _L2_attn_all

    def _L2_ffn_setup():
        import jax, jax.numpy as jnp
        import numpy as np
        B, S, D_IN, D_HID, D_OUT = (32, 128, 192, 768, 192)
        key = jax.random.key(seed)
        k1, k2, k3, k4 = jax.random.split(key, 4)
        init_k = float(np.sqrt(1.0 / D_IN))
        init_k2 = float(np.sqrt(1.0 / D_HID))
        x = jax.random.normal(k1, (B, S, D_IN), dtype=jnp.float32)
        in_weight = jax.random.uniform(k2, (D_HID, D_IN), dtype=jnp.float32, minval=-init_k, maxval=init_k)
        in_bias = jax.random.uniform(k3, (D_HID,), dtype=jnp.float32, minval=-init_k, maxval=init_k)
        out_weight = jax.random.uniform(k4, (D_HID, D_OUT), dtype=jnp.float32, minval=-init_k2, maxval=init_k2)
        return {'x': x, 'in_weight': in_weight, 'in_bias': in_bias, 'out_weight': out_weight}
    _L2_ffn_all = _L2_ffn_setup()
    _L2_ffn_in = {k: v for k, v in _L2_ffn_all.items() if k in ('in_weight', 'in_bias', 'out_weight')}
    del _L2_ffn_all

    def _L3_attn_setup():
        import jax, jax.numpy as jnp
        import numpy as np
        D_MODEL = 192
        H = 6
        DQK = 128
        DV = 64
        SCALE_BASE = 512.0

        def _xpos(x, sign):
            B, T, Hn, d = x.shape
            half = d // 2
            pos = jnp.arange(T, dtype=jnp.float32)
            inv_freq = 1.0 / 10000.0 ** (jnp.arange(half, dtype=jnp.float32) / half)
            angles = pos[:, None] * inv_freq[None, :]
            zeta = (jnp.arange(half, dtype=jnp.float32) + half) / d
            decay = zeta[None, :] ** (sign * pos[:, None] / SCALE_BASE)
            cos_a = (jnp.cos(angles) * decay)[None, :, None, :]
            sin_a = (jnp.sin(angles) * decay)[None, :, None, :]
            x1, x2 = (x[..., :half], x[..., half:])
            return jnp.concatenate([x1 * cos_a - x2 * sin_a, x1 * sin_a + x2 * cos_a], axis=-1)

        def _decay_mask(T):
            gammas = jnp.array([1.0 - 2.0 ** (-(5 + h)) for h in range(H)], dtype=jnp.float32)
            i = jnp.arange(T, dtype=jnp.float32)
            diff = i[:, None] - i[None, :]
            causal = (diff >= 0).astype(jnp.float32)
            D = gammas[:, None, None] ** jnp.clip(diff, 0.0)[None] * causal[None]
            row = jnp.clip(jnp.sum(D, axis=-1, keepdims=True), 1e-06)
            return D / jnp.sqrt(row)
        key = jax.random.key(seed)
        ks = jax.random.split(key, 6)
        B, T = (2, 512)

        def xavier(k, shape):
            lim = float(np.sqrt(6.0 / (shape[0] + shape[1])))
            return jax.random.uniform(k, shape, jnp.float32, -lim, lim)
        return {'x': jax.random.normal(ks[0], (B, T, D_MODEL), jnp.float32), 'Wq': xavier(ks[1], (D_MODEL, H * DQK)), 'Wk': xavier(ks[2], (D_MODEL, H * DQK)), 'Wv': xavier(ks[3], (D_MODEL, H * DV)), 'Wg': xavier(ks[4], (D_MODEL, H * DV)), 'Wo': xavier(ks[5], (H * DV, D_MODEL)), 'gn_weight': jnp.ones((H * DV,), jnp.float32), 'gn_bias': jnp.zeros((H * DV,), jnp.float32)}
    _L3_attn_all = _L3_attn_setup()
    _L3_attn_in = {k: v for k, v in _L3_attn_all.items() if k in ('Wq', 'Wk', 'Wv', 'Wg', 'Wo', 'gn_weight', 'gn_bias')}
    del _L3_attn_all

    def _L3_ffn_setup():
        import jax, jax.numpy as jnp
        import numpy as np
        D_MODEL = 192
        D_FF = 768
        NUM_EXPERTS = 8
        EXPERT_CAPACITY = 256
        key = jax.random.key(seed)
        k0, k1, k2, k3 = jax.random.split(key, 4)
        hidden_states = jax.random.normal(k0, (2, 256, D_MODEL), dtype=jnp.float32)
        router_w = jax.random.normal(k1, (D_MODEL, NUM_EXPERTS), dtype=jnp.float32) * D_MODEL ** (-0.5)
        wi = jax.random.normal(k2, (NUM_EXPERTS, D_MODEL, D_FF), dtype=jnp.float32) * D_MODEL ** (-0.5)
        wo = jax.random.normal(k3, (NUM_EXPERTS, D_FF, D_MODEL), dtype=jnp.float32) * D_FF ** (-0.5)
        return {'hidden_states': hidden_states, 'router_w': router_w, 'wi': wi, 'wo': wo}
    _L3_ffn_all = _L3_ffn_setup()
    _L3_ffn_in = {k: v for k, v in _L3_ffn_all.items() if k in ('router_w', 'wi', 'wo')}
    del _L3_ffn_all
    return {'x': x, 'L0_tok_conv_w': _L0_tok_in['conv_w'], 'L0_tok_conv_b': _L0_tok_in['conv_b'], 'L0_tok_pos_table': _L0_tok_in['pos_table'], 'L0_attn_Wq': _L0_attn_in['Wq'], 'L0_attn_Wk': _L0_attn_in['Wk'], 'L0_attn_Wv': _L0_attn_in['Wv'], 'L0_attn_Wo': _L0_attn_in['Wo'], 'L0_ffn_gate_w': _L0_ffn_in['gate_w'], 'L0_ffn_W1': _L0_ffn_in['W1'], 'L0_ffn_b1': _L0_ffn_in['b1'], 'L0_ffn_W2': _L0_ffn_in['W2'], 'L0_ffn_b2': _L0_ffn_in['b2'], 'L0_ffn_W3': _L0_ffn_in['W3'], 'L0_ffn_b3': _L0_ffn_in['b3'], 'L0_ffn_Wl': _L0_ffn_in['Wl'], 'L0_ffn_bl': _L0_ffn_in['bl'], 'L1_attn_W_attn': _L1_attn_in['W_attn'], 'L1_attn_b_attn': _L1_attn_in['b_attn'], 'L1_attn_W_proj': _L1_attn_in['W_proj'], 'L1_attn_b_proj': _L1_attn_in['b_proj'], 'L1_ffn_Ws': _L1_ffn_in['Ws'], 'L1_ffn_bs': _L1_ffn_in['bs'], 'L1_ffn_W1': _L1_ffn_in['W1'], 'L1_ffn_b1': _L1_ffn_in['b1'], 'L1_ffn_W2': _L1_ffn_in['W2'], 'L1_ffn_b2': _L1_ffn_in['b2'], 'L2_attn_proj_w': _L2_attn_in['proj_w'], 'L2_attn_proj_b': _L2_attn_in['proj_b'], 'L2_ffn_in_weight': _L2_ffn_in['in_weight'], 'L2_ffn_in_bias': _L2_ffn_in['in_bias'], 'L2_ffn_out_weight': _L2_ffn_in['out_weight'], 'L3_attn_Wq': _L3_attn_in['Wq'], 'L3_attn_Wk': _L3_attn_in['Wk'], 'L3_attn_Wv': _L3_attn_in['Wv'], 'L3_attn_Wg': _L3_attn_in['Wg'], 'L3_attn_Wo': _L3_attn_in['Wo'], 'L3_attn_gn_weight': _L3_attn_in['gn_weight'], 'L3_attn_gn_bias': _L3_attn_in['gn_bias'], 'L3_ffn_router_w': _L3_ffn_in['router_w'], 'L3_ffn_wi': _L3_ffn_in['wi'], 'L3_ffn_wo': _L3_ffn_in['wo']}

def reference(x, L0_tok_conv_w, L0_tok_conv_b, L0_tok_pos_table, L0_attn_Wq, L0_attn_Wk, L0_attn_Wv, L0_attn_Wo, L0_ffn_gate_w, L0_ffn_W1, L0_ffn_b1, L0_ffn_W2, L0_ffn_b2, L0_ffn_W3, L0_ffn_b3, L0_ffn_Wl, L0_ffn_bl, L1_attn_W_attn, L1_attn_b_attn, L1_attn_W_proj, L1_attn_b_proj, L1_ffn_Ws, L1_ffn_bs, L1_ffn_W1, L1_ffn_b1, L1_ffn_W2, L1_ffn_b2, L2_attn_proj_w, L2_attn_proj_b, L2_ffn_in_weight, L2_ffn_in_bias, L2_ffn_out_weight, L3_attn_Wq, L3_attn_Wk, L3_attn_Wv, L3_attn_Wg, L3_attn_Wo, L3_attn_gn_weight, L3_attn_gn_bias, L3_ffn_router_w, L3_ffn_wi, L3_ffn_wo):
    import jax
    import jax.numpy as jnp

    def _L0_tok_ref(pixel_values, conv_w, conv_b, pos_table):
        import jax, jax.numpy as jnp
        import numpy as np
        from jax import lax
        HIDDEN = 192
        C_IN = 3
        PATCH = 16
        SIDE = 32
        NUM_PATCHES = SIDE * SIDE

        def _position_ids(nb_h, nb_w):
            boundaries = np.arange(1.0 / SIDE, 1.0, 1.0 / SIDE, dtype=np.float32)
            frac_h = np.arange(0.0, 1.0 - 1e-06, 1.0 / nb_h, dtype=np.float32)
            frac_w = np.arange(0.0, 1.0 - 1e-06, 1.0 / nb_w, dtype=np.float32)
            bh = np.searchsorted(boundaries, frac_h, side='right')
            bw = np.searchsorted(boundaries, frac_w, side='right')
            return jnp.asarray((bh[:, None] * SIDE + bw).reshape(-1), dtype=jnp.int32)
        B, _, H, W = pixel_values.shape
        nb_h, nb_w = (H // PATCH, W // PATCH)
        patches = lax.conv_general_dilated(pixel_values, conv_w, window_strides=(PATCH, PATCH), padding='VALID', dimension_numbers=('NCHW', 'OIHW', 'NCHW'))
        patches = patches + conv_b[None, :, None, None]
        embeddings = patches.reshape(B, HIDDEN, nb_h * nb_w).transpose(0, 2, 1)
        pos_ids = _position_ids(nb_h, nb_w)
        pos_emb = pos_table[pos_ids]
        return embeddings + pos_emb[None, :, :]

    def _L0_attn_ref(x, Wq, Wk, Wv, Wo):
        import jax, jax.numpy as jnp
        import numpy as np
        HIDDEN = 192
        KV_DIM = HIDDEN // 3
        BATCH, SEQ = (2, 2048)
        THETA = 10000.0

        def rope_table(seq_len, dim):
            pos = jnp.arange(seq_len, dtype=jnp.float32)
            freqs = THETA ** (-jnp.arange(0, dim, 2, dtype=jnp.float32) / dim)
            ang = pos[:, None] * freqs[None, :]
            return jnp.concatenate([jnp.sin(ang), jnp.cos(ang)], axis=-1)[None]
        B, S, H = x.shape
        q = jnp.einsum('bsh,oh->bso', x, Wq)
        k = jnp.einsum('bsh,oh->bso', x, Wk)
        v = jnp.einsum('bsh,oh->bso', x, Wv)
        r = rope_table(S, H)
        attn_weights = jnp.matmul(r, jnp.swapaxes(r, -2, -1))
        attn_probs = jax.nn.softmax(attn_weights, axis=-1)
        attn_output = jnp.matmul(attn_probs, v)
        out = jnp.einsum('bsk,ok->bso', attn_output, Wo)
        return out

    def _L0_ffn_ref(x, gate_w, W1, b1, W2, b2, W3, b3, Wl, bl):
        import jax, jax.numpy as jnp
        import numpy as np
        E, TOPK = (32, 2)
        D, HID, BOT, OUT = (192, 512, 64, 192)
        B, S = (2, 128)
        Bz, Sl, d = x.shape
        xt = x.reshape(-1, d)
        scores = jax.nn.softmax(xt @ gate_w.T, axis=-1)
        topk_w, topk_idx = jax.lax.top_k(scores, TOPK)
        topk_w = topk_w / (topk_w.sum(-1, keepdims=True) + 1e-20)
        gelu = lambda v: jax.nn.gelu(v, approximate=False)
        h = gelu(jnp.einsum('nd,edh->enh', xt, W1) + b1[:, None, :])
        h = gelu(jnp.einsum('enh,ehg->eng', h, W2) + b2[:, None, :])
        z = jnp.einsum('eng,egb->enb', h, W3) + b3[:, None, :]
        out_all = jnp.einsum('enb,ebo->eno', z, Wl) + bl[:, None, :]
        sel = jnp.take_along_axis(out_all.transpose(1, 0, 2), topk_idx[:, :, None], axis=1)
        y = (sel * topk_w[:, :, None]).sum(axis=1)
        return y.reshape(Bz, Sl, OUT)

    def _L1_attn_ref(x, W_attn, b_attn, W_proj, b_proj):
        import jax, jax.numpy as jnp
        import numpy as np
        N_HEAD = 12
        B, T, C = x.shape
        H = N_HEAD
        hs = C // H
        qkv = x @ W_attn + b_attn
        q, k, v = jnp.split(qkv, 3, axis=2)
        q = q.reshape(B, T, H, hs).transpose(0, 2, 1, 3)
        k = k.reshape(B, T, H, hs).transpose(0, 2, 1, 3)
        v = v.reshape(B, T, H, hs).transpose(0, 2, 1, 3)
        scale = 1.0 / np.sqrt(hs).astype(np.float32)
        att = jnp.einsum('bhqd,bhkd->bhqk', q, k) * scale
        causal = jnp.tril(jnp.ones((T, T), dtype=bool))
        att = jnp.where(causal, att, -jnp.inf)
        att = jax.nn.softmax(att, axis=-1)
        y = jnp.einsum('bhqk,bhkd->bhqd', att, v)
        y = y.transpose(0, 2, 1, 3).reshape(B, T, C)
        return y @ W_proj + b_proj

    def _L1_ffn_ref(x, Ws, bs, W1, b1, W2, b2):
        import jax, jax.numpy as jnp
        import numpy as np
        D_MODEL = 192
        D_FF = 768
        N_EXPERTS = 9
        B, S, d = x.shape
        xt = x.reshape(-1, d)
        route_prob = jax.nn.softmax(xt @ Ws + bs, axis=-1)
        p = jnp.max(route_prob, axis=-1)
        routes = jnp.argmax(route_prob, axis=-1)
        h = jax.nn.gelu(jnp.einsum('td,edf->tef', xt, W1) + b1, approximate=False)
        out = jnp.einsum('tef,efd->ted', h, W2) + b2
        common = out[:, 0, :]
        sel = jnp.take_along_axis(out, routes[:, None, None], axis=1)[:, 0, :]
        scaling = (p / jax.lax.stop_gradient(p))[:, None]
        pe = p[:, None]
        final = jnp.where((routes == 0)[:, None], common * scaling, pe * sel + (1.0 - pe) * common)
        return final.reshape(B, S, d)

    def _L2_attn_ref(x, proj_w, proj_b):
        import jax, jax.numpy as jnp
        import numpy as np
        B, N, C = (64, 80, 192)
        NUM_HEADS = 12
        LENS_Z = 64
        SCALE = (C // NUM_HEADS) ** (-0.5)
        q = x[:, :LENS_Z]
        k = x[:, LENS_Z:]
        v = k
        attn = jnp.einsum('bqc,bkc->bqk', q, k) * SCALE
        attn = jax.nn.softmax(attn, axis=-1)
        out = jnp.einsum('bqk,bkc->bqc', attn, v)
        out = jnp.transpose(out, (0, 2, 1)).reshape(out.shape[0], -1, C)
        out = out @ proj_w.T + proj_b
        return jnp.concatenate([out, k], axis=1)

    def _L2_ffn_ref(x, in_weight, in_bias, out_weight):
        import jax, jax.numpy as jnp
        import numpy as np
        B, S, D_IN, D_HID, D_OUT = (32, 128, 192, 768, 192)
        lead = x.shape[:-1]
        xt = x.reshape(-1, in_weight.shape[1])
        h = jax.nn.gelu(jnp.einsum('td,hd->th', xt, in_weight) + in_bias, approximate=False)
        out = jnp.einsum('th,ho->to', h, out_weight)
        return out.reshape(*lead, out_weight.shape[1])

    def _L3_attn_ref(x, Wq, Wk, Wv, Wg, Wo, gn_weight, gn_bias):
        import jax, jax.numpy as jnp
        import numpy as np
        D_MODEL = 192
        H = 6
        DQK = 128
        DV = 64
        SCALE_BASE = 512.0

        def _xpos(x, sign):
            B, T, Hn, d = x.shape
            half = d // 2
            pos = jnp.arange(T, dtype=jnp.float32)
            inv_freq = 1.0 / 10000.0 ** (jnp.arange(half, dtype=jnp.float32) / half)
            angles = pos[:, None] * inv_freq[None, :]
            zeta = (jnp.arange(half, dtype=jnp.float32) + half) / d
            decay = zeta[None, :] ** (sign * pos[:, None] / SCALE_BASE)
            cos_a = (jnp.cos(angles) * decay)[None, :, None, :]
            sin_a = (jnp.sin(angles) * decay)[None, :, None, :]
            x1, x2 = (x[..., :half], x[..., half:])
            return jnp.concatenate([x1 * cos_a - x2 * sin_a, x1 * sin_a + x2 * cos_a], axis=-1)

        def _decay_mask(T):
            gammas = jnp.array([1.0 - 2.0 ** (-(5 + h)) for h in range(H)], dtype=jnp.float32)
            i = jnp.arange(T, dtype=jnp.float32)
            diff = i[:, None] - i[None, :]
            causal = (diff >= 0).astype(jnp.float32)
            D = gammas[:, None, None] ** jnp.clip(diff, 0.0)[None] * causal[None]
            row = jnp.clip(jnp.sum(D, axis=-1, keepdims=True), 1e-06)
            return D / jnp.sqrt(row)
        B, T, _ = x.shape
        Q = (x @ Wq).reshape(B, T, H, DQK)
        K = (x @ Wk).reshape(B, T, H, DQK)
        V = (x @ Wv).reshape(B, T, H, DV)
        Q = _xpos(Q, 1.0)
        K = _xpos(K, -1.0)
        scores = jnp.einsum('bihd,bjhd->bhij', Q, K) * DQK ** (-0.5)
        scores = scores * _decay_mask(T)[None]
        out = jnp.einsum('bhij,bjhv->bihv', scores, V)
        concat = out.reshape(B, T, H * DV)
        g = concat.transpose(0, 2, 1).reshape(B, H, DV, T)
        mean = jnp.mean(g, axis=(2, 3), keepdims=True)
        var = jnp.var(g, axis=(2, 3), keepdims=True)
        g = (g - mean) / jnp.sqrt(var + 1e-05)
        g = g.reshape(B, H * DV, T) * gn_weight[None, :, None] + gn_bias[None, :, None]
        normed = g.transpose(0, 2, 1)
        gate = jax.nn.silu(x @ Wg)
        return normed * gate @ Wo

    def _L3_ffn_ref(hidden_states, router_w, wi, wo):
        import jax, jax.numpy as jnp
        import numpy as np
        D_MODEL = 192
        D_FF = 768
        NUM_EXPERTS = 8
        EXPERT_CAPACITY = 256
        B, S, d = hidden_states.shape
        E = router_w.shape[1]
        x = hidden_states.reshape(-1, d)
        logits = x.astype(jnp.float32) @ router_w.astype(jnp.float32)
        probs = jax.nn.softmax(logits, axis=-1).astype(x.dtype)
        p = jnp.max(probs, axis=-1)
        e_idx = jnp.argmax(probs, axis=-1)
        mask = jax.nn.one_hot(e_idx, E, dtype=x.dtype)
        token_priority = jnp.cumsum(mask[:, None, :], axis=-2)[:, 0, :]
        mask = mask * (token_priority <= EXPERT_CAPACITY).astype(x.dtype)
        combine = mask * p[:, None]

        def body(acc, ew):
            Wi_e, Wo_e, w_e = ew
            h = jax.nn.relu(x @ Wi_e) @ Wo_e
            return (acc + w_e[:, None] * h, None)
        out, _ = jax.lax.scan(body, jnp.zeros_like(x), (wi, wo, combine.T))
        return out.reshape(B, S, d)
    h = _L0_tok_ref(x, L0_tok_conv_w, L0_tok_conv_b, L0_tok_pos_table)
    h = _layernorm(h + _L0_attn_ref(h, L0_attn_Wq, L0_attn_Wk, L0_attn_Wv, L0_attn_Wo), axis=-1)
    h = _layernorm(h + _L0_ffn_ref(h, L0_ffn_gate_w, L0_ffn_W1, L0_ffn_b1, L0_ffn_W2, L0_ffn_b2, L0_ffn_W3, L0_ffn_b3, L0_ffn_Wl, L0_ffn_bl), axis=-1)
    h = _layernorm(h + _L1_attn_ref(h, L1_attn_W_attn, L1_attn_b_attn, L1_attn_W_proj, L1_attn_b_proj), axis=-1)
    h = _layernorm(h + _L1_ffn_ref(h, L1_ffn_Ws, L1_ffn_bs, L1_ffn_W1, L1_ffn_b1, L1_ffn_W2, L1_ffn_b2), axis=-1)
    h = _layernorm(h + _L2_attn_ref(h, L2_attn_proj_w, L2_attn_proj_b), axis=-1)
    h = _layernorm(h + _L2_ffn_ref(h, L2_ffn_in_weight, L2_ffn_in_bias, L2_ffn_out_weight), axis=-1)
    h = _layernorm(h + _L3_attn_ref(h, L3_attn_Wq, L3_attn_Wk, L3_attn_Wv, L3_attn_Wg, L3_attn_Wo, L3_attn_gn_weight, L3_attn_gn_bias), axis=-1)
    h = _layernorm(h + _L3_ffn_ref(h, L3_ffn_router_w, L3_ffn_wi, L3_ffn_wo), axis=-1)
    return h

_drawn_inputs = setup_inputs


def setup_inputs(seed=0):
    import zlib

    import numpy as np

    out = dict(_drawn_inputs(seed))
    spreads = {'L0_tok_conv_b': (0.0, 0.1),
     'L0_ffn_b1': (0.0, 0.8),
     'L0_ffn_b2': (0.0, 0.561),
     'L0_ffn_b3': (0.0, 0.268),
     'L0_ffn_bl': (0.0, 0.1),
     'L1_attn_b_attn': (0.0, 0.1),
     'L1_attn_b_proj': (0.0, 0.1),
     'L1_ffn_bs': (0.0, 0.283),
     'L1_ffn_b1': (0.0, 0.1),
     'L1_ffn_b2': (0.0, 0.1),
     'L3_attn_gn_weight': (1.0, 0.2),
     'L3_attn_gn_bias': (0.0, 0.1)}
    factors = {'L0_ffn_W1': 5.245, 'L0_ffn_W2': 4.439, 'L0_ffn_W3': 3.532}
    for name, (base, spread) in spreads.items():
        noise = np.random.default_rng([zlib.crc32(name.encode()), seed]).standard_normal(out[name].shape)
        drawn = base * np.exp(spread * noise) if base else spread * noise
        out[name] = jnp.asarray(drawn.astype(out[name].dtype))
    for name, factor in factors.items():
        out[name] = (out[name] * factor).astype(out[name].dtype)
    return out
```

```python
from contextlib import ExitStack

import numpy as np

import concourse.bass as bass
from concourse import mybir

F32 = mybir.dt.float32
I32 = mybir.dt.int32
BF16 = mybir.dt.bfloat16
ALU = mybir.AluOpType
ACT = mybir.ActivationFunctionType
AX = mybir.AxisListType.X
ds = bass.ds

B, L = 32, 49
D, DH = 192, 96
TR = 2 * L
NT = B // 2
CT = 4
NCH = NT // CT
CW = CT * TR
CB = CW // L
NTOK = B * L
PK = 3 * 16 * 16 // 128
SLOT = 128
HEADS, HD = 12, 16
RH, RQK, RV = 6, 128, 64
FF = 768
FM = FF // 128
EPS = 1e-5
NEG = -1.0e30
PSB = 512


def max_tiles(experts, k):
    n = (NTOK * k - experts) // SLOT + experts
    return n + n % 2


MOE = {0: (32, 2), 1: (9, 1), 2: (8, 1)}
TMAX = max(max_tiles(*v) for v in MOE.values())
THR = (NTOK + SLOT - 1) // SLOT


def constants():
    c = {}
    c["ident"] = np.eye(128, dtype=np.float32)
    blk = np.kron(np.eye(2), np.ones((L, L)))
    c["image_block"] = blk.astype(np.float32)
    c["block_neg"] = np.where(blk > 0, 0.0, NEG).astype(np.float32)
    causal = np.kron(np.eye(2), np.tril(np.ones((L, L))))
    c["causal_neg"] = np.where(causal > 0, 0.0, NEG).astype(np.float32)
    pos = np.arange(L, dtype=np.float32)
    fr = (10000.0 ** (-np.arange(0, D, 2, dtype=np.float32) / D)).astype(np.float32)
    ang = (pos[:, None] * fr[None]).astype(np.float32).astype(np.float64)
    r = np.concatenate([np.sin(ang), np.cos(ang)], -1).astype(np.float32)
    c["ropeT"] = np.concatenate([r, r], 0).T.reshape(2, DH, TR).transpose(1, 0, 2).copy()
    i = np.arange(TR)
    c["before"] = (i[:, None] < i[None]).astype(np.float32)
    c["ones"] = np.ones((128, 128), np.float32)
    c["rank_order"] = np.tile(64.0 - np.arange(32, dtype=np.float32), (TR, 1))
    e = np.arange(32)
    c["exp_order"] = np.stack([SLOT * (e[:, None] < e[None]), 1 * (e[:, None] <= e[None])], 1).astype(np.float32)
    c["fills"] = np.tile(SLOT * np.arange(THR, dtype=np.float32), (32, 1))
    c["tile_no"] = np.arange(TMAX, dtype=np.float32)[None]
    c["pair_no"] = (2 * np.arange(TMAX // 2, dtype=np.float32))[None]
    half = RQK // 2
    p64 = np.arange(L, dtype=np.float64)
    inv = 1.0 / 10000.0 ** (np.arange(half) / half)
    a = p64[:, None] * inv[None]
    zeta = (np.arange(half) + half) / RQK
    for n, s in (("q", 1.0), ("k", -1.0)):
        dec = zeta[None] ** (s * p64[:, None] / 512.0)
        co, si = (np.cos(a) * dec).T, (np.sin(a) * dec).T
        c[f"cos_{n}"] = np.concatenate([co, co], 0).astype(np.float32)
        c[f"sin_{n}"] = np.concatenate([si, -si], 0).astype(np.float32)
    g = 1.0 - 2.0 ** (-(5.0 + np.arange(RH)))
    diff = p64[:, None] - p64[None]
    dm = g[:, None, None] ** np.clip(diff, 0, None)[None] * (diff >= 0)[None]
    dm = dm / np.sqrt(np.clip(dm.sum(-1, keepdims=True), 1e-6, None)) * RQK ** -0.5
    c["decayT"] = np.stack([np.kron(np.eye(2), m.T) for m in dm], 1).astype(np.float32)
    hb = np.kron(np.eye(2), np.ones((RV, RV))) / (RV * L)
    c["head_mean"] = hb.astype(np.float32)
    return c


def hold(eng, sem, value):
    eng.wait_ge(sem, value)
    eng.nop(nofuse=True)


class Chain:

    def __init__(self, eng, sem, per_pass=0):
        self.eng, self.sem, self.n, self.base, self.per_pass = eng, sem, 0, 0, per_pass

    def start(self, i):
        self.n, self.base = 0, i * self.per_pass

    def link(self, ins, alone=False):
        self.n += 1
        ins.then_inc(self.sem, 1)
        if alone:
            hold(self.eng, self.sem, self.base + self.n)
        else:
            self.eng.wait_ge(self.sem, self.base + self.n)

    def end(self):
        assert self.n == self.per_pass, f"links per pass: {self.n}, not {self.per_pass}"


def build(nc, d, out):
    top = ExitStack()
    with top:
        def sb(name, shape, dt=F32):
            return top.enter_context(nc.sbuf_tensor(name, shape, dt))

        def dram(name, shape):
            return nc.dram_tensor(name, shape, F32).ap()

        ps = top.enter_context(nc.psum_tensor("ps", [128, 8, PSB], F32))
        slots_in = dram("slots_in", [TMAX * SLOT, D])
        slots_out = dram("slots_out", [TMAX * SLOT, D])

        tab = {}
        loads = []

        def resident(name, shape):
            tab[name] = sb("t_" + name, shape)
            loads.append((tab[name], d[name]))

        resident("ident", [128, 128])
        for n in ("image_block", "block_neg", "causal_neg", "before"):
            resident(n, [TR, TR])
        resident("ropeT", [DH, 2, TR])
        resident("ones", [128, 128])
        resident("rank_order", [TR, 32])
        resident("exp_order", [32, 2, 32])
        resident("fills", [32, THR])
        resident("tile_no", [1, TMAX])
        resident("pair_no", [1, TMAX // 2])
        for n in ("cos_q", "sin_q", "cos_k", "sin_k"):
            resident(n, [128, L])
        resident("decayT", [TR, RH, TR])
        resident("head_mean", [128, 128])
        resident("pos", [TR, D])
        resident("conv_b", [TR, D])
        resident("conv_w", [128, PK, D])
        resident("wv0", [DH, 2, 64])
        resident("wo0", [64, D])
        resident("gate0", [DH, 2, 32])
        resident("wqk1", [DH, 2, 6, 128])
        resident("bqk1", [128, 6])
        resident("wv1", [DH, 2, D])
        resident("bv1", [TR, D])
        resident("wp1", [DH, 2, D])
        resident("bp1", [TR, D])
        resident("gate1", [DH, 2, 9])
        resident("bgate1", [TR, 9])
        resident("com1", [DH, 2, FF])
        resident("bcom1", [128, FM])
        resident("com2", [128, FM, D])
        resident("bcom2", [TR, D])
        resident("proj_w", [DH, 2, D])
        resident("proj_b", [TR, D])
        resident("ffn1", [DH, 2, FF])
        resident("bffn1", [128, FM])
        resident("ffn2", [128, FM, D])
        resident("wq3", [DH, 2, RH * RQK])
        resident("wk3", [DH, 2, RH * RQK])
        resident("wv3", [DH, 2, RH * RV])
        resident("wg3", [DH, 2, RH * RV])
        resident("wo3", [128, 3, D])
        resident("gnw", [128, 3])
        resident("gnb", [128, 3])
        resident("gate3", [DH, 2, 8])
        ident = tab["ident"]

        H = sb("H", [TR, NT, D])
        G1 = sb("G1", [TR, NT, D])
        G2 = sb("G2", [TR, NT, D])
        logits = sb("logits", [TR, NT, 32])
        coef = sb("coef", [TR, 2, NT])
        slot_of = sb("slot_of", [TR, 2, NT], I32)
        exp_of = sb("exp_of", [1, TMAX], I32)
        n_pairs = sb("n_pairs", [1, 1], I32)
        ropeP = sb("ropeP", [TR, TR])
        negh = sb("negh", [128, 32])
        pbias = sb("pbias", [TR, D])

        before16 = sb("before16", [TR, TR], BF16)
        ones16 = sb("ones16", [TR, TR], BF16)
        mask = sb("mask", [TR, NT * 32], BF16)

        xin = [sb(f"xin{u}", [SLOT, D]) for u in range(2)]
        xT = [sb(f"xT{u}", [DH, 2, SLOT]) for u in range(2)]
        wA = [sb(f"wA{u}", [DH, 2 * FF]) for u in range(2)]
        wB = [sb(f"wB{u}", [128, 2312]) for u in range(2)]
        wC = [sb(f"wC{u}", [64, D + 1]) for u in range(2)]
        wD = [sb(f"wD{u}", [1, D]) for u in range(2)]
        hid = [sb(f"hid{u}", [128, FM, SLOT]) for u in range(2)]
        hid2 = [sb(f"hid2{u}", [128, 4, SLOT]) for u in range(2)]
        zT = [sb(f"zT{u}", [64, SLOT]) for u in range(2)]
        yo = [sb(f"yo{u}", [SLOT, D]) for u in range(2)]

        A0 = sb("A0", [TR, CT, D])
        A1 = sb("A1", [TR, CT, D])
        A2 = sb("A2", [TR, CT, D])
        hT = sb("hT", [DH, 2, CW])
        stats = sb("stats", [TR, CT, 6])
        mv = sb("mv", [TR, CT, 2])
        rstd = sb("rstd", [TR, CT])
        big = sb("big", [128, 6 * CW])
        big2 = sb("big2", [128, 3 * CW])
        sc = sb("sc", [128, 4 * HEADS * TR // 2])
        pT = sb("pT", [TR, HEADS, TR])
        small = sb("small", [128, 64])

        bc = lambda ap, shape: ap.broadcast_to(shape)

        def halves(ps_banks):
            return ps[0:TR, ps_banks:ps_banks + 2, 0:2 * D].rearrange("p b (t n) -> p b t n", t=2)

        def as_tiles(x):
            return x[:, :, :].rearrange("p (b t) n -> p b t n", b=2)

        class stage:

            def __enter__(self):
                self.sems, self.stack = [], ExitStack()
                return self

            def semaphore(self, name):
                self.sems.append(nc.alloc_semaphore(name))
                return self.sems[-1]

            def block(self):
                return self.stack.enter_context(nc.Block())

            def __exit__(self, *error):
                self.stack.__exit__(*error)
                if not error[0]:
                    nc.clear_and_free_semaphores(self.sems)
                    nc.all_engine_barrier()

        def transpose_chunk(pe, src, bank):
            for k in range(2):
                for j in range(CT):
                    mm = pe.transpose(ps[0:DH, bank + k, j * TR:(j + 1) * TR], src[:, j, k * DH:(k + 1) * DH],
                                      ident[0:TR, 0:TR])
            return mm

        def project(pe, xT, w, ncols, out_of, kk=2):
            for j in range(CT):
                for k in range(kk):
                    mm = pe.matmul(out_of(j), xT[:, k, j * TR:(j + 1) * TR], w[:, k, 0:ncols],
                                   start=(k == 0), stop=(k == kk - 1))
            return mm

        def ln_stats(dve, x, ch, sem):
            for j in range(CT):
                ins = dve.bn_stats(stats[:, j, :], x[:, j, :])
            ch.link(ins, alone=True)
            for j in range(CT):
                ins = dve.bn_aggr(mv[:, j, :], stats[:, j, :])
            ins.then_inc(sem, 1)

        def ln_rstd(pool, ch, sem):
            ch.link(pool.tensor_scalar(rstd[:, :], mv[:, :, 1], EPS, None, ALU.add))
            pool.tensor_tensor(rstd[:, :], rstd[:, :], negh[0:TR, 0:CT], ALU.pow).then_inc(sem, 1)

        def ln_apply(dve, y, x, sem):
            for j in range(CT):
                ins = dve.tensor_scalar(y[:, j, :], x[:, j, :], mv[:, j, 0:1], rstd[:, j:j + 1],
                                        ALU.subtract, ALU.mult)
            ins.then_inc(sem, 1)

        def setup():
            with stage() as ctx:
                sem = ctx.semaphore
                loaded, zeros_set = sem("loaded"), sem("zeros_set")
                dve_step = sem("dve_step")
                rope_scores, shifted, exped, rope_probs, turned = (
                    sem("rope_scores"), sem("shifted"), sem("exped"), sem("rope_probs"), sem("turned"))
                zero_proj = sem("zero_proj")
                block = ctx.block()
                zeros = G2[:, :, :].rearrange("p t n -> p (t n)")
                full = 16 * len(loads)

                @block.sync
                def _(sp):
                    for dst, src in loads:
                        sp.dma_start(dst[:], src).then_inc(loaded, 16)
                    sp.wait_ge(loaded, full)

                @block.tensor
                def _(pe):
                    pe.wait_ge(loaded, full)
                    for k in range(2):
                        mm = pe.matmul(ps[0:TR, 0, 0:TR], tab["ropeT"][:, k, :], tab["ropeT"][:, k, :],
                                       start=(k == 0), stop=(k == 1))
                    mm.then_inc(rope_scores, 1)
                    pe.wait_ge(zeros_set, 1)
                    for k in range(2):
                        mm = pe.matmul(ps[0:TR, 1, 0:D], zeros[0:DH, 0:TR], tab["proj_w"][:, k, :],
                                       start=(k == 0), stop=(k == 1))
                    mm.then_inc(zero_proj, 1)
                    pe.wait_ge(rope_probs, 1)
                    pe.transpose(ps[0:TR, 2, 0:TR], sc[0:TR, 0:TR], ident[0:TR, 0:TR]).then_inc(turned, 1)

                @block.scalar
                def _(act):
                    act.wait_ge(shifted, 1)
                    act.activation(sc[0:TR, 0:TR], sc[0:TR, 0:TR], ACT.Exp).then_inc(exped, 1)

                @block.vector
                def _(dve):
                    ch = Chain(dve, dve_step)
                    dve.memset(G2[:, :, :], 0.0).then_inc(zeros_set, 1)
                    dve.memset(negh[:, :], -0.5)
                    dve.wait_ge(loaded, full)
                    dve.tensor_copy(before16[:, :], tab["before"][:, :])
                    dve.tensor_copy(ones16[:, :], tab["ones"][0:TR, 0:TR])
                    s = sc[0:TR, 0:TR]
                    dve.wait_ge(rope_scores, 1)
                    ch.link(dve.tensor_tensor(s, ps[0:TR, 0, 0:TR], tab["block_neg"][:, :], ALU.add))
                    ch.link(dve.tensor_reduce(small[0:TR, 0:1], s, AX, ALU.max))
                    dve.tensor_scalar(s, s, small[0:TR, 0:1], None, ALU.subtract).then_inc(shifted, 1)
                    dve.wait_ge(exped, 1)
                    ch.link(dve.tensor_reduce(small[0:TR, 1:2], s, AX, ALU.add))
                    ch.link(dve.reciprocal(small[0:TR, 2:3], small[0:TR, 1:2]))
                    dve.tensor_scalar(s, s, small[0:TR, 2:3], None, ALU.mult).then_inc(rope_probs, 1)
                    ch.link(dve.tensor_tensor(tab["pos"][:, :], tab["pos"][:, :], tab["conv_b"][:, :], ALU.add))
                    dve.wait_ge(zero_proj, 1)
                    dve.tensor_tensor(pbias[:, :], ps[0:TR, 1, 0:D], tab["proj_b"][:, :], ALU.add)
                    dve.wait_ge(turned, 1)
                    dve.tensor_copy(ropeP[:, :], ps[0:TR, 2, 0:TR])

        def embed_and_rope_attention():
            with stage() as ctx:
                sem = ctx.semaphore
                names = ("patches_in emb_ps h0_made tr_ps hT_made v_ps v_made av_ps av_made o_ps stats_made "
                         "rstd_made h1_made h1_kept logits_ps chunk_done dve_step pool_step cleared")
                S = {n: sem("a_" + n) for n in names.split()}
                block = ctx.block()
                patches = big[:, :].rearrange("p (k n) -> p k n", k=PK)
                v = big2[0:TR, 0:CT * 64].rearrange("p (t n) -> p t n", t=CT)
                av = big2[0:64, 2 * CW:3 * CW]

                @block.sync
                def _(sp):
                    sp.dma_start(big[:, :], d["patches"][0]).then_inc(S["patches_in"], 16)
                    with sp.Fori(1, NCH) as c:
                        sp.wait_ge(S["emb_ps"], c)
                        sp.dma_start(big[:, :], d["patches"][ds(c, 1)].rearrange("o p n -> (o p) n")).then_inc(
                            S["patches_in"], 16)

                @block.tensor
                def _(pe):
                    with pe.Fori(0, NCH) as c:
                        pe.wait_ge(S["chunk_done"], c * 2 + 2)
                        pe.wait_ge(S["patches_in"], c * 16 + 16)
                        project(pe, patches, tab["conv_w"], D,
                                lambda j: ps[0:TR, j // 2, (j % 2) * D:(j % 2 + 1) * D], PK).then_inc(S["emb_ps"], 1)
                        pe.wait_ge(S["h0_made"], c + 1)
                        transpose_chunk(pe, A0, 2).then_inc(S["tr_ps"], 1)
                        pe.wait_ge(S["hT_made"], c * 2 + 1)
                        project(pe, hT, tab["wv0"], 64, lambda j: ps[0:TR, 4, j * 64:(j + 1) * 64]).then_inc(S["v_ps"], 1)
                        pe.wait_ge(S["v_made"], c + 1)
                        for j in range(CT):
                            mm = pe.matmul(ps[0:64, 5, j * TR:(j + 1) * TR], v[:, j, :], ropeP[:, :], start=True, stop=True)
                        mm.then_inc(S["av_ps"], 1)
                        pe.wait_ge(S["av_made"], c + 1)
                        for j in range(CT):
                            mm = pe.matmul(ps[0:TR, 6 + j // 2, (j % 2) * D:(j % 2 + 1) * D], av[:, j * TR:(j + 1) * TR],
                                           tab["wo0"][:, :], start=True, stop=True)
                        mm.then_inc(S["o_ps"], 1)
                        pe.wait_ge(S["h1_made"], c + 1)
                        transpose_chunk(pe, A2, 2).then_inc(S["tr_ps"], 1)
                        pe.wait_ge(S["hT_made"], c * 2 + 2)
                        project(pe, hT, tab["gate0"], 32, lambda j: ps[0:TR, 4, j * 32:(j + 1) * 32]).then_inc(
                            S["logits_ps"], 1)

                @block.scalar
                def _(act):
                    with act.Fori(0, NCH) as c:
                        act.wait_ge(S["tr_ps"], c * 2 + 1)
                        act.activation(hT[:, :, :], ps[0:DH, 2:4, 0:CW], ACT.Copy).then_inc(S["hT_made"], 1)
                        act.wait_ge(S["v_ps"], c + 1)
                        act.activation(big2[0:TR, 0:CT * 64], ps[0:TR, 4, 0:CT * 64], ACT.Copy).then_inc(S["v_made"], 1)
                        act.wait_ge(S["av_ps"], c + 1)
                        act.activation(av, ps[0:64, 5, 0:CW], ACT.Copy).then_inc(S["av_made"], 1)
                        act.wait_ge(S["tr_ps"], c * 2 + 2)
                        act.activation(hT[:, :, :], ps[0:DH, 2:4, 0:CW], ACT.Copy).then_inc(S["hT_made"], 1)

                @block.gpsimd
                def _(pool):
                    for buf in (slots_in, slots_out):
                        v = buf.rearrange("(t p n) d -> t p (n d)", p=64, n=16)
                        for t in range(v.shape[0]):
                            pool.dma_start(v[t], G2[0:64, :, :].rearrange("p t n -> p (t n)")).then_inc(S["cleared"], 16)
                    ch = Chain(pool, S["pool_step"], 1)
                    pool.sem_inc(S["chunk_done"], 1)
                    with pool.Fori(0, NCH) as c:
                        ch.start(c)
                        hold(pool, S["stats_made"], c + 1)
                        ln_rstd(pool, ch, S["rstd_made"])
                        pool.wait_ge(S["h1_made"], c + 1)
                        pool.tensor_copy(H[:, ds(c * CT, CT), :], A2[:, :, :]).then_inc(S["chunk_done"], 1)
                        ch.end()
                    pool.wait_ge(S["cleared"], 2 * TMAX * SLOT // 64 // 16 * 16)

                @block.vector
                def _(dve):
                    ch = Chain(dve, S["dve_step"], 2)
                    dve.sem_inc(S["chunk_done"], 1)
                    with dve.Fori(0, NCH) as c:
                        ch.start(c)
                        dve.wait_ge(S["emb_ps"], c + 1)
                        dve.wait_ge(S["chunk_done"], c * 2 + 2)
                        dve.tensor_tensor(as_tiles(A0), halves(0),
                                          bc(tab["pos"][:, :].unsqueeze(1).unsqueeze(1), [TR, 2, 2, D]),
                                          ALU.add).then_inc(S["h0_made"], 1)
                        dve.wait_ge(S["o_ps"], c + 1)
                        ch.link(dve.tensor_tensor(as_tiles(A1), halves(6), as_tiles(A0), ALU.add))
                        ln_stats(dve, A1, ch, S["stats_made"])
                        dve.wait_ge(S["rstd_made"], c + 1)
                        ln_apply(dve, A2, A1, S["h1_made"])
                        dve.wait_ge(S["logits_ps"], c + 1)
                        dve.tensor_scalar(logits[:, ds(c * CT, CT), :],
                                          ps[0:TR, 4, 0:CT * 32].rearrange("p (t n) -> p t n", t=CT),
                                          1.0, None, ALU.mult).then_inc(S["chunk_done"], 1)
                        ch.end()

        def route(r):
            E, K = MOE[r]
            with stage() as ctx:
                sem = lambda n: ctx.semaphore(f"r{r}_{n}")
                dve_step, shifted, exped, masked, ranked, tiles_known, starts_ps, slots_known, scattered = map(
                    sem, ("dve_step shifted exped masked ranked tiles_known starts_ps slots_known scattered").split())
                block = ctx.block()
                wide = lambda buf, i: buf[0:TR, i * NT * 32:i * NT * 32 + NT * E].rearrange("p (t e) -> p t e", t=NT)
                probs, cand, at_slot = wide(big, 0), wide(big, 1), wide(big, 2)
                hot = [wide(big2, 0), wide(big2, 1)]
                tiny = lambda i: small[0:TR, i * NT:(i + 1) * NT]
                over_e = lambda x: bc(x.unsqueeze(2), [TR, NT, E])
                order = bc(tab["rank_order"][:, 0:E].unsqueeze(1), [TR, NT, E])

                @block.scalar
                def _(act):
                    act.wait_ge(shifted, 1)
                    act.activation(probs, probs, ACT.Exp).then_inc(exped, 1)

                @block.tensor
                def _(pe):
                    pe.wait_ge(masked, 1)
                    m = lambda j, n=1: mask[:, j * E:(j + n) * E]
                    pe.matmul(ps[0:TR, 0, 0:NT * E], before16[:, :], m(0, NT), start=True, stop=True)
                    for j in range(NT - 1):
                        mm = pe.matmul(ps[0:TR, 0, (j + 1) * E:NT * E].rearrange("p (t e) -> p t e", e=E),
                                       ones16[0:TR, 0:TR], bc(m(j).unsqueeze(1), [TR, NT - 1 - j, E]),
                                       start=False, stop=True, skip_group_check=True)
                    for j in range(NT):
                        mm = pe.matmul(ps[0:E, 1, 0:1], m(j), ones16[0:TR, 0:1], start=(j == 0), stop=(j == NT - 1))
                    mm.then_inc(ranked, 1)
                    pe.wait_ge(tiles_known, 1)
                    pe.matmul(ps[0:TR, 2, 0:2 * E].rearrange("p (a e) -> p a e", a=2), sc[0:E, 0:TR],
                              tab["exp_order"][0:E, :, 0:E], start=True, stop=True).then_inc(starts_ps, 1)

                @block.gpsimd
                def _(pool):
                    pool.wait_ge(slots_known, K)
                    for k in range(K):
                        for t in range(NT):
                            pool.indirect_dma_start(slots_in, bass.IndirectOffsetOnAxis(slot_of[:, k, t:t + 1], 0),
                                                    H[:, t, :], None).then_inc(scattered, 16)
                    pool.wait_ge(scattered, 16 * K * NT)

                @block.vector
                def _(dve):
                    ch = Chain(dve, dve_step)
                    ch.link(dve.tensor_reduce(tiny(0), logits[:, :, 0:E], AX, ALU.max))
                    dve.tensor_tensor(probs, logits[:, :, 0:E], over_e(tiny(0)), ALU.subtract).then_inc(shifted, 1)
                    dve.wait_ge(exped, 1)
                    ch.link(dve.tensor_reduce(tiny(1), probs, AX, ALU.add))
                    ch.link(dve.reciprocal(tiny(2), tiny(1)))
                    ch.link(dve.tensor_tensor(probs, probs, over_e(tiny(2)), ALU.mult))
                    for k in range(K):
                        ch.link(dve.tensor_reduce(coef[:, k, :], probs, AX, ALU.max))
                        ch.link(dve.tensor_tensor(cand, probs, over_e(coef[:, k, :]), ALU.is_equal))
                        ch.link(dve.tensor_tensor(cand, cand, order, ALU.mult))
                        ch.link(dve.tensor_reduce(tiny(3), cand, AX, ALU.max))
                        ch.link(dve.tensor_tensor(hot[k], order, over_e(tiny(3)), ALU.is_equal))
                        if k + 1 < K:
                            ch.link(dve.scalar_tensor_tensor(probs, hot[k], -2.0, probs, ALU.mult, ALU.add))
                    mask3 = mask[:, 0:NT * E].rearrange("p (t e) -> p t e", t=NT)
                    if K == 2:
                        dve.tensor_tensor(mask3, hot[0], hot[1], ALU.add).then_inc(masked, 1)
                    else:
                        dve.tensor_copy(mask3, hot[0]).then_inc(masked, 1)
                    if r == 0:
                        ch.link(dve.tensor_tensor(tiny(0), coef[:, 0, :], coef[:, 1, :], ALU.add))
                        ch.link(dve.tensor_scalar(tiny(1), tiny(0), 1e-20, None, ALU.add))
                        ch.link(dve.reciprocal(tiny(2), tiny(1)))
                        ch.link(dve.tensor_tensor(coef[:, :, :], coef[:, :, :],
                                                  bc(tiny(2).unsqueeze(1), [TR, 2, NT]), ALU.mult))
                    if r == 1:
                        is0 = hot[0][:, :, 0]
                        ch.link(dve.reciprocal(tiny(0), coef[:, 0, :]))
                        ch.link(dve.tensor_tensor(tiny(0), tiny(0), coef[:, 0, :], ALU.mult))
                        ch.link(dve.tensor_scalar(tiny(1), coef[:, 0, :], -1.0, 1.0, ALU.mult, ALU.add))
                        ch.link(dve.tensor_tensor(tiny(0), tiny(0), is0, ALU.mult))
                        ch.link(dve.tensor_scalar(tiny(2), is0, -1.0, 1.0, ALU.mult, ALU.add))
                        ch.link(dve.tensor_tensor(tiny(1), tiny(1), tiny(2), ALU.mult))
                        ch.link(dve.tensor_tensor(coef[:, 0, :], coef[:, 0, :], tiny(2), ALU.mult))
                        ch.link(dve.tensor_tensor(coef[:, 1, :], tiny(0), tiny(1), ALU.add))
                    dve.wait_ge(ranked, 1)
                    fill = sc[0:E, 256:256 + THR]
                    ch.link(dve.tensor_scalar(fill, tab["fills"][0:E, :], ps[0:E, 1, 0:1], None, ALU.is_lt))
                    ch.link(dve.tensor_reduce(sc[0:E, 300:301], fill, AX, ALU.add))
                    dve.tensor_scalar(sc[0:E, 0:TR], tab["ones"][0:E, 0:TR], sc[0:E, 300:301], None,
                                      ALU.mult).then_inc(tiles_known, 1)
                    dve.wait_ge(starts_ps, 1)
                    starts = sc[0:TR, 320:320 + 2 * E]
                    ch.link(dve.tensor_copy(starts, ps[0:TR, 2, 0:2 * E]))
                    ch.link(dve.tensor_tensor(at_slot, ps[0:TR, 0, 0:NT * E].rearrange("p (t e) -> p t e", t=NT),
                                              bc(starts[:, 0:E].unsqueeze(1), [TR, NT, E]), ALU.add))
                    for k in range(K):
                        ch.link(dve.tensor_tensor(cand, hot[k], at_slot, ALU.mult))
                        ch.link(dve.tensor_reduce(tiny(3), cand, AX, ALU.add))
                        ch.link(dve.tensor_copy(slot_of[:, k, :], tiny(3)))
                        dve.sem_inc(slots_known, 1)
                    T = max_tiles(E, K)
                    ends = starts[0:1, E:2 * E]
                    past = big[0:1, 0:T * E].rearrange("p (t e) -> p t e", t=T)
                    ch.link(dve.tensor_tensor(past, bc(ends.unsqueeze(1), [1, T, E]),
                                              bc(tab["tile_no"][:, 0:T].unsqueeze(2), [1, T, E]), ALU.is_le))
                    ch.link(dve.tensor_reduce(sc[0:1, 0:T], past, AX, ALU.add))
                    ch.link(dve.tensor_scalar(exp_of[:, 0:T], sc[0:1, 0:T], float(E - 1), None, ALU.min))
                    ch.link(dve.tensor_scalar(sc[0:1, 64:64 + T // 2], tab["pair_no"][:, 0:T // 2],
                                              ends[:, E - 1:E], None, ALU.is_lt))
                    ch.link(dve.tensor_reduce(sc[0:1, 128:129], sc[0:1, 64:64 + T // 2], AX, ALU.add))
                    dve.tensor_copy(n_pairs[:, :], sc[0:1, 128:129])

        def experts(r):
            E, K = MOE[r]
            T = max_tiles(E, K)
            M1 = 4 if r == 0 else FM
            with stage() as ctx:
                sem = lambda n: ctx.semaphore(f"e{r}_{n}")
                two = lambda n: [sem(n + "0"), sem(n + "1")]
                x_in, wa_in, wb_in, wc_in, wd_in, y_out = map(two, "x_in wa_in wb_in wc_in wd_in y_out".split())
                x_ps, xT_made, h1_ps, h1_made, h2_ps, h2_made, z_ps, z_made, y_ps, y_made, y_left, gathered = map(
                    sem, "x_ps xT_made h1_ps h1_made h2_ps h2_made z_ps z_made y_ps y_made y_left gathered".split())
                block = ctx.block()
                funcs = ACT.Relu if r == 2 else ACT.Gelu
                HM = M1 * 128
                loads_of = {0: 5, 1: 4, 2: 3}[r]

                def steps(eng):
                    return eng.value_load(n_pairs[0:1, 0:1], min_val=1, max_val=T // 2)

                @block.sync
                def _(sp):
                    n = steps(sp)
                    for u in range(2):
                        sp.sem_inc(y_ps, 1)
                    with sp.Fori(0, n) as i:
                        for u in range(2):
                            e = sp.value_load(exp_of[0:1, ds(i * 2 + u, 1)], min_val=0, max_val=E - 1)
                            piece = lambda name: d[name][ds(e, 1)].rearrange("o p n -> (o p) n")
                            sp.wait_ge(y_ps, i * 2 + u + 1)
                            sp.dma_start(xin[u][:, :], slots_in[ds((i * 2 + u) * SLOT, SLOT), :]).then_inc(x_in[u], 16)
                            wa = d[f"e{r}_a"].shape[2]
                            sp.dma_start(wA[u][:, 0:wa], piece(f"e{r}_a")).then_inc(wa_in[u], 16)
                            wb = d[f"e{r}_b"].shape[2]
                            sp.dma_start(wB[u][:, 0:wb], piece(f"e{r}_b")).then_inc(wb_in[u], 16)
                            if r == 0:
                                sp.dma_start(wC[u][:, :], piece("e0_c")).then_inc(wc_in[u], 16)
                            if r < 2:
                                sp.dma_start(wD[u][:, :], piece(f"e{r}_d")).then_inc(wd_in[u], 16)

                @block.tensor
                def _(pe):
                    n = steps(pe)
                    with pe.Fori(0, n) as i:
                        for u in range(2):
                            pe.wait_ge(x_in[u], i * 16 + 16)
                            for k in range(2):
                                mm = pe.transpose(ps[0:DH, u, k * SLOT:(k + 1) * SLOT], xin[u][:, k * DH:(k + 1) * DH],
                                                  ident[:, :])
                            mm.then_inc(x_ps, 1)
                        for u in range(2):
                            w1 = wA[u][:, 0:2 * HM].rearrange("p (k n) -> p k n", k=2)
                            pe.wait_ge(xT_made, i * 2 + u + 1)
                            pe.wait_ge(wa_in[u], i * 16 + 16)
                            for m in range(M1):
                                for k in range(2):
                                    mm = pe.matmul(ps[:, 2 + 2 * u + m // 4, (m % 4) * SLOT:(m % 4 + 1) * SLOT],
                                                   w1[:, k, m * 128:(m + 1) * 128], xT[u][:, k, :],
                                                   start=(k == 0), stop=(k == 1))
                            mm.then_inc(h1_ps, 1)
                        if r == 0:
                            for u in range(2):
                                w2 = wB[u][:, 0:2048].rearrange("p (k n) -> p k n", k=4)
                                pe.wait_ge(h1_made, i * 2 + u + 1)
                                pe.wait_ge(wb_in[u], i * 16 + 16)
                                for m in range(4):
                                    for k in range(4):
                                        mm = pe.matmul(ps[:, 3 + 2 * u, m * SLOT:(m + 1) * SLOT],
                                                       w2[:, k, m * 128:(m + 1) * 128], hid[u][:, k, :],
                                                       start=(k == 0), stop=(k == 3))
                                mm.then_inc(h2_ps, 1)
                            for u in range(2):
                                w3 = wB[u][:, 2048:2304].rearrange("p (k n) -> p k n", k=4)
                                pe.wait_ge(h2_made, i * 2 + u + 1)
                                pe.wait_ge(y_made, i * 2 + u + 1)
                                for k in range(4):
                                    mm = pe.matmul(ps[0:64, 6 + u, 0:SLOT], w3[:, k, :], hid2[u][:, k, :],
                                                   start=(k == 0), stop=(k == 3))
                                mm.then_inc(z_ps, 1)
                            for u in range(2):
                                pe.wait_ge(z_made, i * 2 + u + 1)
                                pe.wait_ge(wc_in[u], i * 16 + 16)
                                pe.wait_ge(wd_in[u], i * 16 + 16)
                                y = ps[:, 6 + u, 256:256 + D]
                                pe.matmul(y, zT[u][:, :], wC[u][:, 0:D], start=True, stop=False)
                                pe.matmul(y, tab["ones"][0:1, 0:SLOT], wD[u][:, :], start=False, stop=True).then_inc(y_ps, 1)
                        else:
                            for u in range(2):
                                w2 = wB[u][:, 0:FM * D].rearrange("p (k n) -> p k n", k=FM)
                                pe.wait_ge(h1_made, i * 2 + u + 1)
                                pe.wait_ge(wb_in[u], i * 16 + 16)
                                y = ps[:, 6 + u, 0:D]
                                pe.wait_ge(y_made, i * 2 + u + 1)
                                for k in range(FM):
                                    mm = pe.matmul(y, hid[u][:, k, :], w2[:, k, :], start=(k == 0),
                                                   stop=(r == 2 and k == FM - 1))
                                if r == 1:
                                    pe.wait_ge(wd_in[u], i * 16 + 16)
                                    mm = pe.matmul(y, tab["ones"][0:1, 0:SLOT], wD[u][:, :], start=False, stop=True)
                                mm.then_inc(y_ps, 1)

                @block.scalar
                def _(act):
                    n = steps(act)
                    with act.Fori(0, n) as i:
                        for u in range(2):
                            act.wait_ge(x_ps, i * 2 + u + 1)
                            act.activation(xT[u][:, :, :], ps[0:DH, u, 0:2 * SLOT].rearrange("p (k n) -> p k n", k=2),
                                           ACT.Copy).then_inc(xT_made, 1)
                        for u in range(2):
                            act.wait_ge(h1_ps, i * 2 + u + 1)
                            if r == 2:
                                act.activation(hid[u][:, 0:4, :], ps[:, 2 + 2 * u, :].rearrange("p (m n) -> p m n", m=4),
                                               ACT.Relu)
                                act.activation(hid[u][:, 4:6, :],
                                               ps[:, 3 + 2 * u, 0:256].rearrange("p (m n) -> p m n", m=2),
                                               ACT.Relu).then_inc(h1_made, 1)
                                continue
                            b0 = 2304 if r == 0 else FM * D
                            act.wait_ge(wb_in[u], i * 16 + 16)
                            for m in range(M1):
                                ins = act.activation(hid[u][:, m, :], ps[:, 2 + 2 * u + m // 4, (m % 4) * SLOT:(m % 4 + 1) * SLOT],
                                                     ACT.Gelu, bias=wB[u][:, b0 + m:b0 + m + 1])
                            ins.then_inc(h1_made, 1)
                        if r == 0:
                            for u in range(2):
                                act.wait_ge(h2_ps, i * 2 + u + 1)
                                for m in range(4):
                                    ins = act.activation(hid2[u][:, m, :], ps[:, 3 + 2 * u, m * SLOT:(m + 1) * SLOT],
                                                         ACT.Gelu, bias=wB[u][:, 2308 + m:2309 + m])
                                ins.then_inc(h2_made, 1)

                @block.vector
                def _(dve):
                    n = steps(dve)
                    for u in range(2):
                        dve.sem_inc(y_made, 1)
                    with dve.Fori(0, n) as i:
                        if r == 0:
                            for u in range(2):
                                dve.wait_ge(wc_in[u], i * 16 + 16)
                                dve.wait_ge(z_ps, i * 2 + u + 1)
                                dve.tensor_scalar(zT[u][:, :], ps[0:64, 6 + u, 0:SLOT], wC[u][:, D:D + 1], None,
                                                  ALU.add).then_inc(z_made, 1)
                        for u in range(2):
                            dve.wait_ge(y_left, i * 2 + u + 1)
                            dve.wait_ge(y_ps, i * 2 + u + 3)
                            c0 = 256 if r == 0 else 0
                            dve.tensor_scalar(yo[u][:, :], ps[:, 6 + u, c0:c0 + D], 1.0, None,
                                              ALU.mult).then_inc(y_made, 1)

                @block.gpsimd
                def _(pool):
                    n = steps(pool)
                    for u in range(2):
                        pool.sem_inc(y_left, 1)
                    with pool.Fori(0, n) as i:
                        for u in range(2):
                            hold(pool, y_made, i * 2 + u + 3)
                            pool.dma_start(slots_out[ds((i * 2 + u) * SLOT, SLOT), :], yo[u][:, :]).then_inc(y_out[u], 16)
                        for u in range(2):
                            hold(pool, y_out[u], i * 16 + 16)
                            pool.sem_inc(y_left, 1)
                    for k in range(K):
                        for t in range(NT):
                            pool.indirect_dma_start((G1, G2)[k][:, t, :], None, slots_out,
                                                    bass.IndirectOffsetOnAxis(slot_of[:, k, t:t + 1], 0)).then_inc(gathered, 16)
                    pool.wait_ge(gathered, 16 * K * NT)

        def combine_pool(pool, S, c):
            hold(pool, S["chunk_done"], c * 2 + 2)
            pool.tensor_tensor(A0[:, :, :], G1[:, ds(c * CT, CT), :],
                               bc(coef[:, 0, ds(c * CT, CT)].unsqueeze(2), [TR, CT, D]), ALU.mult).then_inc(S["g1_made"], 1)

        def combine_dve(dve, ch, S, c, second):
            h = H[:, ds(c * CT, CT), :]
            if second:
                ch.link(dve.tensor_tensor(A1[:, :, :], G2[:, ds(c * CT, CT), :],
                                          bc(coef[:, 1, ds(c * CT, CT)].unsqueeze(2), [TR, CT, D]), ALU.mult))
                ch.link(dve.tensor_tensor(A1[:, :, :], A1[:, :, :], h, ALU.add))
                dve.wait_ge(S["g1_made"], c + 1)
                ch.link(dve.tensor_tensor(A1[:, :, :], A1[:, :, :], A0[:, :, :], ALU.add))
            else:
                dve.wait_ge(S["g1_made"], c + 1)
                ch.link(dve.tensor_tensor(A1[:, :, :], A0[:, :, :], h, ALU.add))

        def norm_dve(dve, ch, S, y, x, i):
            ln_stats(dve, x, ch, S["stats_made"])
            dve.wait_ge(S["rstd_made"], i + 1)
            ln_apply(dve, y, x, S["normed"])

        def norm_pool(pool, ch, S, i):
            hold(pool, S["stats_made"], i + 1)
            ln_rstd(pool, ch, S["rstd_made"])

        def hidden_banks(m):
            return (2, 3, 5, 6, 7, 2)[m]

        def mlp_pe(pe, S, c, w1, w2):
            for m in range(FM):
                if m == 5:
                    pe.wait_ge(S["hid_made"], c * FM + 1)
                for k in range(2):
                    mm = pe.matmul(ps[:, hidden_banks(m), 0:CW], w1[:, k, m * 128:(m + 1) * 128], hT[:, k, :],
                                   start=(k == 0), stop=(k == 1))
                mm.then_inc(S["hid_ps"], 1)
            pe.wait_ge(S["hid_made"], c * FM + FM)
            project(pe, big[:, :].rearrange("p (k n) -> p k n", k=FM), w2, D,
                    lambda j: ps[0:TR, j // 2, (j % 2) * D:(j % 2 + 1) * D], FM).then_inc(S["mlp_ps"], 1)

        def mlp_act(act, S, c, bias):
            for m in range(FM):
                act.wait_ge(S["hid_ps"], c * FM + m + 1)
                act.activation(big[:, m * CW:(m + 1) * CW], ps[:, hidden_banks(m), 0:CW], ACT.Gelu,
                               bias=bias[:, m:m + 1]).then_inc(S["hid_made"], 1)

        def turn_act(act, S, i):
            act.wait_ge(S["tr_ps"], i + 1)
            act.activation(hT[:, :, :], ps[0:DH, 0:2, 0:CW], ACT.Copy).then_inc(S["hT_made"], 1)

        def causal_attention():
            with stage() as ctx:
                names = ("g1_made stats_made rstd_made normed tr_ps hT_made qk_ps q_made k_made v_ps v_made s_ps s_taken "
                         "max_made centered exped p_ps pT_made y_ps y_made o_ps logits_ps logits_taken hid_ps hid_made mlp_ps "
                         "chunk_done dve_step pool_step")
                S = {n: ctx.semaphore("b_" + n) for n in names.split()}
                block = ctx.block()
                qk = big[:, :].rearrange("p (g n) -> p g n", g=6)
                v = big2[0:TR, 0:CT * D].rearrange("p (t n) -> p t n", t=CT)
                W = HEADS * TR
                scores = lambda j: sc[0:TR, (j % 2) * W:(j % 2 + 1) * W]
                by_head = lambda x: x.rearrange("p (h n) -> p h n", h=HEADS)
                place = lambda h: (h % 4) * 3 + h // 4
                maxes = lambda j: small[0:TR, (j % 2) * 32:(j % 2) * 32 + HEADS]
                sums = lambda j: small[0:TR, (j % 2) * 32 + 12:(j % 2) * 32 + 24]

                @block.tensor
                def _(pe):
                    with pe.Fori(0, NCH) as c:
                        pe.wait_ge(S["normed"], c * 2 + 1)
                        transpose_chunk(pe, A2, 0).then_inc(S["tr_ps"], 1)
                        pe.wait_ge(S["hT_made"], c * 3 + 1)
                        for g in range(6):
                            for k in range(2):
                                mm = pe.matmul(ps[:, 2 + g, 0:CW], tab["wqk1"][:, k, g, :], hT[:, k, :],
                                               start=(k == 0), stop=(k == 1))
                            mm.then_inc(S["qk_ps"], 1)
                        project(pe, hT, tab["wv1"], D, lambda j: ps[0:TR, j // 2, (j % 2) * D:(j % 2 + 1) * D]).then_inc(
                            S["v_ps"], 1)
                        pe.wait_ge(S["q_made"], c + 1)
                        pe.wait_ge(S["k_made"], c + 1)
                        pe.wait_ge(S["v_made"], c + 1)
                        for j in range(CT + 1):
                            if j < CT:
                                if j > 0:
                                    pe.wait_ge(S["s_taken"], c * CT + j)
                                t = slice(j * TR, (j + 1) * TR)
                                for h in range(HEADS):
                                    g, r = h // 4, h % 4
                                    mm = pe.matmul(ps[0:TR, r, g * TR:(g + 1) * TR], qk[32 * r:32 * r + HD, g, t],
                                                   qk[32 * r:32 * r + HD, 3 + g, t], start=True, stop=True,
                                                   tile_position=(32 * r, 0))
                                mm.then_inc(S["s_ps"], 1)
                            if j > 0:
                                i = j - 1
                                pe.wait_ge(S["exped"], c * CT + i + 1)
                                for n in range(HEADS):
                                    mm = pe.transpose(ps[0:TR, 4 + n // 4, (n % 4) * TR:(n % 4 + 1) * TR],
                                                      scores(i)[:, n * TR:(n + 1) * TR], ident[0:TR, 0:TR])
                                mm.then_inc(S["p_ps"], 1)
                                pe.wait_ge(S["pT_made"], c * CT + i + 1)
                                if i > 0:
                                    pe.wait_ge(S["y_made"], c * CT + i)
                                for h in range(HEADS):
                                    mm = pe.matmul(ps[0:TR, 7, h * HD:(h + 1) * HD], pT[:, place(h), :],
                                                   v[:, i, h * HD:(h + 1) * HD], start=True, stop=True)
                                mm.then_inc(S["y_ps"], 1)
                        pe.wait_ge(S["y_made"], c * CT + CT)
                        transpose_chunk(pe, A0, 0).then_inc(S["tr_ps"], 1)
                        pe.wait_ge(S["hT_made"], c * 3 + 2)
                        project(pe, hT, tab["wp1"], D, lambda j: ps[0:TR, 2 + j // 2, (j % 2) * D:(j % 2 + 1) * D]).then_inc(
                            S["o_ps"], 1)
                        pe.wait_ge(S["normed"], c * 2 + 2)
                        transpose_chunk(pe, A2, 0).then_inc(S["tr_ps"], 1)
                        pe.wait_ge(S["hT_made"], c * 3 + 3)
                        project(pe, hT, tab["gate1"], 9, lambda j: ps[0:TR, 4, j * 9:(j + 1) * 9]).then_inc(S["logits_ps"], 1)
                        mlp_pe(pe, S, c, tab["com1"], tab["com2"])

                @block.scalar
                def _(act):
                    with act.Fori(0, NCH) as c:
                        turn_act(act, S, c * 3)
                        for g in range(3):
                            act.wait_ge(S["qk_ps"], c * 6 + g + 1)
                            ins = act.activation(qk[:, g, :], ps[:, 2 + g, 0:CW], ACT.Identity, bias=tab["bqk1"][:, g:g + 1])
                        ins.then_inc(S["q_made"], 1)
                        for j in range(CT):
                            act.wait_ge(S["centered"], c * CT + j + 1)
                            act.activation(scores(j), scores(j), ACT.Exp, scale=HD ** -0.5).then_inc(S["exped"], 1)
                            act.wait_ge(S["p_ps"], c * CT + j + 1)
                            act.activation(pT[:, :, :].rearrange("p (b h) n -> p b (h n)", b=3), ps[0:TR, 4:7, 0:4 * TR],
                                           ACT.Copy).then_inc(S["pT_made"], 1)
                        turn_act(act, S, c * 3 + 1)
                        turn_act(act, S, c * 3 + 2)
                        mlp_act(act, S, c, tab["bcom1"])

                @block.gpsimd
                def _(pool):
                    ch = Chain(pool, S["pool_step"], 2)
                    pool.sem_inc(S["chunk_done"], 1)
                    with pool.Fori(0, NCH) as c:
                        ch.start(c)
                        combine_pool(pool, S, c)
                        norm_pool(pool, ch, S, c * 2)
                        for j in range(CT):
                            hold(pool, S["max_made"], c * CT + j + 1)
                            x = by_head(scores(j))
                            pool.tensor_tensor(x, x, bc(maxes(j).unsqueeze(2), [TR, HEADS, TR]),
                                               ALU.subtract).then_inc(S["centered"], 1)
                        norm_pool(pool, ch, S, c * 2 + 1)
                        hold(pool, S["normed"], c * 2 + 2)
                        pool.tensor_copy(H[:, ds(c * CT, CT), :], A2[:, :, :]).then_inc(S["chunk_done"], 1)
                        ch.end()

                @block.vector
                def _(dve):
                    ch = Chain(dve, S["dve_step"], 15)
                    dve.sem_inc(S["chunk_done"], 1)
                    with dve.Fori(0, NCH) as c:
                        ch.start(c)
                        dve.wait_ge(S["chunk_done"], c * 2 + 2)
                        combine_dve(dve, ch, S, c, True)
                        norm_dve(dve, ch, S, A2, A1, c * 2)
                        for g in range(3):
                            dve.wait_ge(S["qk_ps"], c * 6 + 3 + g + 1)
                            ins = dve.tensor_scalar(qk[:, 3 + g, :], ps[:, 5 + g, 0:CW], tab["bqk1"][:, 3 + g:4 + g], None,
                                                    ALU.add)
                        ins.then_inc(S["k_made"], 1)
                        dve.wait_ge(S["v_ps"], c + 1)
                        dve.tensor_tensor(v.rearrange("p (b t) n -> p b t n", b=2), halves(0),
                                          bc(tab["bv1"][:, :].unsqueeze(1).unsqueeze(1), [TR, 2, 2, D]),
                                          ALU.add).then_inc(S["v_made"], 1)
                        for j in range(CT + 1):
                            if j < CT:
                                dve.wait_ge(S["s_ps"], c * CT + j + 1)
                                dve.tensor_tensor(
                                    scores(j).rearrange("p (r g n) -> p r g n", r=4, g=3),
                                    ps[0:TR, 0:4, 0:3 * TR].rearrange("p r (g n) -> p r g n", g=3),
                                    bc(tab["causal_neg"][:, :].unsqueeze(1).unsqueeze(1), [TR, 4, 3, TR]),
                                    ALU.add).then_inc(S["s_taken"], 1)
                                dve.wait_ge(S["s_taken"], c * CT + j + 1)
                                dve.tensor_reduce(maxes(j), by_head(scores(j)), AX, ALU.max).then_inc(S["max_made"], 1)
                            if j > 0:
                                i = j - 1
                                dve.wait_ge(S["exped"], c * CT + i + 1)
                                ch.link(dve.tensor_reduce(sums(i), by_head(scores(i)), AX, ALU.add))
                                ch.link(dve.reciprocal(sums(i), sums(i)))
                                dve.wait_ge(S["y_ps"], c * CT + i + 1)
                                dve.tensor_tensor(A0[:, i, :].rearrange("p (g r n) -> p g r n", g=3, r=4),
                                                  ps[0:TR, 7, 0:D].rearrange("p (g r n) -> p g r n", g=3, r=4),
                                                  bc(sums(i).rearrange("p (r g) -> p g r", r=4).unsqueeze(3), [TR, 3, 4, HD]),
                                                  ALU.mult).then_inc(S["y_made"], 1)
                        dve.wait_ge(S["o_ps"], c + 1)
                        ch.link(dve.tensor_tensor(as_tiles(A1), halves(2), as_tiles(A2), ALU.add))
                        ch.link(dve.tensor_tensor(A1[:, :, :], A1[:, :, :],
                                                  bc(tab["bp1"][:, :].unsqueeze(1), [TR, CT, D]), ALU.add))
                        norm_dve(dve, ch, S, A2, A1, c * 2 + 1)
                        dve.wait_ge(S["logits_ps"], c + 1)
                        dve.tensor_tensor(logits[:, ds(c * CT, CT), 0:9],
                                          ps[0:TR, 4, 0:CT * 9].rearrange("p (t n) -> p t n", t=CT),
                                          bc(tab["bgate1"][:, :].unsqueeze(1), [TR, CT, 9]), ALU.add)
                        dve.wait_ge(S["mlp_ps"], c + 1)
                        dve.tensor_tensor(G2[:, ds(c * CT, CT), :].rearrange("p (b t) n -> p b t n", b=2), halves(0),
                                          bc(tab["bcom2"][:, :].unsqueeze(1).unsqueeze(1), [TR, 2, 2, D]),
                                          ALU.add).then_inc(S["chunk_done"], 1)
                        ch.end()

        def ffn_and_retention():
            with stage() as ctx:
                names = ("g1_made stats_made rstd_made normed tr_ps hT_made hid_ps hid_made mlp_ps v_ps v_made g_ps g_made "
                         "qk_ps qk_taken rotated s_ps p_made pv_ps sums_made mean_ps centered squared sq_made var_ps "
                         "var_made gstd_made gated o_ps logits_ps chunk_done dve_step pool_step")
                S = {n: ctx.semaphore("c_" + n) for n in names.split()}
                block = ctx.block()
                v = big[0:TR, 0:CT * RH * RV].rearrange("p (t n) -> p t n", t=CT)
                gate = big2[:, :].rearrange("p (g n) -> p g n", g=3)
                og = big[:, 0:3 * CW].rearrange("p (g n) -> p g n", g=3)
                sq = big[:, 3 * CW:6 * CW]
                rot = lambda i: sc[:, i * CW:(i + 1) * CW]
                imgs = lambda x: x.rearrange("p (b n) -> p b n", n=L)
                probs = lambda h: (A0, A1)[h % 2][:, :, :].rearrange("p t n -> p (t n)")[:, 0:CW].rearrange(
                    "p (t n) -> p t n", t=CT)
                gstat = lambda i: small[:, i * 24:(i + 1) * 24]
                by_image = lambda x: bc(x.rearrange("p (g b) -> p g b", g=3).unsqueeze(3), [128, 3, CB, L])
                og4 = og.rearrange("p g (b n) -> p g b n", n=L)
                o_ps = ps[:, 4:7, 0:CW].rearrange("p g (b n) -> p g b n", n=L)
                qb = lambda h: 2 * (h % 2)

                @block.tensor
                def _(pe):
                    def qk_of(c, h):
                        if h >= 2:
                            pe.wait_ge(S["qk_taken"], c * RH + h - 1)
                        for a, w in enumerate((tab["wq3"], tab["wk3"])):
                            for k in range(2):
                                mm = pe.matmul(ps[:, qb(h) + a, 0:CW], w[:, k, h * RQK:(h + 1) * RQK], hT[:, k, :],
                                               start=(k == 0), stop=(k == 1))
                        mm.then_inc(S["qk_ps"], 1)

                    with pe.Fori(0, NCH) as c:
                        pe.wait_ge(S["normed"], c * 4 + 2)
                        transpose_chunk(pe, A2, 0).then_inc(S["tr_ps"], 1)
                        pe.wait_ge(S["hT_made"], c * 3 + 1)
                        mlp_pe(pe, S, c, tab["ffn1"], tab["ffn2"])
                        pe.wait_ge(S["normed"], c * 4 + 3)
                        transpose_chunk(pe, A2, 0).then_inc(S["tr_ps"], 1)
                        pe.wait_ge(S["hT_made"], c * 3 + 2)
                        project(pe, hT, tab["wv3"], RH * RV, lambda j: ps[0:TR, 4 + j, 0:RH * RV]).then_inc(S["v_ps"], 1)
                        for g in range(3):
                            for k in range(2):
                                mm = pe.matmul(ps[:, (2, 3, 0)[g], 0:CW], tab["wg3"][:, k, g * 128:(g + 1) * 128], hT[:, k, :],
                                               start=(k == 0), stop=(k == 1))
                        mm.then_inc(S["g_ps"], 1)
                        pe.wait_ge(S["g_made"], c + 1)
                        qk_of(c, 0)
                        qk_of(c, 1)
                        pe.wait_ge(S["v_made"], c + 1)
                        for h in range(RH):
                            pe.wait_ge(S["rotated"], c * RH + h + 1)
                            if h > 0:
                                pe.wait_ge(S["p_made"], c * RH + h)
                            q, k = rot(2 * (h % 2)), rot(2 * (h % 2) + 1)
                            for j in range(CT):
                                t = slice(j * TR, (j + 1) * TR)
                                mm = pe.matmul(ps[0:TR, 7, t], k[:, t], q[:, t], start=True, stop=True)
                            mm.then_inc(S["s_ps"], 1)
                            if h + 2 < RH:
                                qk_of(c, h + 2)
                            pe.wait_ge(S["p_made"], c * RH + h + 1)
                            for j in range(CT):
                                mm = pe.matmul(ps[(h % 2) * 64:(h % 2) * 64 + 64, 4 + h // 2, j * TR:(j + 1) * TR],
                                               v[:, j, h * RV:(h + 1) * RV], probs(h)[:, j, :], start=True, stop=True)
                        mm.then_inc(S["pv_ps"], 1)
                        pe.wait_ge(S["sums_made"], c + 1)
                        pe.matmul(ps[:, 0, 0:24], tab["head_mean"][:, :], gstat(0), start=True, stop=True).then_inc(S["mean_ps"], 1)
                        pe.wait_ge(S["sq_made"], c + 1)
                        pe.matmul(ps[:, 1, 0:24], tab["head_mean"][:, :], gstat(1), start=True, stop=True).then_inc(S["var_ps"], 1)
                        pe.wait_ge(S["gated"], c + 1)
                        project(pe, og, tab["wo3"], D, lambda j: ps[0:TR, 2 + j // 2, (j % 2) * D:(j % 2 + 1) * D], 3).then_inc(
                            S["o_ps"], 1)
                        pe.wait_ge(S["normed"], c * 4 + 4)
                        transpose_chunk(pe, A2, 0).then_inc(S["tr_ps"], 1)
                        pe.wait_ge(S["hT_made"], c * 3 + 3)
                        project(pe, hT, tab["gate3"], 8, lambda j: ps[0:TR, 4, j * 8:(j + 1) * 8]).then_inc(S["logits_ps"], 1)

                @block.scalar
                def _(act):
                    with act.Fori(0, NCH) as c:
                        turn_act(act, S, c * 3)
                        mlp_act(act, S, c, tab["bffn1"])
                        turn_act(act, S, c * 3 + 1)
                        act.wait_ge(S["v_ps"], c + 1)
                        act.wait_ge(S["mlp_ps"], c + 1)
                        act.activation(v, ps[0:TR, 4:8, 0:RH * RV], ACT.Copy).then_inc(S["v_made"], 1)
                        act.wait_ge(S["g_ps"], c + 1)
                        for g in range(3):
                            ins = act.activation(gate[:, g, :], ps[:, (2, 3, 0)[g], 0:CW], ACT.Silu)
                        ins.then_inc(S["g_made"], 1)
                        act.wait_ge(S["centered"], c + 1)
                        act.activation(sq, og.rearrange("p g n -> p (g n)"), ACT.Square).then_inc(S["squared"], 1)
                        turn_act(act, S, c * 3 + 2)

                @block.gpsimd
                def _(pool):
                    ch = Chain(pool, S["pool_step"], 4)
                    pool.sem_inc(S["chunk_done"], 1)
                    with pool.Fori(0, NCH) as c:
                        ch.start(c)
                        combine_pool(pool, S, c)
                        for i in range(3):
                            norm_pool(pool, ch, S, c * 4 + i)
                        for h in range(RH):
                            pool.wait_ge(S["qk_taken"], c * RH + h + 1)
                            for a in range(2):
                                ins = pool.tensor_tensor(rot(2 * (h % 2) + a), rot(2 * (h % 2) + a), rot(4 + a), ALU.add)
                            ins.then_inc(S["rotated"], 1)
                        pool.wait_ge(S["var_made"], c + 1)
                        pool.tensor_tensor(gstat(1), gstat(1), negh[:, 0:24], ALU.pow).then_inc(S["gstd_made"], 1)
                        norm_pool(pool, ch, S, c * 4 + 3)
                        hold(pool, S["normed"], c * 4 + 4)
                        pool.tensor_copy(H[:, ds(c * CT, CT), :], A2[:, :, :]).then_inc(S["chunk_done"], 1)
                        ch.end()

                @block.vector
                def _(dve):
                    def weigh(dve, c, h):
                        dve.wait_ge(S["s_ps"], c * RH + h + 1)
                        dve.tensor_tensor(probs(h), ps[0:TR, 7, 0:CW].rearrange("p (t n) -> p t n", t=CT),
                                          bc(tab["decayT"][:, h, :].unsqueeze(1), [TR, CT, TR]),
                                          ALU.mult).then_inc(S["p_made"], 1)

                    ch = Chain(dve, S["dve_step"], 13)
                    dve.sem_inc(S["chunk_done"], 1)
                    with dve.Fori(0, NCH) as c:
                        ch.start(c)
                        dve.wait_ge(S["chunk_done"], c * 2 + 2)
                        combine_dve(dve, ch, S, c, True)
                        norm_dve(dve, ch, S, A2, A1, c * 4)
                        dve.wait_ge(S["normed"], c * 4 + 1)
                        ch.link(dve.tensor_tensor(A1[:, :, :], A2[:, :, :],
                                                  bc(pbias[:, :].unsqueeze(1), [TR, CT, D]), ALU.add))
                        norm_dve(dve, ch, S, A2, A1, c * 4 + 1)
                        dve.wait_ge(S["mlp_ps"], c + 1)
                        ch.link(dve.tensor_tensor(as_tiles(A1), halves(0), as_tiles(A2), ALU.add))
                        norm_dve(dve, ch, S, A2, A1, c * 4 + 2)
                        for h in range(RH):
                            dve.wait_ge(S["qk_ps"], c * RH + h + 1)
                            if h > 0:
                                dve.wait_ge(S["rotated"], c * RH + h)
                            for a, n in enumerate("qk"):
                                x = ps[:, qb(h) + a, 0:CW]
                                r, t = rot(2 * (h % 2) + a), rot(4 + a)
                                co, si = tab["cos_" + n], tab["sin_" + n]
                                dve.tensor_tensor(imgs(r), imgs(x), bc(co[:, :].unsqueeze(1), [128, CB, L]), ALU.mult)
                                for p, o in ((0, 64), (64, 0)):
                                    ins = dve.tensor_tensor(imgs(t[o:o + 64, :]), imgs(x[p:p + 64, :]),
                                                            bc(si[p:p + 64, :].unsqueeze(1), [64, CB, L]), ALU.mult)
                            ins.then_inc(S["qk_taken"], 1)
                            if h > 0:
                                weigh(dve, c, h - 1)
                        weigh(dve, c, RH - 1)
                        dve.wait_ge(S["pv_ps"], c + 1)
                        dve.tensor_reduce(gstat(0), o_ps, AX, ALU.add).then_inc(S["sums_made"], 1)
                        dve.wait_ge(S["mean_ps"], c + 1)
                        ch.link(dve.tensor_copy(gstat(0), ps[:, 0, 0:24]))
                        dve.tensor_tensor(og4, o_ps, by_image(gstat(0)), ALU.subtract).then_inc(S["centered"], 1)
                        dve.wait_ge(S["squared"], c + 1)
                        dve.tensor_reduce(gstat(1), sq.rearrange("p (g n) -> p g n", n=L), AX, ALU.add).then_inc(S["sq_made"], 1)
                        dve.wait_ge(S["var_ps"], c + 1)
                        dve.tensor_scalar(gstat(1), ps[:, 1, 0:24], EPS, None, ALU.add).then_inc(S["var_made"], 1)
                        dve.wait_ge(S["gstd_made"], c + 1)
                        ch.link(dve.tensor_tensor(og4, og4, by_image(gstat(1)), ALU.mult))
                        for g in range(3):
                            ins = dve.tensor_scalar(og[:, g, :], og[:, g, :], tab["gnw"][:, g:g + 1], tab["gnb"][:, g:g + 1],
                                                    ALU.mult, ALU.add)
                        ch.link(ins)
                        dve.tensor_tensor(og, og, gate, ALU.mult).then_inc(S["gated"], 1)
                        dve.wait_ge(S["o_ps"], c + 1)
                        ch.link(dve.tensor_tensor(as_tiles(A1), halves(2), as_tiles(A2), ALU.add))
                        norm_dve(dve, ch, S, A2, A1, c * 4 + 3)
                        dve.wait_ge(S["logits_ps"], c + 1)
                        dve.tensor_scalar(logits[:, ds(c * CT, CT), 0:8],
                                          ps[0:TR, 4, 0:CT * 8].rearrange("p (t n) -> p t n", t=CT),
                                          1.0, None, ALU.mult).then_inc(S["chunk_done"], 1)
                        ch.end()

        def last_norm():
            with stage() as ctx:
                names = "g1_made stats_made rstd_made normed stored chunk_done dve_step pool_step"
                S = {n: ctx.semaphore("d_" + n) for n in names.split()}
                block = ctx.block()
                rows = out.rearrange("(t p) n -> p t n", p=TR)

                @block.sync
                def _(sp):
                    sp.sem_inc(S["chunk_done"], 1)
                    with sp.Fori(0, NCH) as c:
                        sp.wait_ge(S["normed"], c + 1)
                        sp.dma_start(rows[:, ds(c * CT, CT), :], A2[:, :, :]).then_inc(S["stored"], 16)
                        sp.wait_ge(S["stored"], c * 16 + 16)
                        sp.sem_inc(S["chunk_done"], 1)

                @block.gpsimd
                def _(pool):
                    ch = Chain(pool, S["pool_step"], 1)
                    pool.sem_inc(S["chunk_done"], 1)
                    with pool.Fori(0, NCH) as c:
                        ch.start(c)
                        combine_pool(pool, S, c)
                        norm_pool(pool, ch, S, c)
                        pool.sem_inc(S["chunk_done"], 1)
                        ch.end()

                @block.vector
                def _(dve):
                    ch = Chain(dve, S["dve_step"], 2)
                    with dve.Fori(0, NCH) as c:
                        ch.start(c)
                        dve.wait_ge(S["chunk_done"], c * 2 + 2)
                        combine_dve(dve, ch, S, c, False)
                        norm_dve(dve, ch, S, A2, A1, c)
                        ch.end()

        setup()
        embed_and_rope_attention()
        route(0)
        experts(0)
        causal_attention()
        route(1)
        experts(1)
        ffn_and_retention()
        route(2)
        experts(2)
        last_norm()


def halves_k(w):
    return w.reshape(2, DH, -1).transpose(1, 0, 2)


def rows_k(w):
    return w.reshape(-1, 128, w.shape[-1]).transpose(1, 0, 2)


def lay_out(i):
    d = dict(constants())
    rep = lambda v: np.tile(np.asarray(v)[None], (TR, 1))
    x = i["x"].reshape(B, 3, 7, 16, 7, 16).transpose(1, 3, 5, 0, 2, 4).reshape(PK, 128, NCH, CW)
    d["patches"] = x.transpose(2, 1, 0, 3).reshape(NCH, 128, PK * CW)
    d["conv_w"] = rows_k(i["L0_tok_conv_w"].reshape(D, -1).T)
    d["conv_b"] = rep(i["L0_tok_conv_b"])
    bounds = np.arange(1.0 / 32, 1.0, 1.0 / 32, dtype=np.float32)
    at = np.searchsorted(bounds, np.arange(0.0, 1.0 - 1e-06, 1.0 / 7, dtype=np.float32), side="right")
    ids = (at[:, None] * 32 + at).reshape(-1)
    pos = i["L0_tok_pos_table"][ids]
    d["pos"] = np.concatenate([pos, pos], 0)
    d["wv0"] = halves_k(i["L0_attn_Wv"].T)
    d["wo0"] = i["L0_attn_Wo"].T
    d["gate0"] = halves_k(i["L0_ffn_gate_w"].T)
    w, b = i["L1_attn_W_attn"], i["L1_attn_b_attn"]
    wqk = np.zeros((D, 6, 4, 32), np.float32)
    bqk = np.zeros((6, 4, 32), np.float32)
    wqk[..., :HD] = w[:, :2 * D].reshape(D, 6, 4, HD)
    bqk[..., :HD] = b[:2 * D].reshape(6, 4, HD)
    d["wqk1"] = halves_k(wqk.reshape(D, -1)).reshape(DH, 2, 6, 128)
    d["bqk1"] = bqk.reshape(6, 128).T
    d["wv1"], d["bv1"] = halves_k(w[:, 2 * D:]), rep(b[2 * D:])
    d["wp1"], d["bp1"] = halves_k(i["L1_attn_W_proj"]), rep(i["L1_attn_b_proj"])
    d["gate1"], d["bgate1"] = halves_k(i["L1_ffn_Ws"]), rep(i["L1_ffn_bs"])
    d["com1"], d["bcom1"] = halves_k(i["L1_ffn_W1"][0]), i["L1_ffn_b1"][0].reshape(FM, 128).T
    d["com2"], d["bcom2"] = rows_k(i["L1_ffn_W2"][0]), rep(i["L1_ffn_b2"][0])
    d["proj_w"], d["proj_b"] = halves_k(i["L2_attn_proj_w"].T), rep(i["L2_attn_proj_b"])
    d["ffn1"], d["bffn1"] = halves_k(i["L2_ffn_in_weight"].T), i["L2_ffn_in_bias"].reshape(FM, 128).T
    d["ffn2"] = rows_k(i["L2_ffn_out_weight"])
    for n, k in (("wq3", "Wq"), ("wk3", "Wk"), ("wv3", "Wv"), ("wg3", "Wg")):
        d[n] = halves_k(i["L3_attn_" + k])
    d["wo3"] = rows_k(i["L3_attn_Wo"])
    d["gnw"], d["gnb"] = (i["L3_attn_gn_" + n].reshape(3, 128).T for n in ("weight", "bias"))
    d["gate3"] = halves_k(i["L3_ffn_router_w"])
    ek = lambda w: w.reshape(w.shape[0], 2, DH, -1).transpose(0, 2, 1, 3).reshape(w.shape[0], DH, -1)
    er = lambda w: w.reshape(w.shape[0], -1, 128, w.shape[-1]).transpose(0, 2, 1, 3).reshape(w.shape[0], 128, -1)
    col = lambda b: b.reshape(b.shape[0], -1, 128).transpose(0, 2, 1)
    d["e0_a"] = ek(i["L0_ffn_W1"])
    d["e0_b"] = np.concatenate([er(i["L0_ffn_W2"]), er(i["L0_ffn_W3"]), col(i["L0_ffn_b1"]), col(i["L0_ffn_b2"])], -1)
    d["e0_c"] = np.concatenate([i["L0_ffn_Wl"], i["L0_ffn_b3"][:, :, None]], -1)
    d["e0_d"] = i["L0_ffn_bl"][:, None]
    d["e1_a"] = ek(i["L1_ffn_W1"])
    d["e1_b"] = np.concatenate([er(i["L1_ffn_W2"]), col(i["L1_ffn_b1"])], -1)
    d["e1_d"] = i["L1_ffn_b2"][:, None]
    d["e2_a"] = ek(i["L3_ffn_wi"])
    d["e2_b"] = er(i["L3_ffn_wo"])
    return {k: np.ascontiguousarray(v) for k, v in d.items()}


def kernel(**inputs):
    import concourse.bacc as bacc
    from concourse.bass_utils import run_bass_kernel_spmd

    arrays = lay_out({k: np.asarray(v) for k, v in inputs.items()})
    nc = bacc.Bacc("TRN2", target_bir_lowering=False, num_devices=1)
    d = {k: nc.dram_tensor(k, v.shape, mybir.dt.from_np(v.dtype), kind="ExternalInput").ap()
         for k, v in arrays.items()}
    out = nc.dram_tensor("out", [NTOK, D], F32, kind="ExternalOutput").ap()
    build(nc, d, out)
    r = run_bass_kernel_spmd(nc, [arrays], core_ids=[0])
    return r.results[0]["out"].reshape(B, L, D)
```

```python
from contextlib import ExitStack

import numpy as np

import concourse.bass as bass
from concourse import mybir

F32 = mybir.dt.float32
I32 = mybir.dt.int32
BF16 = mybir.dt.bfloat16
ALU = mybir.AluOpType
ACT = mybir.ActivationFunctionType
AX = mybir.AxisListType.X
ds = bass.ds

B, L = 32, 49
D, DH = 192, 96
TR = 2 * L
NT = B // 2
CT = 2
NCH = NT // CT
CW = CT * TR
CB = CW // L
LANES = range(2)
NSTEP = NCH // 2
NTOK = B * L
PK = 3 * 16 * 16 // 128
SLOT = 128
HEADS, HD = 12, 16
RH, RQK, RV = 6, 128, 64
FF = 768
FM = FF // 128
EPS = 1e-5
NEG = -1.0e30
PSB = 512
HALF = PSB // 2


def max_tiles(experts, k):
    n = (NTOK * k - experts) // SLOT + experts
    return n + n % 2


MOE = {0: (32, 2), 1: (9, 1), 2: (8, 1)}
TMAX = max(max_tiles(*v) for v in MOE.values())
THR = (NTOK + SLOT - 1) // SLOT


def constants():
    c = {}
    c["ident"] = np.eye(128, dtype=np.float32)
    blk = np.kron(np.eye(2), np.ones((L, L)))
    c["block_neg"] = np.where(blk > 0, 0.0, NEG).astype(np.float32)
    causal = np.kron(np.eye(2), np.tril(np.ones((L, L))))
    c["causal_neg"] = np.where(causal > 0, 0.0, NEG).astype(np.float32)
    pos = np.arange(L, dtype=np.float32)
    fr = (10000.0 ** (-np.arange(0, D, 2, dtype=np.float32) / D)).astype(np.float32)
    ang = (pos[:, None] * fr[None]).astype(np.float32).astype(np.float64)
    r = np.concatenate([np.sin(ang), np.cos(ang)], -1).astype(np.float32)
    c["ropeT"] = np.concatenate([r, r], 0).T.reshape(2, DH, TR).transpose(1, 0, 2).copy()
    i = np.arange(TR)
    c["before"] = (i[:, None] < i[None]).astype(np.float32)
    c["ones"] = np.ones((128, 128), np.float32)
    c["rank_order"] = np.tile(64.0 - np.arange(32, dtype=np.float32), (TR, 1))
    e = np.arange(32)
    c["exp_order"] = np.stack([SLOT * (e[:, None] < e[None]), 1 * (e[:, None] <= e[None])], 1).astype(np.float32)
    c["fills"] = np.tile(SLOT * np.arange(THR, dtype=np.float32), (32, 1))
    c["tile_no"] = np.arange(TMAX + 1, dtype=np.float32)[None]
    c["pair_no"] = (2 * np.arange(TMAX // 2, dtype=np.float32))[None]
    half = RQK // 2
    p64 = np.arange(L, dtype=np.float64)
    inv = 1.0 / 10000.0 ** (np.arange(half) / half)
    a = p64[:, None] * inv[None]
    zeta = (np.arange(half) + half) / RQK
    cos, sin = [], []
    for s in (1.0, -1.0):
        dec = zeta[None] ** (s * p64[:, None] / 512.0)
        co, si = (np.cos(a) * dec).T, (np.sin(a) * dec).T
        cos.append(np.concatenate([co, co], 0))
        sin.append(np.concatenate([si, -si], 0))
    c["cos_qk"], c["sin_qk"] = np.stack(cos, 1).astype(np.float32), np.stack(sin, 1).astype(np.float32)
    g = 1.0 - 2.0 ** (-(5.0 + np.arange(RH)))
    diff = p64[:, None] - p64[None]
    dm = g[:, None, None] ** np.clip(diff, 0, None)[None] * (diff >= 0)[None]
    dm = dm / np.sqrt(np.clip(dm.sum(-1, keepdims=True), 1e-6, None)) * RQK ** -0.5
    c["decayT"] = np.stack([np.kron(np.eye(2), m.T) for m in dm], 1).astype(np.float32)
    hb = np.kron(np.eye(2), np.ones((RV, RV))) / (RV * L)
    c["head_mean"] = hb.astype(np.float32)
    return c


def hold(eng, sem, value):
    eng.wait_ge(sem, value)
    eng.nop(nofuse=True)


class Chain:

    def __init__(self, eng, sem, per_pass=0):
        self.eng, self.sem, self.n, self.base, self.per_pass = eng, sem, 0, 0, per_pass

    def start(self, i, before=0):
        self.n, self.base = 0, i * self.per_pass + before

    def link(self, ins, alone=False):
        self.n += 1
        ins.then_inc(self.sem, 1)
        if alone:
            hold(self.eng, self.sem, self.base + self.n)
        else:
            self.eng.wait_ge(self.sem, self.base + self.n)

    def end(self):
        assert self.n == self.per_pass, f"links per pass: {self.n}, not {self.per_pass}"


def build(nc, d, out):
    top = ExitStack()
    with top:
        def sb(name, shape, dt=F32):
            return top.enter_context(nc.sbuf_tensor(name, shape, dt))

        def dram(name, shape):
            return nc.dram_tensor(name, shape, F32).ap()

        ps = top.enter_context(nc.psum_tensor("ps", [128, 8, PSB], F32))
        slots_in = dram("slots_in", [(TMAX + 8) * SLOT, D])
        slots_out = dram("slots_out", [TMAX * SLOT, D])

        tab = {}
        loads = []

        def resident(name, shape):
            tab[name] = sb("t_" + name, shape)
            loads.append((tab[name], d[name]))

        for n in ("ropeT block_neg proj_w".split()):
            resident(n, {"ropeT": [DH, 2, TR], "block_neg": [TR, TR], "proj_w": [DH, 2, D]}[n])
        resident("ident", [128, 128])
        resident("before", [TR, TR])
        resident("ones", [128, 128])
        resident("proj_b", [TR, D])
        resident("pos", [TR, D])
        resident("conv_b", [TR, D])
        resident("conv_w", [128, PK, D])
        resident("wv0", [DH, 2, 64])
        resident("wo0", [64, D])
        resident("gate0", [DH, 2, 32])
        early = len(loads)
        resident("causal_neg", [TR, TR])
        resident("rank_order", [TR, 32])
        resident("exp_order", [32, 2, 32])
        resident("fills", [32, THR])
        resident("tile_no", [1, TMAX + 1])
        resident("pair_no", [1, TMAX // 2])
        for n in ("cos_qk", "sin_qk"):
            resident(n, [128, 2, L])
        resident("decayT", [TR, RH, TR])
        resident("head_mean", [128, 128])
        resident("wqk1", [DH, 2, 6 * 128])
        resident("bqk1", [128, 6])
        resident("wv1", [DH, 2, D])
        resident("bv1", [TR, D])
        resident("wp1", [DH, 2, D])
        resident("bp1", [TR, D])
        resident("gate1", [DH, 2, 9])
        resident("bgate1", [TR, 9])
        resident("com1", [DH, 2, FF])
        resident("bcom1", [128, FM])
        resident("com2", [128, FM, D])
        resident("bcom2", [TR, D])
        resident("ffn1", [DH, 2, FF])
        resident("bffn1", [128, FM])
        resident("ffn2", [128, FM, D])
        resident("wq3", [DH, 2, RH * RQK])
        resident("wk3", [DH, 2, RH * RQK])
        resident("wv3", [DH, 2, RH * RV])
        resident("wg3", [DH, 2, RH * RV])
        resident("wo3", [128, 3, D])
        resident("gnw", [128, 3])
        resident("gnb", [128, 3])
        resident("gate3", [DH, 2, 8])
        ident = tab["ident"]

        H = sb("H", [TR, NT, D])
        common = sb("common", [TR, NT, D])
        logits = sb("logits", [TR, NT, 32])
        coef = sb("coef", [TR, 2, NT])
        slot_of = sb("slot_of", [TR, 2, NT + 2 * CT], I32)
        exp_of = sb("exp_of", [1, TMAX + 1], I32)
        n_pairs = sb("n_pairs", [1, 1], I32)
        ropeP = sb("ropeP", [TR, TR])
        negh = sb("negh", [128, 32])
        pbias = sb("pbias", [TR, D])

        before16 = sb("before16", [TR, TR], BF16)
        ones16 = sb("ones16", [TR, TR], BF16)
        mask = sb("mask", [TR, NT * 32], BF16)

        xin = [sb(f"xin{u}", [SLOT, D]) for u in range(2)]
        xT = [sb(f"xT{u}", [DH, 2, SLOT]) for u in range(2)]
        wA = [sb(f"wA{u}", [128, 2 * FF]) for u in range(2)]
        b1 = [sb(f"b1{u}", [128, FM]) for u in range(2)]
        wB = [sb(f"wB{u}", [128, 2308]) for u in range(2)]
        wC = [sb(f"wC{u}", [65, D + 1]) for u in range(2)]
        wD = [sb(f"wD{u}", [1, D]) for u in range(2)]
        hid = [sb(f"hid{u}", [128, FM, SLOT]) for u in range(2)]
        hid2 = [sb(f"hid2{u}", [128, 4, SLOT]) for u in range(2)]
        zT = [sb(f"zT{u}", [65, SLOT]) for u in range(2)]
        yo = [sb(f"yo{u}", [SLOT, D]) for u in range(2)]

        per_lane = lambda name, shape, dt=F32: [sb(f"{name}{l}", shape, dt) for l in LANES]
        A0, A1, A2 = (per_lane(n, [TR, CT, D]) for n in ("A0", "A1", "A2"))
        found = per_lane("found", [TR, 2, CT, D])
        find = per_lane("find", [TR, 2, CT], I32)
        hT = per_lane("hT", [DH, 2, CW])
        stats = per_lane("stats", [TR, CT, 6])
        mv = per_lane("mv", [TR, CT, 2])
        rstd = per_lane("rstd", [TR, CT])
        big = per_lane("big", [128, 6 * CW])
        big2 = per_lane("big2", [128, 3 * CW])
        sc = per_lane("sc", [128, HEADS * TR])
        pT = per_lane("pT", [TR, HEADS, TR])
        small = per_lane("small", [128, 64])
        r_wide = [wB[0][0:TR, n * NT * 32:(n + 1) * NT * 32] for n in range(4)] + [wA[0][0:TR, 0:NT * 32]]
        r_row = wB[1][0:1, :]
        r_small = wA[1][:, 0:1024]

        bc = lambda ap, shape: ap.broadcast_to(shape)

        ps_flat = ps[:, :, :].rearrange("p b n -> p (b n)")

        def half(l, n, rows, cols):
            o = (8 * l + n) * HALF
            return ps_flat[0:rows, o:o + cols]

        def span(l, n, count, rows, cols):
            o = (8 * l + n) * HALF
            return ps_flat[0:rows, o:o + count * HALF].rearrange("p (c n) -> p c n", c=count)[:, :, 0:cols]

        class stage:

            def __enter__(self):
                self.sems, self.stack = [], ExitStack()
                return self

            def semaphore(self, name):
                self.sems.append(nc.alloc_semaphore(name))
                return self.sems[-1]

            def block(self):
                return self.stack.enter_context(nc.Block())

            def __exit__(self, *error):
                self.stack.__exit__(*error)
                if not error[0]:
                    nc.clear_and_free_semaphores(self.sems)
                    nc.all_engine_barrier()

        def transpose_chunk(pe, src, l, n):
            for k in range(2):
                for j in range(CT):
                    mm = pe.transpose(half(l, n + k, DH, CW)[:, j * TR:(j + 1) * TR], src[:, j, k * DH:(k + 1) * DH],
                                      ident[0:TR, 0:TR])
            return mm

        def project(pe, xT, w, ncols, out_of, kk=2):
            for j in range(CT):
                for k in range(kk):
                    mm = pe.matmul(out_of(j), xT[:, k, j * TR:(j + 1) * TR], w[:, k, 0:ncols],
                                   start=(k == 0), stop=(k == kk - 1))
            return mm

        def project_wide(pe, l, n, rows, w, m, xT=None):
            for k in range(2):
                mm = pe.matmul(half(l, n, rows, CW), w[:, k, m:m + rows], hT[l][:, k, :], start=(k == 0), stop=(k == 1))
            return mm

        def norm_dve(dve, ch, S, l, i):
            for j in range(CT):
                ins = dve.bn_stats(stats[l][:, j, :], A1[l][:, j, :])
            ch.link(ins, alone=True)
            for j in range(CT):
                ins = dve.bn_aggr(mv[l][:, j, :], stats[l][:, j, :])
            ins.then_inc(S["stats_made"], 1)

        def norm_dve_end(dve, S, l, i):
            dve.wait_ge(S["rstd_made"], i + 1)
            for j in range(CT):
                ins = dve.tensor_scalar(A2[l][:, j, :], A1[l][:, j, :], mv[l][:, j, 0:1], rstd[l][:, j:j + 1],
                                        ALU.subtract, ALU.mult)
            ins.then_inc(S["normed"], 1)

        def norm_pool(pool, ch, S, l, i):
            hold(pool, S["stats_made"], i + 1)
            ch.link(pool.tensor_scalar(rstd[l][:, :], mv[l][:, :, 1], EPS, None, ALU.add))
            pool.tensor_tensor(rstd[l][:, :], rstd[l][:, :], negh[0:TR, 0:CT], ALU.pow).then_inc(S["rstd_made"], 1)

        def lane_semaphores(ctx, stage_name, names):
            return [{n: ctx.semaphore(f"{stage_name}{l}_{n}") for n in names.split()} for l in LANES]

        def turn_act(act, S, l, n, i):
            act.wait_ge(S["tr_ps"], i + 1)
            act.activation(hT[l][:, :, :], span(l, n, 2, DH, CW), ACT.Copy).then_inc(S["hT_made"], 1)

        def keep(pool, S, l, i, norms):
            hold(pool, S["normed"], norms + 1)
            pool.tensor_copy(H[:, ds((i * 2 + l) * CT, CT), :], A2[l][:, :, :]).then_inc(S["kept"], 1)

        def gather(pool, ch, S, l, chunk, choices):
            ch.link(pool.tensor_copy(find[l][:, :, :], slot_of[:, :, ds(chunk * CT, CT)]), alone=True)
            for k in range(choices):
                for j in range(CT):
                    pool.indirect_dma_start(found[l][:, k, j, :], None, slots_out,
                                            bass.IndirectOffsetOnAxis(find[l][:, k, j:j + 1], 0)).then_inc(S["gathered"], 16)

        def end_gathers(pool, S, choices):
            for l in LANES:
                pool.wait_ge(S[l]["gathered"], (NSTEP + 1) * 16 * choices * CT)

        def combine_pool(pool, S, l, i, choices):
            hold(pool, S["gathered"], (i + 1) * (16 * choices * CT))
            pool.tensor_tensor(A0[l][:, :, :], found[l][:, 0, :, :],
                               bc(coef[:, 0, ds((i * 2 + l) * CT, CT)].unsqueeze(2), [TR, CT, D]),
                               ALU.mult).then_inc(S["first_made"], 1)

        def combine_dve(dve, ch, S, l, i, second):
            tiles = ds((i * 2 + l) * CT, CT)
            dve.wait_ge(S["first_made"], i + 1)
            if second is None:
                ch.link(dve.tensor_tensor(A1[l][:, :, :], A0[l][:, :, :], H[:, tiles, :], ALU.add))
                return
            ch.link(dve.tensor_tensor(A1[l][:, :, :], second, bc(coef[:, 1, tiles].unsqueeze(2), [TR, CT, D]), ALU.mult))
            dve.tensor_tensor(A0[l][:, :, :], A0[l][:, :, :], H[:, tiles, :], ALU.add).then_inc(S["found_used"], 1)
            dve.wait_ge(S["found_used"], i + 1)
            ch.link(dve.tensor_tensor(A1[l][:, :, :], A1[l][:, :, :], A0[l][:, :, :], ALU.add))

        def hidden_pe(pe, S, l, w1):
            for m in range(FM):
                mm = project_wide(pe, l, 2 + m, 128, w1, m * 128)
                if m % 2:
                    mm.then_inc(S["hid_ps"], 1)

        def hidden_act(act, S, l, i, bias):
            for m in range(FM):
                act.wait_ge(S["hid_ps"], i * (FM // 2) + m // 2 + 1)
                ins = act.activation(big[l][:, m * CW:(m + 1) * CW], half(l, 2 + m, 128, CW), ACT.Gelu, bias=bias[:, m:m + 1])
            ins.then_inc(S["hid_made"], 1)

        def mlp_out_pe(pe, S, l, i, w2):
            pe.wait_ge(S["hid_made"], i + 1)
            project(pe, big[l][:, :].rearrange("p (k n) -> p k n", k=FM), w2, D, lambda j: half(l, j, TR, D), FM).then_inc(
                S["mlp_ps"], 1)

        def setup():
            with stage() as ctx:
                sem = ctx.semaphore
                loaded, zeros_set = sem("loaded"), sem("zeros_set")
                dve_step = sem("dve_step")
                rope_scores, shifted, exped, rope_probs, turned = (
                    sem("rope_scores"), sem("shifted"), sem("exped"), sem("rope_probs"), sem("turned"))
                zero_proj = sem("zero_proj")
                block = ctx.block()
                zeros = common[:, :, :].rearrange("p t n -> p (t n)")
                full = 16 * early

                @block.sync
                def _(sp):
                    for dst, src in loads[:early]:
                        sp.dma_start(dst[:], src).then_inc(loaded, 16)
                    sp.wait_ge(loaded, full)

                @block.tensor
                def _(pe):
                    pe.wait_ge(loaded, full)
                    for k in range(2):
                        mm = pe.matmul(ps[0:TR, 0, 0:TR], tab["ropeT"][:, k, :], tab["ropeT"][:, k, :],
                                       start=(k == 0), stop=(k == 1))
                    mm.then_inc(rope_scores, 1)
                    pe.wait_ge(zeros_set, 1)
                    for k in range(2):
                        mm = pe.matmul(ps[0:TR, 1, 0:D], zeros[0:DH, 0:TR], tab["proj_w"][:, k, :],
                                       start=(k == 0), stop=(k == 1))
                    mm.then_inc(zero_proj, 1)
                    pe.wait_ge(rope_probs, 1)
                    pe.transpose(ps[0:TR, 2, 0:TR], sc[0][0:TR, 0:TR], ident[0:TR, 0:TR]).then_inc(turned, 1)

                @block.scalar
                def _(act):
                    act.wait_ge(shifted, 1)
                    act.activation(sc[0][0:TR, 0:TR], sc[0][0:TR, 0:TR], ACT.Exp).then_inc(exped, 1)

                @block.vector
                def _(dve):
                    ch = Chain(dve, dve_step)
                    dve.memset(common[:, :, :], 0.0).then_inc(zeros_set, 1)
                    dve.memset(negh[:, :], -0.5)
                    dve.memset(slot_of[:, :, :], 0)
                    for u in range(2):
                        dve.memset(zT[u][64:65, :], 1.0)
                    dve.wait_ge(loaded, full)
                    dve.tensor_copy(before16[:, :], tab["before"][:, :])
                    dve.tensor_copy(ones16[:, :], tab["ones"][0:TR, 0:TR])
                    s = sc[0][0:TR, 0:TR]
                    dve.wait_ge(rope_scores, 1)
                    ch.link(dve.tensor_tensor(s, ps[0:TR, 0, 0:TR], tab["block_neg"][:, :], ALU.add))
                    ch.link(dve.tensor_reduce(small[0][0:TR, 0:1], s, AX, ALU.max))
                    dve.tensor_scalar(s, s, small[0][0:TR, 0:1], None, ALU.subtract).then_inc(shifted, 1)
                    dve.wait_ge(exped, 1)
                    ch.link(dve.tensor_reduce(small[0][0:TR, 1:2], s, AX, ALU.add))
                    ch.link(dve.reciprocal(small[0][0:TR, 2:3], small[0][0:TR, 1:2]))
                    dve.tensor_scalar(s, s, small[0][0:TR, 2:3], None, ALU.mult).then_inc(rope_probs, 1)
                    ch.link(dve.tensor_tensor(tab["pos"][:, :], tab["pos"][:, :], tab["conv_b"][:, :], ALU.add))
                    dve.wait_ge(zero_proj, 1)
                    dve.tensor_tensor(pbias[:, :], ps[0:TR, 1, 0:D], tab["proj_b"][:, :], ALU.add)
                    dve.wait_ge(turned, 1)
                    dve.tensor_copy(ropeP[:, :], ps[0:TR, 2, 0:TR])

        def embed_and_rope_attention():
            with stage() as ctx:
                S = lane_semaphores(ctx, "a", "patches_in emb_ps h0_made tr_ps hT_made v_ps v_made av_ps av_made o_ps "
                                    "stats_made rstd_made normed kept logits_ps logits_taken")
                dve_step, pool_step, cleared, loaded = map(ctx.semaphore, "a_dve_step a_pool_step a_cleared a_loaded".split())
                block = ctx.block()
                patches = [x[:, :].rearrange("p (k n) -> p k n", k=PK) for x in big]
                v = [x[0:TR, 0:CT * 64].rearrange("p (t n) -> p t n", t=CT) for x in big2]
                av = [x[0:64, 2 * CW:3 * CW] for x in big2]

                @block.sync
                def _(sp):
                    for l in LANES:
                        sp.dma_start(big[l][:, :], d["patches"][l]).then_inc(S[l]["patches_in"], 16)
                    with sp.Fori(1, NSTEP) as i:
                        for l in LANES:
                            hold(sp, S[l]["emb_ps"], i)
                            sp.dma_start(big[l][:, :], d["patches"][ds(i * 2 + l, 1)].rearrange("o p n -> (o p) n")
                                         ).then_inc(S[l]["patches_in"], 16)
                    for dst, src in loads[early:]:
                        sp.dma_start(dst[:], src).then_inc(loaded, 16)
                    sp.wait_ge(loaded, 16 * (len(loads) - early))

                @block.tensor
                def _(pe):
                    with pe.Fori(0, NSTEP) as i:
                        for l in LANES:
                            pe.wait_ge(S[l]["patches_in"], i * 16 + 16)
                            project(pe, patches[l], tab["conv_w"], D, lambda j: half(l, j, TR, D), PK).then_inc(
                                S[l]["emb_ps"], 1)
                        for l in LANES:
                            pe.wait_ge(S[l]["h0_made"], i + 1)
                            transpose_chunk(pe, A0[l], l, 2).then_inc(S[l]["tr_ps"], 1)
                        for l in LANES:
                            pe.wait_ge(S[l]["hT_made"], i * 2 + 1)
                            project(pe, hT[l], tab["wv0"], 64, lambda j: half(l, 4, TR, 128)[:, j * 64:(j + 1) * 64]).then_inc(
                                S[l]["v_ps"], 1)
                        for l in LANES:
                            pe.wait_ge(S[l]["v_made"], i + 1)
                            for j in range(CT):
                                mm = pe.matmul(half(l, 6, 64, CW)[:, j * TR:(j + 1) * TR], v[l][:, j, :], ropeP[:, :],
                                               start=True, stop=True)
                            mm.then_inc(S[l]["av_ps"], 1)
                        for l in LANES:
                            pe.wait_ge(S[l]["av_made"], i + 1)
                            for j in range(CT):
                                mm = pe.matmul(half(l, j, TR, D), av[l][:, j * TR:(j + 1) * TR], tab["wo0"][:, :],
                                               start=True, stop=True)
                            mm.then_inc(S[l]["o_ps"], 1)
                        for l in LANES:
                            pe.wait_ge(S[l]["normed"], i + 1)
                            transpose_chunk(pe, A2[l], l, 2).then_inc(S[l]["tr_ps"], 1)
                        for l in LANES:
                            pe.wait_ge(S[l]["hT_made"], i * 2 + 2)
                            project(pe, hT[l], tab["gate0"], 32, lambda j: half(l, 4, TR, 64)[:, j * 32:(j + 1) * 32]).then_inc(
                                S[l]["logits_ps"], 1)

                @block.scalar
                def _(act):
                    with act.Fori(0, NSTEP) as i:
                        for l in LANES:
                            turn_act(act, S[l], l, 2, i * 2)
                        for l in LANES:
                            act.wait_ge(S[l]["v_ps"], i + 1)
                            act.activation(big2[l][0:TR, 0:CT * 64], half(l, 4, TR, CT * 64), ACT.Copy).then_inc(
                                S[l]["v_made"], 1)
                        for l in LANES:
                            act.wait_ge(S[l]["av_ps"], i + 1)
                            act.activation(av[l], half(l, 6, 64, CW), ACT.Copy).then_inc(S[l]["av_made"], 1)
                        for l in LANES:
                            turn_act(act, S[l], l, 2, i * 2 + 1)

                @block.gpsimd
                def _(pool):
                    for buf in (slots_in, slots_out):
                        w = buf.rearrange("(t p n) d -> t p (n d)", p=64, n=16)
                        for t in range(w.shape[0]):
                            pool.dma_start(w[t], common[0:64, :, :].rearrange("p t n -> p (t n)")).then_inc(cleared, 16)
                    ch = Chain(pool, pool_step, 2)
                    for l in LANES:
                        pool.sem_inc(S[l]["kept"], 1)
                    with pool.Fori(0, NSTEP) as i:
                        ch.start(i)
                        for l in LANES:
                            norm_pool(pool, ch, S[l], l, i)
                        for l in LANES:
                            keep(pool, S[l], l, i, i)
                        ch.end()
                    pool.wait_ge(cleared, (2 * TMAX + 8) * SLOT // 64 // 16 * 16)

                @block.vector
                def _(dve):
                    ch = Chain(dve, dve_step, 4)
                    with dve.Fori(0, NSTEP) as i:
                        ch.start(i)
                        for l in LANES:
                            dve.wait_ge(S[l]["emb_ps"], i + 1)
                            dve.tensor_tensor(A0[l][:, :, :], span(l, 0, 2, TR, D),
                                              bc(tab["pos"][:, :].unsqueeze(1), [TR, CT, D]), ALU.add).then_inc(
                                S[l]["h0_made"], 1)
                        for l in LANES:
                            dve.wait_ge(S[l]["o_ps"], i + 1)
                            ch.link(dve.tensor_tensor(A1[l][:, :, :], span(l, 0, 2, TR, D), A0[l][:, :, :], ALU.add))
                            norm_dve(dve, ch, S[l], l, i)
                        for l in LANES:
                            dve.wait_ge(S[l]["kept"], i + 1)
                            norm_dve_end(dve, S[l], l, i)
                        for l in LANES:
                            dve.wait_ge(S[l]["logits_ps"], i + 1)
                            dve.tensor_scalar(logits[:, ds((i * 2 + l) * CT, CT), :],
                                              half(l, 4, TR, 64).rearrange("p (t n) -> p t n", t=CT),
                                              1.0, None, ALU.mult)
                        ch.end()

        def route(r):
            E, K = MOE[r]
            with stage() as ctx:
                sem = lambda n: ctx.semaphore(f"r{r}_{n}")
                dve_step, shifted, exped, masked, ranked, tiles_known, starts_ps, slots_known, scattered = map(
                    sem, ("dve_step shifted exped masked ranked tiles_known starts_ps slots_known scattered").split())
                block = ctx.block()
                wide = lambda i: r_wide[i][:, 0:NT * E].rearrange("p (t e) -> p t e", t=NT)
                probs, cand, at_slot = wide(0), wide(1), wide(2)
                hot = [wide(3), wide(4)]
                tiny = lambda i: r_small[0:TR, 512 + i * NT:512 + (i + 1) * NT]
                over_e = lambda x: bc(x.unsqueeze(2), [TR, NT, E])
                order = bc(tab["rank_order"][:, 0:E].unsqueeze(1), [TR, NT, E])

                @block.scalar
                def _(act):
                    act.wait_ge(shifted, 1)
                    act.activation(probs, probs, ACT.Exp).then_inc(exped, 1)

                @block.tensor
                def _(pe):
                    pe.wait_ge(masked, 1)
                    m = lambda j, n=1: mask[:, j * E:(j + n) * E]
                    pe.matmul(ps[0:TR, 0, 0:NT * E], before16[:, :], m(0, NT), start=True, stop=True)
                    for j in range(NT - 1):
                        mm = pe.matmul(ps[0:TR, 0, (j + 1) * E:NT * E].rearrange("p (t e) -> p t e", e=E),
                                       ones16[0:TR, 0:TR], bc(m(j).unsqueeze(1), [TR, NT - 1 - j, E]),
                                       start=False, stop=True, skip_group_check=True)
                    for j in range(NT):
                        mm = pe.matmul(ps[0:E, 1, 0:1], m(j), ones16[0:TR, 0:1], start=(j == 0), stop=(j == NT - 1))
                    mm.then_inc(ranked, 1)
                    pe.wait_ge(tiles_known, 1)
                    pe.matmul(ps[0:TR, 2, 0:2 * E].rearrange("p (a e) -> p a e", a=2), r_small[0:E, 0:TR],
                              tab["exp_order"][0:E, :, 0:E], start=True, stop=True).then_inc(starts_ps, 1)

                @block.gpsimd
                def _(pool):
                    pool.wait_ge(slots_known, K)
                    for k in range(K):
                        for t in range(NT):
                            pool.indirect_dma_start(slots_in, bass.IndirectOffsetOnAxis(slot_of[:, k, t:t + 1], 0),
                                                    H[:, t, :], None).then_inc(scattered, 16)
                    pool.wait_ge(scattered, 16 * K * NT)

                @block.vector
                def _(dve):
                    ch = Chain(dve, dve_step)
                    ch.link(dve.tensor_reduce(tiny(0), logits[:, :, 0:E], AX, ALU.max))
                    dve.tensor_tensor(probs, logits[:, :, 0:E], over_e(tiny(0)), ALU.subtract).then_inc(shifted, 1)
                    dve.wait_ge(exped, 1)
                    ch.link(dve.tensor_reduce(tiny(1), probs, AX, ALU.add))
                    ch.link(dve.reciprocal(tiny(2), tiny(1)))
                    ch.link(dve.tensor_tensor(probs, probs, over_e(tiny(2)), ALU.mult))
                    for k in range(K):
                        ch.link(dve.tensor_reduce(coef[:, k, :], probs, AX, ALU.max))
                        ch.link(dve.tensor_tensor(cand, probs, over_e(coef[:, k, :]), ALU.is_equal))
                        ch.link(dve.tensor_tensor(cand, cand, order, ALU.mult))
                        ch.link(dve.tensor_reduce(tiny(3), cand, AX, ALU.max))
                        ch.link(dve.tensor_tensor(hot[k], order, over_e(tiny(3)), ALU.is_equal))
                        if k + 1 < K:
                            ch.link(dve.scalar_tensor_tensor(probs, hot[k], -2.0, probs, ALU.mult, ALU.add))
                    mask3 = mask[:, 0:NT * E].rearrange("p (t e) -> p t e", t=NT)
                    if K == 2:
                        dve.tensor_tensor(mask3, hot[0], hot[1], ALU.add).then_inc(masked, 1)
                    else:
                        dve.tensor_copy(mask3, hot[0]).then_inc(masked, 1)
                    if r == 0:
                        ch.link(dve.tensor_tensor(tiny(0), coef[:, 0, :], coef[:, 1, :], ALU.add))
                        ch.link(dve.tensor_scalar(tiny(1), tiny(0), 1e-20, None, ALU.add))
                        ch.link(dve.reciprocal(tiny(2), tiny(1)))
                        ch.link(dve.tensor_tensor(coef[:, :, :], coef[:, :, :],
                                                  bc(tiny(2).unsqueeze(1), [TR, 2, NT]), ALU.mult))
                    if r == 1:
                        is0 = hot[0][:, :, 0]
                        ch.link(dve.reciprocal(tiny(0), coef[:, 0, :]))
                        ch.link(dve.tensor_tensor(tiny(0), tiny(0), coef[:, 0, :], ALU.mult))
                        ch.link(dve.tensor_scalar(tiny(1), coef[:, 0, :], -1.0, 1.0, ALU.mult, ALU.add))
                        ch.link(dve.tensor_tensor(tiny(0), tiny(0), is0, ALU.mult))
                        ch.link(dve.tensor_scalar(tiny(2), is0, -1.0, 1.0, ALU.mult, ALU.add))
                        ch.link(dve.tensor_tensor(tiny(1), tiny(1), tiny(2), ALU.mult))
                        ch.link(dve.tensor_tensor(coef[:, 0, :], coef[:, 0, :], tiny(2), ALU.mult))
                        ch.link(dve.tensor_tensor(coef[:, 1, :], tiny(0), tiny(1), ALU.add))
                    dve.wait_ge(ranked, 1)
                    fill = r_small[0:E, 256:256 + THR]
                    ch.link(dve.tensor_scalar(fill, tab["fills"][0:E, :], ps[0:E, 1, 0:1], None, ALU.is_lt))
                    ch.link(dve.tensor_reduce(r_small[0:E, 300:301], fill, AX, ALU.add))
                    dve.tensor_scalar(r_small[0:E, 0:TR], tab["ones"][0:E, 0:TR], r_small[0:E, 300:301], None,
                                      ALU.mult).then_inc(tiles_known, 1)
                    dve.wait_ge(starts_ps, 1)
                    starts = r_small[0:TR, 320:320 + 2 * E]
                    ch.link(dve.tensor_copy(starts, ps[0:TR, 2, 0:2 * E]))
                    ch.link(dve.tensor_tensor(at_slot, ps[0:TR, 0, 0:NT * E].rearrange("p (t e) -> p t e", t=NT),
                                              bc(starts[:, 0:E].unsqueeze(1), [TR, NT, E]), ALU.add))
                    for k in range(K):
                        ch.link(dve.tensor_tensor(cand, hot[k], at_slot, ALU.mult))
                        ch.link(dve.tensor_reduce(tiny(3), cand, AX, ALU.add))
                        ch.link(dve.tensor_copy(slot_of[:, k, 0:NT], tiny(3)))
                        dve.sem_inc(slots_known, 1)
                    T = max_tiles(E, K)
                    T1 = T + 1
                    ends = starts[0:1, E:2 * E]
                    past = r_row[:, 0:T1 * E].rearrange("p (t e) -> p t e", t=T1)
                    ch.link(dve.tensor_tensor(past, bc(ends.unsqueeze(1), [1, T1, E]),
                                              bc(tab["tile_no"][:, 0:T1].unsqueeze(2), [1, T1, E]), ALU.is_le))
                    ch.link(dve.tensor_reduce(r_small[0:1, 0:T1], past, AX, ALU.add))
                    ch.link(dve.tensor_scalar(exp_of[:, 0:T1], r_small[0:1, 0:T1], float(E - 1), None, ALU.min))
                    ch.link(dve.tensor_scalar(r_small[0:1, 80:80 + T // 2], tab["pair_no"][:, 0:T // 2],
                                              ends[:, E - 1:E], None, ALU.is_lt))
                    ch.link(dve.tensor_reduce(r_small[0:1, 128:129], r_small[0:1, 80:80 + T // 2], AX, ALU.add))
                    dve.tensor_copy(n_pairs[:, :], r_small[0:1, 128:129])

        def experts(r):
            E, K = MOE[r]
            T = max_tiles(E, K)
            M1 = 4 if r == 0 else FM
            HM = M1 * 128
            with stage() as ctx:
                sem = lambda n: ctx.semaphore(f"e{r}_{n}")
                two = lambda n: [sem(n + "0"), sem(n + "1")]
                x_in, wa_in, b_in, wb_in, wc_in, y_out = map(two, "x_in wa_in b_in wb_in wc_in y_out".split())
                x_ps, xT_made, h1_ps, h1_made, h2_ps, h2_made, z_ps, z_made, y_ps, y_made, y_left = map(
                    sem, "x_ps xT_made h1_ps h1_made h2_ps h2_made z_ps z_made y_ps y_made y_left".split())
                block = ctx.block()
                h1_bank = lambda u: 2 + u if r == 0 else 2 + 2 * u
                wb_free = z_ps if r == 0 else y_ps

                def steps(eng):
                    return eng.value_load(n_pairs[0:1, 0:1], min_val=1, max_val=T // 2)

                @block.sync
                def _(sp):
                    n = steps(sp)
                    for s in (h1_ps, h1_made, z_ps, y_ps):
                        sp.sem_inc(s, 2)

                    def piece(name, t):
                        e = sp.value_load(exp_of[0:1, ds(t, 1)], min_val=0, max_val=E - 1)
                        return d[name][ds(e, 1)].rearrange("o p n -> (o p) n")

                    def load_x(t, u):
                        sp.dma_start(xin[u][:, :], slots_in[ds(t * SLOT, SLOT), :]).then_inc(x_in[u], 16)
                        sp.dma_start(wA[u][0:DH, 0:2 * HM], piece(f"e{r}_a", t)).then_inc(wa_in[u], 16)
                        if r < 2:
                            hold(sp, h1_made, t + 1)
                            sp.dma_start(b1[u][:, 0:M1], piece(f"e{r}_b1", t)).then_inc(b_in[u], 16)

                    def load_w(t, u):
                        hold(sp, wb_free, t + 1)
                        sp.dma_start(wB[u][:, 0:d[f"e{r}_b"].shape[2]], piece(f"e{r}_b", t)).then_inc(wb_in[u], 16)
                        if r == 0:
                            hold(sp, y_ps, t + 1)
                            sp.dma_start(wC[u][:, :], piece("e0_c", t)).then_inc(wc_in[u], 16)
                        if r == 1:
                            sp.dma_start(wD[u][:, :], piece("e1_d", t)).then_inc(wc_in[u], 16)

                    load_x(0, 0)
                    with sp.Fori(0, n) as i:
                        for u in range(2):
                            t = i * 2 + u
                            hold(sp, h1_ps, t + 2)
                            load_x(t + 1, 1 - u)
                            load_w(t, u)
                    hold(sp, x_in[0], n * 16 + 16)
                    hold(sp, wa_in[0], n * 16 + 16)
                    if r < 2:
                        hold(sp, b_in[0], n * 16 + 16)

                @block.tensor
                def _(pe):
                    n = steps(pe)

                    def turn(t, u, nth):
                        pe.wait_ge(x_in[u], nth * 16)
                        for k in range(2):
                            mm = pe.transpose(ps[0:DH, u, k * SLOT:(k + 1) * SLOT], xin[u][:, k * DH:(k + 1) * DH],
                                              ident[:, :])
                        mm.then_inc(x_ps, 1)

                    def first_layer(t, u, nth):
                        w1 = wA[u][0:DH, 0:2 * HM].rearrange("p (k n) -> p k n", k=2)
                        pe.wait_ge(xT_made, t + 1)
                        pe.wait_ge(wa_in[u], nth * 16)
                        for m in range(M1):
                            for k in range(2):
                                mm = pe.matmul(ps[:, h1_bank(u) + m // 4, (m % 4) * SLOT:(m % 4 + 1) * SLOT],
                                               w1[:, k, m * 128:(m + 1) * 128], xT[u][:, k, :],
                                               start=(k == 0), stop=(k == 1))
                        mm.then_inc(h1_ps, 1)

                    turn(0, 0, 1)
                    first_layer(0, 0, 1)
                    with pe.Fori(0, n) as i:
                        for u in range(2):
                            t = i * 2 + u
                            following = (t + 1, 1 - u, i + 1 + u)
                            if r == 0:
                                turn(*following)
                                w2 = wB[u][:, 0:2048].rearrange("p (k n) -> p k n", k=4)
                                w3 = wB[u][:, 2048:2304].rearrange("p (k n) -> p k n", k=4)
                                pe.wait_ge(h1_made, t + 3)
                                pe.wait_ge(wb_in[u], i * 16 + 16)
                                for m in range(4):
                                    for k in range(4):
                                        mm = pe.matmul(ps[:, 4 + u, m * SLOT:(m + 1) * SLOT],
                                                       w2[:, k, m * 128:(m + 1) * 128], hid[u][:, k, :],
                                                       start=(k == 0), stop=(k == 3))
                                mm.then_inc(h2_ps, 1)
                                first_layer(*following)
                                pe.wait_ge(h2_made, t + 1)
                                pe.wait_ge(y_made, t + 1)
                                for k in range(4):
                                    mm = pe.matmul(ps[0:64, 6 + u, 0:SLOT], w3[:, k, :], hid2[u][:, k, :],
                                                   start=(k == 0), stop=(k == 3))
                                mm.then_inc(z_ps, 1)
                                pe.wait_ge(z_made, t + 1)
                                pe.wait_ge(wc_in[u], i * 16 + 16)
                                pe.matmul(ps[:, 6 + u, 256:256 + D], zT[u][:, :], wC[u][:, 0:D],
                                          start=True, stop=True).then_inc(y_ps, 1)
                            else:
                                turn(*following)
                                first_layer(*following)
                                w2 = wB[u][:, 0:FM * D].rearrange("p (k n) -> p k n", k=FM)
                                pe.wait_ge(h1_made, t + 3)
                                pe.wait_ge(wb_in[u], i * 16 + 16)
                                y = ps[:, 6 + u, 256:256 + D]
                                pe.wait_ge(y_made, t + 1)
                                for k in range(FM):
                                    mm = pe.matmul(y, hid[u][:, k, :], w2[:, k, :], start=(k == 0),
                                                   stop=(r == 2 and k == FM - 1))
                                if r == 1:
                                    pe.wait_ge(wc_in[u], i * 16 + 16)
                                    mm = pe.matmul(y, tab["ones"][0:1, 0:SLOT], wD[u][:, :], start=False, stop=True)
                                mm.then_inc(y_ps, 1)

                @block.scalar
                def _(act):
                    n = steps(act)

                    def x_copied(t, u):
                        act.wait_ge(x_ps, t + 1)
                        act.activation(xT[u][:, :, :], ps[0:DH, u, 0:2 * SLOT].rearrange("p (k n) -> p k n", k=2),
                                       ACT.Copy).then_inc(xT_made, 1)

                    def first_act(t, u, nth):
                        bank = h1_bank(u)
                        act.wait_ge(h1_ps, t + 3)
                        if r < 2:
                            act.wait_ge(b_in[u], nth * 16)
                        if r == 2:
                            for b, m0, m1 in ((0, 0, 4), (1, 4, 6)):
                                ins = act.activation(hid[u][:, m0:m1, :],
                                                     ps[:, bank + b, 0:(m1 - m0) * SLOT].rearrange("p (m n) -> p m n", m=m1 - m0),
                                                     ACT.Relu)
                        else:
                            for m in range(M1):
                                ins = act.activation(hid[u][:, m, :], ps[:, bank + m // 4, (m % 4) * SLOT:(m % 4 + 1) * SLOT],
                                                     ACT.Gelu, bias=b1[u][:, m:m + 1])
                        ins.then_inc(h1_made, 1)

                    x_copied(0, 0)
                    first_act(0, 0, 1)
                    with act.Fori(0, n) as i:
                        for u in range(2):
                            t = i * 2 + u
                            x_copied(t + 1, 1 - u)
                            if r == 0:
                                act.wait_ge(h2_ps, t + 1)
                                for m in range(4):
                                    ins = act.activation(hid2[u][:, m, :], ps[:, 4 + u, m * SLOT:(m + 1) * SLOT],
                                                         ACT.Gelu, bias=wB[u][:, 2304 + m:2305 + m])
                                ins.then_inc(h2_made, 1)
                            first_act(t + 1, 1 - u, i + 1 + u)

                @block.vector
                def _(dve):
                    n = steps(dve)
                    dve.sem_inc(y_made, 2)
                    with dve.Fori(0, n) as i:
                        for u in range(2):
                            t = i * 2 + u
                            if r == 0:
                                dve.wait_ge(wc_in[u], i * 16 + 16)
                                dve.wait_ge(z_ps, t + 3)
                                dve.tensor_scalar(zT[u][0:64, :], ps[0:64, 6 + u, 0:SLOT], wC[u][0:64, D:D + 1], None,
                                                  ALU.add).then_inc(z_made, 1)
                            dve.wait_ge(y_left, t + 1)
                            dve.wait_ge(y_ps, t + 3)
                            dve.tensor_scalar(yo[u][:, :], ps[:, 6 + u, 256:256 + D], 1.0, None,
                                              ALU.mult).then_inc(y_made, 1)

                @block.gpsimd
                def _(pool):
                    n = steps(pool)
                    pool.sem_inc(y_left, 2)
                    with pool.Fori(0, n) as i:
                        for u in range(2):
                            t = i * 2 + u
                            hold(pool, y_made, t + 3)
                            pool.dma_start(slots_out[ds(t * SLOT, SLOT), :], yo[u][:, :]).then_inc(y_out[u], 16)
                            hold(pool, y_out[u], i * 16 + 16)
                            pool.sem_inc(y_left, 1)

        def causal_attention():
            with stage() as ctx:
                S = lane_semaphores(ctx, "b", "gathered found_used first_made stats_made rstd_made normed kept tr_ps hT_made "
                                    "qk_ps q_made k_made v_ps v_made s_ps s_taken max_made centered exped p_ps pT_made "
                                    "y_ps y_made o_ps logits_ps logits_taken hid_ps hid_made mlp_ps")
                dve_step, pool_step = map(ctx.semaphore, "b_dve_step b_pool_step".split())
                block = ctx.block()
                qk = [x[:, :].rearrange("p (g n) -> p g n", g=6) for x in big]
                v = [x[0:TR, 0:CT * D].rearrange("p (t n) -> p t n", t=CT) for x in big2]
                scores = [x[0:TR, :] for x in sc]
                by_head = lambda x: x.rearrange("p (h n) -> p h n", h=HEADS)
                place = lambda h: (h % 4) * 3 + h // 4
                maxes = [x[0:TR, 0:HEADS] for x in small]
                sums = [x[0:TR, 16:16 + HEADS] for x in small]

                @block.tensor
                def _(pe):
                    with pe.Fori(0, NSTEP) as i:
                        for l in LANES:
                            pe.wait_ge(S[l]["normed"], i * 2 + 1)
                            transpose_chunk(pe, A2[l], l, 0).then_inc(S[l]["tr_ps"], 1)
                        for l in LANES:
                            pe.wait_ge(S[l]["hT_made"], i * 3 + 1)
                            for g in range(6):
                                mm = project_wide(pe, l, 2 + g, 128, tab["wqk1"], g * 128)
                                if g % 2:
                                    mm.then_inc(S[l]["qk_ps"], 1)
                            project(pe, hT[l], tab["wv1"], D, lambda j: half(l, j, TR, D)).then_inc(S[l]["v_ps"], 1)
                        for j in range(CT):
                            t = slice(j * TR, (j + 1) * TR)
                            for l in LANES:
                                if j == 0:
                                    pe.wait_ge(S[l]["q_made"], i + 1)
                                    pe.wait_ge(S[l]["k_made"], i + 1)
                                    pe.wait_ge(S[l]["v_made"], i + 1)
                                else:
                                    pe.wait_ge(S[l]["y_made"], i * CT + j)
                                for h in range(HEADS):
                                    g, r = h // 4, h % 4
                                    mm = pe.matmul(ps[0:TR, 4 * l + r, g * TR:(g + 1) * TR], qk[l][32 * r:32 * r + HD, g, t],
                                                   qk[l][32 * r:32 * r + HD, 3 + g, t], start=True, stop=True,
                                                   tile_position=(32 * r, 0))
                                mm.then_inc(S[l]["s_ps"], 1)
                            for l in LANES:
                                pe.wait_ge(S[l]["exped"], i * CT + j + 1)
                                for n in range(HEADS):
                                    mm = pe.transpose(ps[0:TR, 4 * l + n // 4, (n % 4) * TR:(n % 4 + 1) * TR],
                                                      scores[l][:, n * TR:(n + 1) * TR], ident[0:TR, 0:TR])
                                mm.then_inc(S[l]["p_ps"], 1)
                            for l in LANES:
                                pe.wait_ge(S[l]["pT_made"], i * CT + j + 1)
                                for h in range(HEADS):
                                    mm = pe.matmul(half(l, 6, TR, D)[:, h * HD:(h + 1) * HD], pT[l][:, place(h), :],
                                                   v[l][:, j, h * HD:(h + 1) * HD], start=True, stop=True)
                                mm.then_inc(S[l]["y_ps"], 1)
                        for l in LANES:
                            pe.wait_ge(S[l]["y_made"], i * CT + CT)
                            transpose_chunk(pe, A0[l], l, 0).then_inc(S[l]["tr_ps"], 1)
                        for l in LANES:
                            pe.wait_ge(S[l]["hT_made"], i * 3 + 2)
                            project(pe, hT[l], tab["wp1"], D, lambda j: half(l, 2 + j, TR, D)).then_inc(S[l]["o_ps"], 1)
                        for l in LANES:
                            pe.wait_ge(S[l]["normed"], i * 2 + 2)
                            transpose_chunk(pe, A2[l], l, 0).then_inc(S[l]["tr_ps"], 1)
                        for l in LANES:
                            pe.wait_ge(S[l]["hT_made"], i * 3 + 3)
                            project(pe, hT[l], tab["gate1"], 9, lambda j: half(l, 0, TR, 18)[:, j * 9:(j + 1) * 9]).then_inc(
                                S[l]["logits_ps"], 1)
                            hidden_pe(pe, S[l], l, tab["com1"])
                        for l in LANES:
                            pe.wait_ge(S[l]["logits_taken"], i + 1)
                            mlp_out_pe(pe, S[l], l, i, tab["com2"])

                @block.scalar
                def _(act):
                    with act.Fori(0, NSTEP) as i:
                        for l in LANES:
                            turn_act(act, S[l], l, 0, i * 3)
                        for l in LANES:
                            for g in range(4):
                                act.wait_ge(S[l]["qk_ps"], i * 3 + g // 2 + 1)
                                ins = act.activation(qk[l][:, g, :], half(l, 2 + g, 128, CW), ACT.Identity,
                                                     bias=tab["bqk1"][:, g:g + 1])
                            ins.then_inc(S[l]["q_made"], 1)
                        for j in range(CT):
                            for l in LANES:
                                act.wait_ge(S[l]["centered"], i * CT + j + 1)
                                act.activation(scores[l], scores[l], ACT.Exp, scale=HD ** -0.5).then_inc(S[l]["exped"], 1)
                            for l in LANES:
                                act.wait_ge(S[l]["p_ps"], i * CT + j + 1)
                                act.activation(pT[l][:, :, :].rearrange("p (b h) n -> p b (h n)", b=3),
                                               ps[0:TR, 4 * l:4 * l + 3, 0:4 * TR], ACT.Copy).then_inc(S[l]["pT_made"], 1)
                        for l in LANES:
                            turn_act(act, S[l], l, 0, i * 3 + 1)
                        for l in LANES:
                            turn_act(act, S[l], l, 0, i * 3 + 2)
                        for l in LANES:
                            hidden_act(act, S[l], l, i, tab["bcom1"])

                @block.gpsimd
                def _(pool):
                    ch = Chain(pool, pool_step, 4 + 2)
                    for l in LANES:
                        pool.sem_inc(S[l]["kept"], 1)
                        gather(pool, ch, S[l], l, l, 2)
                    ch2 = len(LANES)
                    with pool.Fori(0, NSTEP) as i:
                        ch.start(i, ch2)
                        for l in LANES:
                            combine_pool(pool, S[l], l, i, 2)
                        for l in LANES:
                            norm_pool(pool, ch, S[l], l, i * 2)
                        for l in LANES:
                            hold(pool, S[l]["found_used"], i + 1)
                            gather(pool, ch, S[l], l, i * 2 + 2 + l, 2)
                        for j in range(CT):
                            for l in LANES:
                                hold(pool, S[l]["max_made"], i * CT + j + 1)
                                x = by_head(scores[l])
                                pool.tensor_tensor(x, x, bc(maxes[l].unsqueeze(2), [TR, HEADS, TR]),
                                                   ALU.subtract).then_inc(S[l]["centered"], 1)
                        for l in LANES:
                            norm_pool(pool, ch, S[l], l, i * 2 + 1)
                        for l in LANES:
                            keep(pool, S[l], l, i, i * 2 + 1)
                        ch.end()
                    end_gathers(pool, S, 2)

                @block.vector
                def _(dve):
                    ch = Chain(dve, dve_step, 20)
                    with dve.Fori(0, NSTEP) as i:
                        ch.start(i)
                        for l in LANES:
                            combine_dve(dve, ch, S[l], l, i, found[l][:, 1, :, :])
                            norm_dve(dve, ch, S[l], l, i * 2)
                        for l in LANES:
                            dve.wait_ge(S[l]["kept"], i + 1)
                            norm_dve_end(dve, S[l], l, i * 2)
                        for l in LANES:
                            dve.wait_ge(S[l]["qk_ps"], i * 3 + 3)
                            for g in (4, 5):
                                ins = dve.tensor_scalar(qk[l][:, g, :], half(l, 2 + g, 128, CW), tab["bqk1"][:, g:g + 1], None,
                                                        ALU.add)
                            ins.then_inc(S[l]["k_made"], 1)
                            dve.wait_ge(S[l]["v_ps"], i + 1)
                            dve.tensor_tensor(v[l], span(l, 0, 2, TR, D), bc(tab["bv1"][:, :].unsqueeze(1), [TR, CT, D]),
                                              ALU.add).then_inc(S[l]["v_made"], 1)
                        for j in range(CT):
                            for l in LANES:
                                dve.wait_ge(S[l]["s_ps"], i * CT + j + 1)
                                dve.tensor_tensor(
                                    scores[l].rearrange("p (r g n) -> p r g n", r=4, g=3),
                                    ps[0:TR, 4 * l:4 * l + 4, 0:3 * TR].rearrange("p r (g n) -> p r g n", g=3),
                                    bc(tab["causal_neg"][:, :].unsqueeze(1).unsqueeze(1), [TR, 4, 3, TR]),
                                    ALU.add).then_inc(S[l]["s_taken"], 1)
                                dve.wait_ge(S[l]["s_taken"], i * CT + j + 1)
                                dve.tensor_reduce(maxes[l], by_head(scores[l]), AX, ALU.max).then_inc(S[l]["max_made"], 1)
                            for l in LANES:
                                dve.wait_ge(S[l]["exped"], i * CT + j + 1)
                                ch.link(dve.tensor_reduce(sums[l], by_head(scores[l]), AX, ALU.add))
                                ch.link(dve.reciprocal(sums[l], sums[l]))
                            for l in LANES:
                                dve.wait_ge(S[l]["y_ps"], i * CT + j + 1)
                                dve.tensor_tensor(A0[l][:, j, :].rearrange("p (g r n) -> p g r n", g=3, r=4),
                                                  half(l, 6, TR, D).rearrange("p (g r n) -> p g r n", g=3, r=4),
                                                  bc(sums[l].rearrange("p (r g) -> p g r", r=4).unsqueeze(3), [TR, 3, 4, HD]),
                                                  ALU.mult).then_inc(S[l]["y_made"], 1)
                        for l in LANES:
                            dve.wait_ge(S[l]["o_ps"], i + 1)
                            ch.link(dve.tensor_tensor(A1[l][:, :, :], span(l, 2, 2, TR, D), A2[l][:, :, :], ALU.add))
                            ch.link(dve.tensor_tensor(A1[l][:, :, :], A1[l][:, :, :],
                                                      bc(tab["bp1"][:, :].unsqueeze(1), [TR, CT, D]), ALU.add))
                            norm_dve(dve, ch, S[l], l, i * 2 + 1)
                        for l in LANES:
                            norm_dve_end(dve, S[l], l, i * 2 + 1)
                        for l in LANES:
                            dve.wait_ge(S[l]["logits_ps"], i + 1)
                            dve.tensor_tensor(logits[:, ds((i * 2 + l) * CT, CT), 0:9],
                                              half(l, 0, TR, 18).rearrange("p (t n) -> p t n", t=CT),
                                              bc(tab["bgate1"][:, :].unsqueeze(1), [TR, CT, 9]),
                                              ALU.add).then_inc(S[l]["logits_taken"], 1)
                        for l in LANES:
                            dve.wait_ge(S[l]["mlp_ps"], i + 1)
                            dve.tensor_tensor(common[:, ds((i * 2 + l) * CT, CT), :], span(l, 0, 2, TR, D),
                                              bc(tab["bcom2"][:, :].unsqueeze(1), [TR, CT, D]), ALU.add)
                        ch.end()

        def ffn_and_retention():
            with stage() as ctx:
                S = lane_semaphores(ctx, "c", "gathered found_used first_made stats_made rstd_made normed kept tr_ps hT_made "
                                    "hid_ps hid_made mlp_ps v_ps v_made g_ps g_made qk_ps qk_taken rotated s_ps p_made "
                                    "pv_ps sums_made mean_ps centered squared sq_made var_ps var_made gstd_made gated o_ps "
                                    "logits_ps")
                dve_step, pool_step = map(ctx.semaphore, "c_dve_step c_pool_step".split())
                block = ctx.block()
                v = [x[0:TR, 0:CT * RH * RV].rearrange("p (t n) -> p t n", t=CT) for x in big]
                gate = [x[:, :].rearrange("p (g n) -> p g n", g=3) for x in big2]
                og = [x[:, 0:3 * CW].rearrange("p (g n) -> p g n", g=3) for x in big]
                sq = [x[:, 3 * CW:6 * CW] for x in big]
                rot = lambda l, n: sc[l][:, n * 2 * CW:(n + 1) * 2 * CW].rearrange("p (a n) -> p a n", a=2)
                imgs = lambda x: x.rearrange("p a (b n) -> p a b n", n=L)
                probs = lambda l, h: (A0, A1)[h % 2][l][:, :, :].rearrange("p t n -> p (t n)")[:, 0:CW].rearrange(
                    "p (t n) -> p t n", t=CT)
                NG = 3 * CB
                gstat = lambda l, n: small[l][:, n * NG:(n + 1) * NG]
                by_image = lambda x: bc(x.rearrange("p (g b) -> p g b", g=3).unsqueeze(3), [128, 3, CB, L])
                og4 = [x.rearrange("p g (b n) -> p g b n", n=L) for x in og]
                o_ps = [span(l, 2, 3, 128, CW).rearrange("p g (b n) -> p g b n", n=L) for l in LANES]
                qb = lambda h: 6 * (h % 2)

                @block.tensor
                def _(pe):
                    def qk_of(i, l, h):
                        if h >= 2:
                            pe.wait_ge(S[l]["qk_taken"], i * RH + h - 1)
                        project_wide(pe, l, qb(h), 128, tab["wq3"], h * RQK)
                        project_wide(pe, l, qb(h) + 1, 128, tab["wk3"], h * RQK).then_inc(S[l]["qk_ps"], 1)

                    with pe.Fori(0, NSTEP) as i:
                        for l in LANES:
                            pe.wait_ge(S[l]["normed"], i * 4 + 2)
                            transpose_chunk(pe, A2[l], l, 0).then_inc(S[l]["tr_ps"], 1)
                        for l in LANES:
                            pe.wait_ge(S[l]["hT_made"], i * 3 + 1)
                            hidden_pe(pe, S[l], l, tab["ffn1"])
                        for l in LANES:
                            mlp_out_pe(pe, S[l], l, i, tab["ffn2"])
                        for l in LANES:
                            pe.wait_ge(S[l]["normed"], i * 4 + 3)
                            transpose_chunk(pe, A2[l], l, 0).then_inc(S[l]["tr_ps"], 1)
                        for l in LANES:
                            pe.wait_ge(S[l]["hT_made"], i * 3 + 2)
                            for g in range(3):
                                mm = project_wide(pe, l, (6, 7, 0)[g], 128, tab["wg3"], g * 128)
                            mm.then_inc(S[l]["g_ps"], 1)
                            project(pe, hT[l], tab["wv3"], RH * RV, lambda j: ps[0:TR, 4 * l + 1 + j, 0:RH * RV]).then_inc(
                                S[l]["v_ps"], 1)
                        for l in LANES:
                            pe.wait_ge(S[l]["g_made"], i + 1)
                            qk_of(i, l, 0)
                        for l in LANES:
                            qk_of(i, l, 1)
                        for h in range(RH):
                            for l in LANES:
                                if h == 0:
                                    pe.wait_ge(S[l]["v_made"], i + 1)
                                pe.wait_ge(S[l]["rotated"], i * RH + h + 1)
                                r = rot(l, h % 2)
                                for j in range(CT):
                                    t = slice(j * TR, (j + 1) * TR)
                                    mm = pe.matmul(half(l, 5, TR, CW)[:, t], r[:, 1, t], r[:, 0, t], start=True, stop=True)
                                mm.then_inc(S[l]["s_ps"], 1)
                            if h + 2 < RH:
                                for l in LANES:
                                    qk_of(i, l, h + 2)
                            for l in LANES:
                                pe.wait_ge(S[l]["p_made"], i * RH + h + 1)
                                o = (8 * l + 2 + h // 2) * HALF
                                for j in range(CT):
                                    mm = pe.matmul(ps_flat[(h % 2) * 64:(h % 2) * 64 + 64, o + j * TR:o + (j + 1) * TR],
                                                   v[l][:, j, h * RV:(h + 1) * RV], probs(l, h)[:, j, :], start=True, stop=True)
                                if h == RH - 1:
                                    mm.then_inc(S[l]["pv_ps"], 1)
                        for l in LANES:
                            pe.wait_ge(S[l]["sums_made"], i + 1)
                            pe.matmul(half(l, 0, 128, NG), tab["head_mean"][:, :], gstat(l, 0), start=True, stop=True).then_inc(
                                S[l]["mean_ps"], 1)
                        for l in LANES:
                            pe.wait_ge(S[l]["sq_made"], i + 1)
                            pe.matmul(half(l, 0, 128, NG), tab["head_mean"][:, :], gstat(l, 1), start=True, stop=True).then_inc(
                                S[l]["var_ps"], 1)
                        for l in LANES:
                            pe.wait_ge(S[l]["gated"], i + 1)
                            project(pe, og[l], tab["wo3"], D, lambda j: half(l, 6 + j, TR, D), 3).then_inc(S[l]["o_ps"], 1)
                        for l in LANES:
                            pe.wait_ge(S[l]["normed"], i * 4 + 4)
                            transpose_chunk(pe, A2[l], l, 0).then_inc(S[l]["tr_ps"], 1)
                        for l in LANES:
                            pe.wait_ge(S[l]["hT_made"], i * 3 + 3)
                            project(pe, hT[l], tab["gate3"], 8, lambda j: half(l, 2, TR, 16)[:, j * 8:(j + 1) * 8]).then_inc(
                                S[l]["logits_ps"], 1)

                @block.scalar
                def _(act):
                    with act.Fori(0, NSTEP) as i:
                        for l in LANES:
                            turn_act(act, S[l], l, 0, i * 3)
                        for l in LANES:
                            hidden_act(act, S[l], l, i, tab["bffn1"])
                        for l in LANES:
                            turn_act(act, S[l], l, 0, i * 3 + 1)
                        for l in LANES:
                            act.wait_ge(S[l]["g_ps"], i + 1)
                            for g in range(3):
                                ins = act.activation(gate[l][:, g, :], half(l, (6, 7, 0)[g], 128, CW), ACT.Silu)
                            ins.then_inc(S[l]["g_made"], 1)
                            act.wait_ge(S[l]["v_ps"], i + 1)
                            act.activation(v[l], ps[0:TR, 4 * l + 1:4 * l + 3, 0:RH * RV], ACT.Copy).then_inc(S[l]["v_made"], 1)
                        for l in LANES:
                            act.wait_ge(S[l]["centered"], i + 1)
                            act.activation(sq[l], og[l].rearrange("p g n -> p (g n)"), ACT.Square).then_inc(S[l]["squared"], 1)
                        for l in LANES:
                            turn_act(act, S[l], l, 0, i * 3 + 2)

                @block.gpsimd
                def _(pool):
                    ch = Chain(pool, pool_step, 8 + 2)
                    for l in LANES:
                        pool.sem_inc(S[l]["kept"], 1)
                        gather(pool, ch, S[l], l, l, 1)
                    with pool.Fori(0, NSTEP) as i:
                        ch.start(i, len(LANES))
                        for l in LANES:
                            combine_pool(pool, S[l], l, i, 1)
                        for n in range(3):
                            for l in LANES:
                                norm_pool(pool, ch, S[l], l, i * 4 + n)
                            if n == 0:
                                for l in LANES:
                                    hold(pool, S[l]["found_used"], i + 1)
                                    gather(pool, ch, S[l], l, i * 2 + 2 + l, 1)
                        for h in range(RH):
                            for l in LANES:
                                pool.wait_ge(S[l]["qk_taken"], i * RH + h + 1)
                                pool.tensor_tensor(rot(l, h % 2), rot(l, h % 2), rot(l, 2), ALU.add).then_inc(
                                    S[l]["rotated"], 1)
                        for l in LANES:
                            pool.wait_ge(S[l]["var_made"], i + 1)
                            pool.tensor_tensor(gstat(l, 1), gstat(l, 1), negh[:, 0:NG], ALU.pow).then_inc(S[l]["gstd_made"], 1)
                        for l in LANES:
                            norm_pool(pool, ch, S[l], l, i * 4 + 3)
                        for l in LANES:
                            keep(pool, S[l], l, i, i * 4 + 3)
                        ch.end()
                    end_gathers(pool, S, 1)

                @block.vector
                def _(dve):
                    def rotate(i, l, h):
                        dve.wait_ge(S[l]["qk_ps"], i * RH + h + 1)
                        if h > 0:
                            dve.wait_ge(S[l]["rotated"], i * RH + h)
                        x, r, t = span(l, qb(h), 2, 128, CW), rot(l, h % 2), rot(l, 2)
                        dve.tensor_tensor(imgs(r), imgs(x), bc(tab["cos_qk"][:, :, :].unsqueeze(2), [128, 2, CB, L]), ALU.mult)
                        for p, o in ((0, 64), (64, 0)):
                            ins = dve.tensor_tensor(imgs(t[o:o + 64]), imgs(x[p:p + 64]),
                                                    bc(tab["sin_qk"][p:p + 64, :, :].unsqueeze(2), [64, 2, CB, L]), ALU.mult)
                        ins.then_inc(S[l]["qk_taken"], 1)

                    def weigh(i, l, h):
                        dve.wait_ge(S[l]["s_ps"], i * RH + h + 1)
                        dve.tensor_tensor(probs(l, h), half(l, 5, TR, CW).rearrange("p (t n) -> p t n", t=CT),
                                          bc(tab["decayT"][:, h, :].unsqueeze(1), [TR, CT, TR]),
                                          ALU.mult).then_inc(S[l]["p_made"], 1)

                    ch = Chain(dve, dve_step, 24)
                    with dve.Fori(0, NSTEP) as i:
                        ch.start(i)
                        for l in LANES:
                            combine_dve(dve, ch, S[l], l, i, common[:, ds((i * 2 + l) * CT, CT), :])
                            norm_dve(dve, ch, S[l], l, i * 4)
                        for l in LANES:
                            dve.wait_ge(S[l]["kept"], i + 1)
                            norm_dve_end(dve, S[l], l, i * 4)
                        for l in LANES:
                            dve.wait_ge(S[l]["normed"], i * 4 + 1)
                            ch.link(dve.tensor_tensor(A1[l][:, :, :], A2[l][:, :, :],
                                                      bc(pbias[:, :].unsqueeze(1), [TR, CT, D]), ALU.add))
                            norm_dve(dve, ch, S[l], l, i * 4 + 1)
                        for l in LANES:
                            norm_dve_end(dve, S[l], l, i * 4 + 1)
                        for l in LANES:
                            dve.wait_ge(S[l]["mlp_ps"], i + 1)
                            ch.link(dve.tensor_tensor(A1[l][:, :, :], span(l, 0, 2, TR, D), A2[l][:, :, :], ALU.add))
                            norm_dve(dve, ch, S[l], l, i * 4 + 2)
                        for l in LANES:
                            norm_dve_end(dve, S[l], l, i * 4 + 2)
                        for h in range(RH + 1):
                            if h < RH:
                                for l in LANES:
                                    rotate(i, l, h)
                            if h > 0:
                                for l in LANES:
                                    weigh(i, l, h - 1)
                        for l in LANES:
                            dve.wait_ge(S[l]["pv_ps"], i + 1)
                            dve.tensor_reduce(gstat(l, 0), o_ps[l], AX, ALU.add).then_inc(S[l]["sums_made"], 1)
                        for l in LANES:
                            dve.wait_ge(S[l]["mean_ps"], i + 1)
                            ch.link(dve.tensor_copy(gstat(l, 0), half(l, 0, 128, NG)))
                            dve.tensor_tensor(og4[l], o_ps[l], by_image(gstat(l, 0)), ALU.subtract).then_inc(S[l]["centered"], 1)
                        for l in LANES:
                            dve.wait_ge(S[l]["squared"], i + 1)
                            dve.tensor_reduce(gstat(l, 1), sq[l].rearrange("p (g n) -> p g n", n=L), AX, ALU.add).then_inc(
                                S[l]["sq_made"], 1)
                        for l in LANES:
                            dve.wait_ge(S[l]["var_ps"], i + 1)
                            dve.tensor_scalar(gstat(l, 1), half(l, 0, 128, NG), EPS, None, ALU.add).then_inc(
                                S[l]["var_made"], 1)
                        for l in LANES:
                            dve.wait_ge(S[l]["gstd_made"], i + 1)
                            ch.link(dve.tensor_tensor(og4[l], og4[l], by_image(gstat(l, 1)), ALU.mult))
                            for g in range(3):
                                ins = dve.tensor_scalar(og[l][:, g, :], og[l][:, g, :], tab["gnw"][:, g:g + 1],
                                                        tab["gnb"][:, g:g + 1], ALU.mult, ALU.add)
                            ch.link(ins)
                            dve.tensor_tensor(og[l], og[l], gate[l], ALU.mult).then_inc(S[l]["gated"], 1)
                        for l in LANES:
                            dve.wait_ge(S[l]["o_ps"], i + 1)
                            ch.link(dve.tensor_tensor(A1[l][:, :, :], span(l, 6, 2, TR, D), A2[l][:, :, :], ALU.add))
                            norm_dve(dve, ch, S[l], l, i * 4 + 3)
                        for l in LANES:
                            norm_dve_end(dve, S[l], l, i * 4 + 3)
                        for l in LANES:
                            dve.wait_ge(S[l]["logits_ps"], i + 1)
                            dve.tensor_scalar(logits[:, ds((i * 2 + l) * CT, CT), 0:8],
                                              half(l, 2, TR, 16).rearrange("p (t n) -> p t n", t=CT), 1.0, None, ALU.mult)
                        ch.end()

        def last_norm():
            with stage() as ctx:
                S = lane_semaphores(ctx, "d", "gathered found_used first_made stats_made rstd_made normed stored")
                dve_step, pool_step = map(ctx.semaphore, "d_dve_step d_pool_step".split())
                block = ctx.block()
                rows = out.rearrange("(t p) n -> p t n", p=TR)

                @block.sync
                def _(sp):
                    for l in LANES:
                        sp.sem_inc(S[l]["stored"], 16)
                    with sp.Fori(0, NSTEP) as i:
                        for l in LANES:
                            hold(sp, S[l]["normed"], i + 1)
                            sp.dma_start(rows[:, ds((i * 2 + l) * CT, CT), :], A2[l][:, :, :]).then_inc(S[l]["stored"], 16)
                    for l in LANES:
                        sp.wait_ge(S[l]["stored"], NSTEP * 16 + 16)

                @block.gpsimd
                def _(pool):
                    ch = Chain(pool, pool_step, 4)
                    for l in LANES:
                        gather(pool, ch, S[l], l, l, 1)
                    with pool.Fori(0, NSTEP) as i:
                        ch.start(i, len(LANES))
                        for l in LANES:
                            combine_pool(pool, S[l], l, i, 1)
                        for l in LANES:
                            hold(pool, S[l]["first_made"], i + 1)
                            gather(pool, ch, S[l], l, i * 2 + 2 + l, 1)
                        for l in LANES:
                            norm_pool(pool, ch, S[l], l, i)
                        ch.end()
                    end_gathers(pool, S, 1)

                @block.vector
                def _(dve):
                    ch = Chain(dve, dve_step, 4)
                    with dve.Fori(0, NSTEP) as i:
                        ch.start(i)
                        for l in LANES:
                            combine_dve(dve, ch, S[l], l, i, None)
                            norm_dve(dve, ch, S[l], l, i)
                        for l in LANES:
                            dve.wait_ge(S[l]["stored"], i * 16 + 16)
                            norm_dve_end(dve, S[l], l, i)
                        for l in LANES:
                            dve.wait_ge(S[l]["normed"], i + 1)
                        ch.end()

        setup()
        embed_and_rope_attention()
        route(0)
        experts(0)
        causal_attention()
        route(1)
        experts(1)
        ffn_and_retention()
        route(2)
        experts(2)
        last_norm()


def halves_k(w):
    return w.reshape(2, DH, -1).transpose(1, 0, 2)


def rows_k(w):
    return w.reshape(-1, 128, w.shape[-1]).transpose(1, 0, 2)


def lay_out(i):
    d = dict(constants())
    rep = lambda v: np.tile(np.asarray(v)[None], (TR, 1))
    x = i["x"].reshape(B, 3, 7, 16, 7, 16).transpose(1, 3, 5, 0, 2, 4).reshape(PK, 128, NCH, CW)
    d["patches"] = x.transpose(2, 1, 0, 3).reshape(NCH, 128, PK * CW)
    d["conv_w"] = rows_k(i["L0_tok_conv_w"].reshape(D, -1).T)
    d["conv_b"] = rep(i["L0_tok_conv_b"])
    bounds = np.arange(1.0 / 32, 1.0, 1.0 / 32, dtype=np.float32)
    at = np.searchsorted(bounds, np.arange(0.0, 1.0 - 1e-06, 1.0 / 7, dtype=np.float32), side="right")
    ids = (at[:, None] * 32 + at).reshape(-1)
    pos = i["L0_tok_pos_table"][ids]
    d["pos"] = np.concatenate([pos, pos], 0)
    d["wv0"] = halves_k(i["L0_attn_Wv"].T)
    d["wo0"] = i["L0_attn_Wo"].T
    d["gate0"] = halves_k(i["L0_ffn_gate_w"].T)
    w, b = i["L1_attn_W_attn"], i["L1_attn_b_attn"]
    wqk = np.zeros((D, 6, 4, 32), np.float32)
    bqk = np.zeros((6, 4, 32), np.float32)
    wqk[..., :HD] = w[:, :2 * D].reshape(D, 6, 4, HD)
    bqk[..., :HD] = b[:2 * D].reshape(6, 4, HD)
    d["wqk1"] = halves_k(wqk.reshape(D, -1))
    d["bqk1"] = bqk.reshape(6, 128).T
    d["wv1"], d["bv1"] = halves_k(w[:, 2 * D:]), rep(b[2 * D:])
    d["wp1"], d["bp1"] = halves_k(i["L1_attn_W_proj"]), rep(i["L1_attn_b_proj"])
    d["gate1"], d["bgate1"] = halves_k(i["L1_ffn_Ws"]), rep(i["L1_ffn_bs"])
    d["com1"], d["bcom1"] = halves_k(i["L1_ffn_W1"][0]), i["L1_ffn_b1"][0].reshape(FM, 128).T
    d["com2"], d["bcom2"] = rows_k(i["L1_ffn_W2"][0]), rep(i["L1_ffn_b2"][0])
    d["proj_w"], d["proj_b"] = halves_k(i["L2_attn_proj_w"].T), rep(i["L2_attn_proj_b"])
    d["ffn1"], d["bffn1"] = halves_k(i["L2_ffn_in_weight"].T), i["L2_ffn_in_bias"].reshape(FM, 128).T
    d["ffn2"] = rows_k(i["L2_ffn_out_weight"])
    for n, k in (("wq3", "Wq"), ("wk3", "Wk"), ("wv3", "Wv"), ("wg3", "Wg")):
        d[n] = halves_k(i["L3_attn_" + k])
    d["wo3"] = rows_k(i["L3_attn_Wo"])
    d["gnw"], d["gnb"] = (i["L3_attn_gn_" + n].reshape(3, 128).T for n in ("weight", "bias"))
    d["gate3"] = halves_k(i["L3_ffn_router_w"])
    ek = lambda w: w.reshape(w.shape[0], 2, DH, -1).transpose(0, 2, 1, 3).reshape(w.shape[0], DH, -1)
    er = lambda w: w.reshape(w.shape[0], -1, 128, w.shape[-1]).transpose(0, 2, 1, 3).reshape(w.shape[0], 128, -1)
    col = lambda b: b.reshape(b.shape[0], -1, 128).transpose(0, 2, 1)
    d["e0_a"] = ek(i["L0_ffn_W1"])
    d["e0_b1"] = col(i["L0_ffn_b1"])
    d["e0_b"] = np.concatenate([er(i["L0_ffn_W2"]), er(i["L0_ffn_W3"]), col(i["L0_ffn_b2"])], -1)
    wl = np.concatenate([i["L0_ffn_Wl"], i["L0_ffn_bl"][:, None]], 1)
    b3 = np.concatenate([i["L0_ffn_b3"], np.zeros((MOE[0][0], 1), np.float32)], 1)
    d["e0_c"] = np.concatenate([wl, b3[:, :, None]], -1)
    d["e1_a"] = ek(i["L1_ffn_W1"])
    d["e1_b1"] = col(i["L1_ffn_b1"])
    d["e1_b"] = er(i["L1_ffn_W2"])
    d["e1_d"] = i["L1_ffn_b2"][:, None]
    d["e2_a"] = ek(i["L3_ffn_wi"])
    d["e2_b"] = er(i["L3_ffn_wo"])
    return {k: np.ascontiguousarray(v) for k, v in d.items()}


def kernel(**inputs):
    import concourse.bacc as bacc
    from concourse.bass_utils import run_bass_kernel_spmd

    arrays = lay_out({k: np.asarray(v) for k, v in inputs.items()})
    nc = bacc.Bacc("TRN2", target_bir_lowering=False, num_devices=1)
    d = {k: nc.dram_tensor(k, v.shape, mybir.dt.from_np(v.dtype), kind="ExternalInput").ap()
         for k, v in arrays.items()}
    out = nc.dram_tensor("out", [NTOK, D], F32, kind="ExternalOutput").ap()
    build(nc, d, out)
    r = run_bass_kernel_spmd(nc, [arrays], core_ids=[0])
    return r.results[0]["out"].reshape(B, L, D)
```

```python
from contextlib import ExitStack

import numpy as np

import concourse.bass as bass
from concourse import mybir

F32 = mybir.dt.float32
I32 = mybir.dt.int32
BF16 = mybir.dt.bfloat16
ALU = mybir.AluOpType
ACT = mybir.ActivationFunctionType
AX = mybir.AxisListType.X
ds = bass.ds

B, L = 32, 49
D, DH = 192, 96
TR = 2 * L
NT = B // 2
CT = 2
NCH = NT // CT
CW = CT * TR
CB = CW // L
LANES = range(2)
NSTEP = NCH // 2
NTOK = B * L
PK = 3 * 16 * 16 // 128
SLOT = 128
HEADS, HD = 12, 16
RH, RQK, RV = 6, 128, 64
FF = 768
FM = FF // 128
EPS = 1e-5
NEG = -1.0e30
PSB = 512
HALF = PSB // 2


def max_tiles(experts, k):
    n = (NTOK * k - experts) // SLOT + experts
    return n + n % 2


MOE = {0: (32, 2), 1: (9, 1), 2: (8, 1)}
TMAX = max(max_tiles(*v) for v in MOE.values())
THR = (NTOK + SLOT - 1) // SLOT


def constants():
    c = {}
    c["ident"] = np.eye(128, dtype=np.float32)
    blk = np.kron(np.eye(2), np.ones((L, L)))
    c["block_neg"] = np.where(blk > 0, 0.0, NEG).astype(np.float32)
    causal = np.kron(np.eye(2), np.tril(np.ones((L, L))))
    c["causal_neg"] = np.where(causal > 0, 0.0, NEG).astype(np.float32)
    pos = np.arange(L, dtype=np.float32)
    fr = (10000.0 ** (-np.arange(0, D, 2, dtype=np.float32) / D)).astype(np.float32)
    ang = (pos[:, None] * fr[None]).astype(np.float32).astype(np.float64)
    r = np.concatenate([np.sin(ang), np.cos(ang)], -1).astype(np.float32)
    c["ropeT"] = np.concatenate([r, r], 0).T.reshape(2, DH, TR).transpose(1, 0, 2).copy()
    i = np.arange(TR)
    c["before"] = (i[:, None] < i[None]).astype(np.float32)
    c["ones"] = np.ones((128, 128), np.float32)
    c["rank_order"] = np.tile(64.0 - np.arange(32, dtype=np.float32), (TR, 1))
    e = np.arange(32)
    c["exp_order"] = np.stack([SLOT * (e[:, None] < e[None]), 1 * (e[:, None] <= e[None])], 1).astype(np.float32)
    c["fills"] = np.tile(SLOT * np.arange(THR, dtype=np.float32), (32, 1))
    c["tile_no"] = np.arange(TMAX + 1, dtype=np.float32)[None]
    c["pair_no"] = (2 * np.arange(TMAX // 2, dtype=np.float32))[None]
    half = RQK // 2
    p64 = np.arange(L, dtype=np.float64)
    inv = 1.0 / 10000.0 ** (np.arange(half) / half)
    a = p64[:, None] * inv[None]
    zeta = (np.arange(half) + half) / RQK
    cos, sin = [], []
    for s in (1.0, -1.0):
        dec = zeta[None] ** (s * p64[:, None] / 512.0)
        co, si = (np.cos(a) * dec).T, (np.sin(a) * dec).T
        cos.append(np.concatenate([co, co], 0))
        sin.append(np.concatenate([si, -si], 0))
    c["cos_qk"], c["sin_qk"] = np.stack(cos, 1).astype(np.float32), np.stack(sin, 1).astype(np.float32)
    g = 1.0 - 2.0 ** (-(5.0 + np.arange(RH)))
    diff = p64[:, None] - p64[None]
    dm = g[:, None, None] ** np.clip(diff, 0, None)[None] * (diff >= 0)[None]
    dm = dm / np.sqrt(np.clip(dm.sum(-1, keepdims=True), 1e-6, None)) * RQK ** -0.5
    c["decayT"] = np.stack([np.kron(np.eye(2), m.T) for m in dm], 1).astype(np.float32)
    hb = np.kron(np.eye(2), np.ones((RV, RV))) / (RV * L)
    c["head_mean"] = hb.astype(np.float32)
    return c


def hold(eng, sem, value):
    eng.wait_ge(sem, value)
    eng.nop(nofuse=True)


class Chain:

    def __init__(self, eng, sem, per_pass=0):
        self.eng, self.sem, self.n, self.base, self.per_pass = eng, sem, 0, 0, per_pass

    def start(self, i, before=0):
        self.n, self.base = 0, i * self.per_pass + before

    def link(self, ins, alone=False):
        self.n += 1
        ins.then_inc(self.sem, 1)
        if alone:
            hold(self.eng, self.sem, self.base + self.n)
        else:
            self.eng.wait_ge(self.sem, self.base + self.n)

    def end(self):
        assert self.n == self.per_pass, f"links per pass: {self.n}, not {self.per_pass}"


def build(nc, d, out):
    top = ExitStack()
    with top:
        def sb(name, shape, dt=F32):
            return top.enter_context(nc.sbuf_tensor(name, shape, dt))

        def dram(name, shape):
            return nc.dram_tensor(name, shape, F32).ap()

        ps = top.enter_context(nc.psum_tensor("ps", [128, 8, PSB], F32))
        slots_in = dram("slots_in", [(TMAX + 8) * SLOT, D])
        slots_out = dram("slots_out", [(TMAX + 8) * SLOT, D])

        tab = {}
        loads = []

        def resident(name, shape):
            tab[name] = sb("t_" + name, shape)
            loads.append((tab[name], d[name]))

        for n in ("ropeT block_neg proj_w".split()):
            resident(n, {"ropeT": [DH, 2, TR], "block_neg": [TR, TR], "proj_w": [DH, 2, D]}[n])
        resident("ident", [128, 128])
        resident("before", [TR, TR])
        resident("ones", [128, 128])
        resident("proj_b", [TR, D])
        resident("pos", [TR, D])
        resident("conv_b", [TR, D])
        resident("conv_w", [128, PK, D])
        resident("wv0", [DH, 2, 64])
        resident("wo0", [64, D])
        resident("gate0", [DH, 2, 32])
        early = len(loads)
        resident("causal_neg", [TR, TR])
        resident("rank_order", [TR, 32])
        resident("exp_order", [32, 2, 32])
        resident("fills", [32, THR])
        resident("tile_no", [1, TMAX + 1])
        resident("pair_no", [1, TMAX // 2])
        for n in ("cos_qk", "sin_qk"):
            resident(n, [128, 2, L])
        resident("decayT", [TR, RH, TR])
        resident("head_mean", [128, 128])
        resident("wqk1", [DH, 2, 6 * 128])
        resident("bqk1", [128, 6])
        resident("wv1", [DH, 2, D])
        resident("bv1", [TR, D])
        resident("wp1", [128, 3, D])
        resident("bp1", [TR, D])
        resident("gate1", [DH, 2, 9])
        resident("bgate1", [TR, 9])
        resident("com1", [DH, 2, FF])
        resident("bcom1", [128, FM])
        resident("com2", [128, FM, D])
        resident("bcom2", [TR, D])
        resident("ffn1", [DH, 2, FF])
        resident("bffn1", [128, FM])
        resident("ffn2", [128, FM, D])
        resident("wq3", [DH, 2, RH * RQK])
        resident("wk3", [DH, 2, RH * RQK])
        resident("wv3", [DH, 2, RH * RV])
        resident("wg3", [DH, 2, RH * RV])
        resident("wo3", [128, 3, D])
        resident("gnw", [128, 3])
        resident("gnb", [128, 3])
        resident("gate3", [DH, 2, 8])
        ident = tab["ident"]

        NA = NT + 2 * CT
        H = sb("H", [TR, NA, D])
        common = sb("common", [TR, NA, D])
        logits = sb("logits", [TR, NT, 32])
        coef = sb("coef", [TR, 2, NA])
        slot_of = sb("slot_of", [TR, 2, NA], I32)
        exp_of = sb("exp_of", [1, TMAX + 1], I32)
        n_pairs = sb("n_pairs", [1, 1], I32)
        ropeP = sb("ropeP", [TR, TR])
        negh = sb("negh", [128, 32])
        pbias = sb("pbias", [TR, D])

        before16 = sb("before16", [TR, TR], BF16)
        ones16 = sb("ones16", [TR, TR], BF16)
        mask = sb("mask", [TR, NT * 32], BF16)

        xin = [sb(f"xin{u}", [SLOT, D]) for u in range(2)]
        xT = [sb(f"xT{u}", [DH, 2, SLOT]) for u in range(2)]
        wA = [sb(f"wA{u}", [128, 2 * FF]) for u in range(2)]
        b1 = [sb(f"b1{u}", [128, FM]) for u in range(2)]
        wB = [sb(f"wB{u}", [128, 2308]) for u in range(2)]
        wC = [sb(f"wC{u}", [65, D + 1]) for u in range(2)]
        wD = [sb(f"wD{u}", [1, D]) for u in range(2)]
        hid = [sb(f"hid{u}", [128, FM, SLOT]) for u in range(2)]
        hid2 = [sb(f"hid2{u}", [128, 4, SLOT]) for u in range(2)]
        zT = [sb(f"zT{u}", [65, SLOT]) for u in range(2)]
        yo = [sb(f"yo{u}", [SLOT, D]) for u in range(2)]

        per_lane = lambda name, shape, dt=F32: [sb(f"{name}{l}", shape, dt) for l in LANES]
        A0, A1, A2 = (per_lane(n, [TR, CT, D]) for n in ("A0", "A1", "A2"))
        found = per_lane("found", [TR, 2, CT, D])
        find = per_lane("find", [TR, 2, CT], I32)
        hT = per_lane("hT", [DH, 2, CW])
        stats = per_lane("stats", [TR, CT, 6])
        mv = per_lane("mv", [TR, CT, 2])
        rstd = per_lane("rstd", [TR, CT])
        big = per_lane("big", [128, 6 * CW])
        big2 = per_lane("big2", [128, 3 * CW])
        sc = per_lane("sc", [128, HEADS * TR])
        pT = per_lane("pT", [TR, HEADS, TR])
        small = per_lane("small", [128, 64])
        r_wide = [wB[0][0:TR, n * NT * 32:(n + 1) * NT * 32] for n in range(4)] + [wA[0][0:TR, 0:NT * 32]]
        r_row = wB[1][0:1, :]
        r_small = wA[1][:, 0:1024]

        bc = lambda ap, shape: ap.broadcast_to(shape)

        ps_flat = ps[:, :, :].rearrange("p b n -> p (b n)")

        def half(l, n, rows, cols):
            o = (8 * l + n) * HALF
            return ps_flat[0:rows, o:o + cols]

        def span(l, n, count, rows, cols):
            o = (8 * l + n) * HALF
            return ps_flat[0:rows, o:o + count * HALF].rearrange("p (c n) -> p c n", c=count)[:, :, 0:cols]

        class stage:

            def __enter__(self):
                self.sems, self.stack = [], ExitStack()
                return self

            def semaphore(self, name):
                self.sems.append(nc.alloc_semaphore(name))
                return self.sems[-1]

            def block(self):
                return self.stack.enter_context(nc.Block())

            def __exit__(self, *error):
                self.stack.__exit__(*error)
                if not error[0]:
                    nc.clear_and_free_semaphores(self.sems)
                    nc.all_engine_barrier()

        def transpose_chunk(pe, src, l, n):
            for k in range(2):
                for j in range(CT):
                    mm = pe.transpose(half(l, n + k, DH, CW)[:, j * TR:(j + 1) * TR], src[:, j, k * DH:(k + 1) * DH],
                                      ident[0:TR, 0:TR])
            return mm

        def project(pe, xT, w, ncols, out_of, kk=2):
            for j in range(CT):
                for k in range(kk):
                    mm = pe.matmul(out_of(j), xT[:, k, j * TR:(j + 1) * TR], w[:, k, 0:ncols],
                                   start=(k == 0), stop=(k == kk - 1))
            return mm

        def project_wide(pe, l, n, rows, w, m, xT=None):
            for k in range(2):
                mm = pe.matmul(half(l, n, rows, CW), w[:, k, m:m + rows], hT[l][:, k, :], start=(k == 0), stop=(k == 1))
            return mm

        def norm_dve(dve, ch, S, l, i, src=None):
            for j in range(CT):
                ins = dve.bn_stats(stats[l][:, j, :], (src or A1)[l][:, j, :])
            ch.link(ins, alone=True)
            for j in range(CT):
                ins = dve.bn_aggr(mv[l][:, j, :], stats[l][:, j, :])
            ins.then_inc(S["stats_made"], 1)

        def norm_dve_end(dve, S, l, i, src=None, dst=None):
            dve.wait_ge(S["rstd_made"], i + 1)
            for j in range(CT):
                ins = dve.tensor_scalar((dst or A2)[l][:, j, :], (src or A1)[l][:, j, :], mv[l][:, j, 0:1], rstd[l][:, j:j + 1],
                                        ALU.subtract, ALU.mult)
            ins.then_inc(S["normed"], 1)

        def norm_pool(pool, ch, S, l, i):
            hold(pool, S["stats_made"], i + 1)
            ch.link(pool.tensor_scalar(rstd[l][:, :], mv[l][:, :, 1], EPS, None, ALU.add))
            pool.tensor_tensor(rstd[l][:, :], rstd[l][:, :], negh[0:TR, 0:CT], ALU.pow).then_inc(S["rstd_made"], 1)

        def lane_semaphores(ctx, stage_name, names):
            return [{n: ctx.semaphore(f"{stage_name}{l}_{n}") for n in names.split()} for l in LANES]

        def turn_act(act, S, l, n, i):
            act.wait_ge(S["tr_ps"], i + 1)
            act.activation(hT[l][:, :, :], span(l, n, 2, DH, CW), ACT.Copy).then_inc(S["hT_made"], 1)

        def keep(pool, S, l, i, norms):
            hold(pool, S["normed"], norms + 1)
            pool.tensor_copy(H[:, ds((i * 2 + l) * CT, CT), :], A2[l][:, :, :]).then_inc(S["kept"], 1)

        def gather(pool, ch, S, l, chunk, choices):
            ch.link(pool.tensor_copy(find[l][:, :, :], slot_of[:, :, ds(chunk * CT, CT)]), alone=True)
            for k in range(choices):
                for j in range(CT):
                    pool.indirect_dma_start(found[l][:, k, j, :], None, slots_out,
                                            bass.IndirectOffsetOnAxis(find[l][:, k, j:j + 1], 0)).then_inc(S["gathered"], 16)

        def combine_pool(pool, S, l, i, choices):
            hold(pool, S["gathered"], (i + 1) * (16 * choices * CT))
            pool.tensor_tensor(A0[l][:, :, :], found[l][:, 0, :, :],
                               bc(coef[:, 0, ds((i * 2 + l) * CT, CT)].unsqueeze(2), [TR, CT, D]),
                               ALU.mult).then_inc(S["first_made"], 1)

        def combine_dve(dve, ch, S, l, i, second):
            tiles = ds((i * 2 + l) * CT, CT)
            dve.wait_ge(S["first_made"], i + 1)
            ch.link(dve.tensor_tensor(A1[l][:, :, :], second, bc(coef[:, 1, tiles].unsqueeze(2), [TR, CT, D]), ALU.mult))
            dve.tensor_tensor(A0[l][:, :, :], A0[l][:, :, :], H[:, tiles, :], ALU.add).then_inc(S["found_used"], 1)
            dve.wait_ge(S["found_used"], i + 1)
            ch.link(dve.tensor_tensor(A1[l][:, :, :], A1[l][:, :, :], A0[l][:, :, :], ALU.add))

        def hidden_pe(pe, S, l, w1):
            for m in range(FM):
                mm = project_wide(pe, l, 2 + m, 128, w1, m * 128)
                if m % 2:
                    mm.then_inc(S["hid_ps"], 1)

        def hidden_act(act, S, l, i, bias):
            for m in range(FM):
                act.wait_ge(S["hid_ps"], i * (FM // 2) + m // 2 + 1)
                ins = act.activation(big[l][:, m * CW:(m + 1) * CW], half(l, 2 + m, 128, CW), ACT.Gelu, bias=bias[:, m:m + 1])
            ins.then_inc(S["hid_made"], 1)

        def mlp_out_pe(pe, S, l, i, w2):
            pe.wait_ge(S["hid_made"], i + 1)
            project(pe, big[l][:, :].rearrange("p (k n) -> p k n", k=FM), w2, D, lambda j: half(l, j, TR, D), FM).then_inc(
                S["mlp_ps"], 1)

        def setup():
            with stage() as ctx:
                sem = ctx.semaphore
                loaded, zeros_set = sem("loaded"), sem("zeros_set")
                dve_step = sem("dve_step")
                rope_scores, shifted, exped, rope_probs, turned = (
                    sem("rope_scores"), sem("shifted"), sem("exped"), sem("rope_probs"), sem("turned"))
                zero_proj = sem("zero_proj")
                block = ctx.block()
                zeros = common[:, 0:NT, :].rearrange("p t n -> p (t n)")
                full = 16 * early

                @block.sync
                def _(sp):
                    for dst, src in loads[:early]:
                        sp.dma_start(dst[:], src).then_inc(loaded, 16)
                    sp.wait_ge(loaded, full)

                @block.tensor
                def _(pe):
                    pe.wait_ge(loaded, full)
                    for k in range(2):
                        mm = pe.matmul(ps[0:TR, 0, 0:TR], tab["ropeT"][:, k, :], tab["ropeT"][:, k, :],
                                       start=(k == 0), stop=(k == 1))
                    mm.then_inc(rope_scores, 1)
                    pe.wait_ge(zeros_set, 1)
                    for k in range(2):
                        mm = pe.matmul(ps[0:TR, 1, 0:D], zeros[0:DH, 0:TR], tab["proj_w"][:, k, :],
                                       start=(k == 0), stop=(k == 1))
                    mm.then_inc(zero_proj, 1)
                    pe.wait_ge(rope_probs, 1)
                    pe.transpose(ps[0:TR, 2, 0:TR], sc[0][0:TR, 0:TR], ident[0:TR, 0:TR]).then_inc(turned, 1)

                @block.scalar
                def _(act):
                    act.wait_ge(shifted, 1)
                    act.activation(sc[0][0:TR, 0:TR], sc[0][0:TR, 0:TR], ACT.Exp).then_inc(exped, 1)

                @block.vector
                def _(dve):
                    ch = Chain(dve, dve_step)
                    dve.memset(common[:, :, :], 0.0).then_inc(zeros_set, 1)
                    dve.memset(H[:, NT:NA, :], 0.0)
                    dve.memset(coef[:, :, NT:NA], 0.0)
                    dve.memset(negh[:, :], -0.5)
                    dve.memset(slot_of[:, :, :], 0)
                    for u in range(2):
                        dve.memset(zT[u][0:64, :], 0.0)
                        dve.memset(zT[u][64:65, :], 1.0)
                        dve.memset(wC[u][:, :], 0.0)
                    dve.wait_ge(loaded, full)
                    dve.tensor_copy(before16[:, :], tab["before"][:, :])
                    dve.tensor_copy(ones16[:, :], tab["ones"][0:TR, 0:TR])
                    s = sc[0][0:TR, 0:TR]
                    dve.wait_ge(rope_scores, 1)
                    ch.link(dve.tensor_tensor(s, ps[0:TR, 0, 0:TR], tab["block_neg"][:, :], ALU.add))
                    ch.link(dve.tensor_reduce(small[0][0:TR, 0:1], s, AX, ALU.max))
                    dve.tensor_scalar(s, s, small[0][0:TR, 0:1], None, ALU.subtract).then_inc(shifted, 1)
                    dve.wait_ge(exped, 1)
                    ch.link(dve.tensor_reduce(small[0][0:TR, 1:2], s, AX, ALU.add))
                    ch.link(dve.reciprocal(small[0][0:TR, 2:3], small[0][0:TR, 1:2]))
                    dve.tensor_scalar(s, s, small[0][0:TR, 2:3], None, ALU.mult).then_inc(rope_probs, 1)
                    ch.link(dve.tensor_tensor(tab["pos"][:, :], tab["pos"][:, :], tab["conv_b"][:, :], ALU.add))
                    dve.wait_ge(zero_proj, 1)
                    dve.tensor_tensor(pbias[:, :], ps[0:TR, 1, 0:D], tab["proj_b"][:, :], ALU.add)
                    dve.wait_ge(turned, 1)
                    dve.tensor_copy(ropeP[:, :], ps[0:TR, 2, 0:TR])

        def embed_and_rope_attention():
            with stage() as ctx:
                S = lane_semaphores(ctx, "a", "patches_in emb_ps h0_made tr_ps hT_made v_ps v_made av_ps av_made o_ps "
                                    "stats_made rstd_made normed kept logits_ps logits_taken")
                dve_step, pool_step, cleared, loaded = map(ctx.semaphore, "a_dve_step a_pool_step a_cleared a_loaded".split())
                block = ctx.block()
                patches = [x[:, :].rearrange("p (k n) -> p k n", k=PK) for x in big]
                v = [x[0:TR, 0:CT * 64].rearrange("p (t n) -> p t n", t=CT) for x in big2]
                av = [x[0:64, 2 * CW:3 * CW] for x in big2]

                @block.sync
                def _(sp):
                    for l in LANES:
                        sp.dma_start(big[l][:, :], d["patches"][l]).then_inc(S[l]["patches_in"], 16)
                    with sp.Fori(1, NSTEP) as i:
                        for l in LANES:
                            hold(sp, S[l]["emb_ps"], i)
                            sp.dma_start(big[l][:, :], d["patches"][ds(i * 2 + l, 1)].rearrange("o p n -> (o p) n")
                                         ).then_inc(S[l]["patches_in"], 16)
                    for dst, src in loads[early:]:
                        sp.dma_start(dst[:], src).then_inc(loaded, 16)
                    sp.wait_ge(loaded, 16 * (len(loads) - early))

                @block.tensor
                def _(pe):
                    with pe.Fori(0, NSTEP) as i:
                        for l in LANES:
                            pe.wait_ge(S[l]["patches_in"], i * 16 + 16)
                            project(pe, patches[l], tab["conv_w"], D, lambda j: half(l, j, TR, D), PK).then_inc(
                                S[l]["emb_ps"], 1)
                        for l in LANES:
                            pe.wait_ge(S[l]["h0_made"], i + 1)
                            transpose_chunk(pe, A0[l], l, 2).then_inc(S[l]["tr_ps"], 1)
                        for l in LANES:
                            pe.wait_ge(S[l]["hT_made"], i * 2 + 1)
                            project(pe, hT[l], tab["wv0"], 64, lambda j: half(l, 4, TR, 128)[:, j * 64:(j + 1) * 64]).then_inc(
                                S[l]["v_ps"], 1)
                        for l in LANES:
                            pe.wait_ge(S[l]["v_made"], i + 1)
                            for j in range(CT):
                                mm = pe.matmul(half(l, 6, 64, CW)[:, j * TR:(j + 1) * TR], v[l][:, j, :], ropeP[:, :],
                                               start=True, stop=True)
                            mm.then_inc(S[l]["av_ps"], 1)
                        for l in LANES:
                            pe.wait_ge(S[l]["av_made"], i + 1)
                            for j in range(CT):
                                mm = pe.matmul(half(l, j, TR, D), av[l][:, j * TR:(j + 1) * TR], tab["wo0"][:, :],
                                               start=True, stop=True)
                            mm.then_inc(S[l]["o_ps"], 1)
                        for l in LANES:
                            pe.wait_ge(S[l]["normed"], i + 1)
                            transpose_chunk(pe, A2[l], l, 2).then_inc(S[l]["tr_ps"], 1)
                        for l in LANES:
                            pe.wait_ge(S[l]["hT_made"], i * 2 + 2)
                            project(pe, hT[l], tab["gate0"], 32, lambda j: half(l, 4, TR, 64)[:, j * 32:(j + 1) * 32]).then_inc(
                                S[l]["logits_ps"], 1)

                @block.scalar
                def _(act):
                    with act.Fori(0, NSTEP) as i:
                        for l in LANES:
                            turn_act(act, S[l], l, 2, i * 2)
                        for l in LANES:
                            act.wait_ge(S[l]["v_ps"], i + 1)
                            act.activation(big2[l][0:TR, 0:CT * 64], half(l, 4, TR, CT * 64), ACT.Copy).then_inc(
                                S[l]["v_made"], 1)
                        for l in LANES:
                            act.wait_ge(S[l]["av_ps"], i + 1)
                            act.activation(av[l], half(l, 6, 64, CW), ACT.Copy).then_inc(S[l]["av_made"], 1)
                        for l in LANES:
                            turn_act(act, S[l], l, 2, i * 2 + 1)

                @block.gpsimd
                def _(pool):
                    slots = [buf.rearrange("(t p n) d -> t p (n d)", p=64, n=16) for buf in (slots_in, slots_out)]
                    parts = slots[0].shape[0] // NSTEP
                    assert parts * NSTEP == slots[0].shape[0]
                    ch = Chain(pool, pool_step, 2)
                    for l in LANES:
                        pool.sem_inc(S[l]["kept"], 1)
                    with pool.Fori(0, NSTEP) as i:
                        ch.start(i)
                        for w in slots:
                            for n in range(parts):
                                pool.dma_start(w[ds(i * parts + n, 1)].rearrange("o p n -> (o p) n"),
                                               common[0:64, 0:NT, :].rearrange("p t n -> p (t n)")).then_inc(cleared, 16)
                        for l in LANES:
                            norm_pool(pool, ch, S[l], l, i)
                        for l in LANES:
                            keep(pool, S[l], l, i, i)
                        ch.end()
                    pool.wait_ge(cleared, 2 * NSTEP * parts * 16)

                @block.vector
                def _(dve):
                    ch = Chain(dve, dve_step, 4)
                    with dve.Fori(0, NSTEP) as i:
                        ch.start(i)
                        for l in LANES:
                            dve.wait_ge(S[l]["emb_ps"], i + 1)
                            dve.tensor_tensor(A0[l][:, :, :], span(l, 0, 2, TR, D),
                                              bc(tab["pos"][:, :].unsqueeze(1), [TR, CT, D]), ALU.add).then_inc(
                                S[l]["h0_made"], 1)
                        for l in LANES:
                            dve.wait_ge(S[l]["o_ps"], i + 1)
                            ch.link(dve.tensor_tensor(A1[l][:, :, :], span(l, 0, 2, TR, D), A0[l][:, :, :], ALU.add))
                            norm_dve(dve, ch, S[l], l, i)
                        for l in LANES:
                            dve.wait_ge(S[l]["kept"], i + 1)
                            norm_dve_end(dve, S[l], l, i)
                        for l in LANES:
                            dve.wait_ge(S[l]["logits_ps"], i + 1)
                            dve.tensor_scalar(logits[:, ds((i * 2 + l) * CT, CT), :],
                                              half(l, 4, TR, 64).rearrange("p (t n) -> p t n", t=CT),
                                              1.0, None, ALU.mult)
                        ch.end()

        def route(r):
            E, K = MOE[r]
            with stage() as ctx:
                sem = lambda n: ctx.semaphore(f"r{r}_{n}")
                dve_step, shifted, exped, masked, ranked, counted, tiles_known, starts_ps, slots_known, scattered = map(
                    sem, ("dve_step shifted exped masked ranked counted tiles_known starts_ps slots_known scattered").split())
                block = ctx.block()
                wide = lambda i: r_wide[i][:, 0:NT * E].rearrange("p (t e) -> p t e", t=NT)
                probs, cand, at_slot = wide(0), wide(1), wide(2)
                hot = [wide(3), wide(4)]
                tiny = lambda i: r_small[0:TR, 512 + i * NT:512 + (i + 1) * NT]
                over_e = lambda x: bc(x.unsqueeze(2), [TR, NT, E])
                order = bc(tab["rank_order"][:, 0:E].unsqueeze(1), [TR, NT, E])

                @block.scalar
                def _(act):
                    act.wait_ge(shifted, 1)
                    act.activation(probs, probs, ACT.Exp).then_inc(exped, 1)

                @block.tensor
                def _(pe):
                    pe.wait_ge(masked, 1)
                    m = lambda j, n=1: mask[:, j * E:(j + n) * E]
                    for j in range(NT):
                        mm = pe.matmul(ps[0:E, 1, 0:1], m(j), ones16[0:TR, 0:1], start=(j == 0), stop=(j == NT - 1))
                    mm.then_inc(counted, 1)
                    pe.matmul(ps[0:TR, 0, 0:NT * E], before16[:, :], m(0, NT), start=True, stop=True)
                    for j in range(NT - 1):
                        mm = pe.matmul(ps[0:TR, 0, (j + 1) * E:NT * E].rearrange("p (t e) -> p t e", e=E),
                                       ones16[0:TR, 0:TR], bc(m(j).unsqueeze(1), [TR, NT - 1 - j, E]),
                                       start=False, stop=True, skip_group_check=True)
                    mm.then_inc(ranked, 1)
                    pe.wait_ge(tiles_known, 1)
                    pe.matmul(ps[0:TR, 2, 0:2 * E].rearrange("p (a e) -> p a e", a=2), r_small[0:E, 0:TR],
                              tab["exp_order"][0:E, :, 0:E], start=True, stop=True).then_inc(starts_ps, 1)

                @block.gpsimd
                def _(pool):
                    for k in range(K):
                        pool.wait_ge(slots_known, k + 1)
                        for t in range(NT):
                            pool.indirect_dma_start(slots_in, bass.IndirectOffsetOnAxis(slot_of[:, k, t:t + 1], 0),
                                                    H[:, t, :], None).then_inc(scattered, 16)
                    pool.wait_ge(scattered, 16 * K * NT)

                @block.vector
                def _(dve):
                    ch = Chain(dve, dve_step)
                    ch.link(dve.tensor_reduce(tiny(0), logits[:, :, 0:E], AX, ALU.max))
                    dve.tensor_tensor(probs, logits[:, :, 0:E], over_e(tiny(0)), ALU.subtract).then_inc(shifted, 1)
                    dve.wait_ge(exped, 1)
                    ch.link(dve.tensor_reduce(tiny(1), probs, AX, ALU.add))
                    ch.link(dve.reciprocal(tiny(2), tiny(1)))
                    ch.link(dve.tensor_tensor(probs, probs, over_e(tiny(2)), ALU.mult))
                    for k in range(K):
                        ch.link(dve.tensor_reduce(coef[:, k, 0:NT], probs, AX, ALU.max))
                        ch.link(dve.tensor_tensor(cand, probs, over_e(coef[:, k, 0:NT]), ALU.is_equal))
                        ch.link(dve.tensor_tensor(cand, cand, order, ALU.mult))
                        ch.link(dve.tensor_reduce(tiny(3), cand, AX, ALU.max))
                        ch.link(dve.tensor_tensor(hot[k], order, over_e(tiny(3)), ALU.is_equal))
                        if k + 1 < K:
                            ch.link(dve.scalar_tensor_tensor(probs, hot[k], -2.0, probs, ALU.mult, ALU.add))
                    mask3 = mask[:, 0:NT * E].rearrange("p (t e) -> p t e", t=NT)
                    if K == 2:
                        dve.tensor_tensor(mask3, hot[0], hot[1], ALU.add).then_inc(masked, 1)
                    else:
                        dve.tensor_copy(mask3, hot[0]).then_inc(masked, 1)
                    dve.wait_ge(counted, 1)
                    fill = r_small[0:E, 256:256 + THR]
                    ch.link(dve.tensor_scalar(fill, tab["fills"][0:E, :], ps[0:E, 1, 0:1], None, ALU.is_lt))
                    ch.link(dve.tensor_reduce(r_small[0:E, 300:301], fill, AX, ALU.add))
                    dve.tensor_scalar(r_small[0:E, 0:TR], tab["ones"][0:E, 0:TR], r_small[0:E, 300:301], None,
                                      ALU.mult).then_inc(tiles_known, 1)
                    if r == 0:
                        ch.link(dve.tensor_tensor(tiny(0), coef[:, 0, 0:NT], coef[:, 1, 0:NT], ALU.add))
                        ch.link(dve.tensor_scalar(tiny(1), tiny(0), 1e-20, None, ALU.add))
                        ch.link(dve.reciprocal(tiny(2), tiny(1)))
                        ch.link(dve.tensor_tensor(coef[:, :, 0:NT], coef[:, :, 0:NT],
                                                  bc(tiny(2).unsqueeze(1), [TR, 2, NT]), ALU.mult))
                    if r == 1:
                        is0 = hot[0][:, :, 0]
                        ch.link(dve.reciprocal(tiny(0), coef[:, 0, 0:NT]))
                        ch.link(dve.tensor_tensor(tiny(0), tiny(0), coef[:, 0, 0:NT], ALU.mult))
                        ch.link(dve.tensor_scalar(tiny(1), coef[:, 0, 0:NT], -1.0, 1.0, ALU.mult, ALU.add))
                        ch.link(dve.tensor_tensor(tiny(0), tiny(0), is0, ALU.mult))
                        ch.link(dve.tensor_scalar(tiny(2), is0, -1.0, 1.0, ALU.mult, ALU.add))
                        ch.link(dve.tensor_tensor(tiny(1), tiny(1), tiny(2), ALU.mult))
                        ch.link(dve.tensor_tensor(coef[:, 0, 0:NT], coef[:, 0, 0:NT], tiny(2), ALU.mult))
                        ch.link(dve.tensor_tensor(coef[:, 1, 0:NT], tiny(0), tiny(1), ALU.add))
                    dve.wait_ge(starts_ps, 1)
                    starts = r_small[0:TR, 320:320 + 2 * E]
                    ch.link(dve.tensor_copy(starts, ps[0:TR, 2, 0:2 * E]))
                    dve.wait_ge(ranked, 1)
                    ch.link(dve.tensor_tensor(at_slot, ps[0:TR, 0, 0:NT * E].rearrange("p (t e) -> p t e", t=NT),
                                              bc(starts[:, 0:E].unsqueeze(1), [TR, NT, E]), ALU.add))
                    for k in range(K):
                        ch.link(dve.tensor_tensor(cand, hot[k], at_slot, ALU.mult))
                        ch.link(dve.tensor_reduce(tiny(3), cand, AX, ALU.add))
                        ch.link(dve.tensor_copy(slot_of[:, k, 0:NT], tiny(3)))
                        dve.sem_inc(slots_known, 1)
                    T = max_tiles(E, K)
                    T1 = T + 1
                    ends = starts[0:1, E:2 * E]
                    past = r_row[:, 0:T1 * E].rearrange("p (t e) -> p t e", t=T1)
                    ch.link(dve.tensor_tensor(past, bc(ends.unsqueeze(1), [1, T1, E]),
                                              bc(tab["tile_no"][:, 0:T1].unsqueeze(2), [1, T1, E]), ALU.is_le))
                    ch.link(dve.tensor_reduce(r_small[0:1, 0:T1], past, AX, ALU.add))
                    ch.link(dve.tensor_scalar(exp_of[:, 0:T1], r_small[0:1, 0:T1], float(E - 1), None, ALU.min))
                    ch.link(dve.tensor_scalar(r_small[0:1, 80:80 + T // 2], tab["pair_no"][:, 0:T // 2],
                                              ends[:, E - 1:E], None, ALU.is_lt))
                    ch.link(dve.tensor_reduce(r_small[0:1, 128:129], r_small[0:1, 80:80 + T // 2], AX, ALU.add))
                    dve.tensor_copy(n_pairs[:, :], r_small[0:1, 128:129])

        def experts(r):
            E, K = MOE[r]
            T = max_tiles(E, K)
            M1 = 4 if r == 0 else FM
            HM = M1 * 128
            with stage() as ctx:
                sem = lambda n: ctx.semaphore(f"e{r}_{n}")
                two = lambda n: [sem(n + "0"), sem(n + "1")]
                x_in, wa_in, b_in, wb_in, wc_in, y_out = map(two, "x_in wa_in b_in wb_in wc_in y_out".split())
                x_ps, xT_made, h1_ps, h1_made, h2_ps, h2_made, z_ps, z_made, y_ps, y_made, y_left = map(
                    sem, "x_ps xT_made h1_ps h1_made h2_ps h2_made z_ps z_made y_ps y_made y_left".split())
                block = ctx.block()
                h1_bank = lambda u: 2 + u if r == 0 else 2 + 2 * u
                wb_free = z_ps if r == 0 else y_ps

                def steps(eng):
                    return eng.value_load(n_pairs[0:1, 0:1], min_val=1, max_val=T // 2)

                @block.sync
                def _(sp):
                    n = steps(sp)
                    for s in (h1_ps, h1_made, z_ps):
                        sp.sem_inc(s, 2)
                    sp.sem_inc(y_ps, 1 if r == 0 else 2)
                    if r == 0:
                        sp.sem_inc(z_made, 1)
                        for u in range(2):
                            sp.sem_inc(wc_in[u], 16)

                    def piece(name, t):
                        e = sp.value_load(exp_of[0:1, ds(t, 1)], min_val=0, max_val=E - 1)
                        return d[name][ds(e, 1)].rearrange("o p n -> (o p) n")

                    def load_x(t, u):
                        sp.dma_start(xin[u][:, :], slots_in[ds(t * SLOT, SLOT), :]).then_inc(x_in[u], 16)

                    def load_first(t, u):
                        sp.dma_start(wA[u][0:DH, 0:2 * HM], piece(f"e{r}_a", t)).then_inc(wa_in[u], 16)
                        if r < 2:
                            hold(sp, h1_made, t + 1)
                            sp.dma_start(b1[u][:, 0:M1], piece(f"e{r}_b1", t)).then_inc(b_in[u], 16)

                    def load_w(t, u):
                        hold(sp, wb_free, t + 1)
                        sp.dma_start(wB[u][:, 0:d[f"e{r}_b"].shape[2]], piece(f"e{r}_b", t)).then_inc(wb_in[u], 16)
                        if r == 0:
                            hold(sp, y_ps, t + 1)
                            sp.dma_start(wC[u][:, :], piece("e0_c", t)).then_inc(wc_in[u], 16)
                        if r == 1:
                            sp.dma_start(wD[u][:, :], piece("e1_d", t)).then_inc(wc_in[u], 16)

                    load_x(0, 0)
                    if r > 0:
                        load_x(1, 1)
                    load_first(0, 0)
                    with sp.Fori(0, n) as i:
                        for u in range(2):
                            t = i * 2 + u
                            if r > 0:
                                hold(sp, x_ps, t + 1)
                                load_x(t + 2, u)
                            hold(sp, h1_ps, t + 2)
                            if r == 0:
                                load_x(t + 1, 1 - u)
                            load_first(t + 1, 1 - u)
                            load_w(t, u)
                    for u in range(2 if r > 0 else 1):
                        hold(sp, x_in[u], n * 16 + 16)
                    hold(sp, wa_in[0], n * 16 + 16)
                    if r < 2:
                        hold(sp, b_in[0], n * 16 + 16)

                @block.tensor
                def _(pe):
                    n = steps(pe)

                    def turn(t, u, nth):
                        pe.wait_ge(x_in[u], nth * 16)
                        for k in range(2):
                            mm = pe.transpose(ps[0:DH, u, k * SLOT:(k + 1) * SLOT], xin[u][:, k * DH:(k + 1) * DH],
                                              ident[:, :])
                        mm.then_inc(x_ps, 1)

                    def first_layer(t, u, nth):
                        w1 = wA[u][0:DH, 0:2 * HM].rearrange("p (k n) -> p k n", k=2)
                        pe.wait_ge(xT_made, t + 1)
                        pe.wait_ge(wa_in[u], nth * 16)
                        for m in range(M1):
                            for k in range(2):
                                mm = pe.matmul(ps[:, h1_bank(u) + m // 4, (m % 4) * SLOT:(m % 4 + 1) * SLOT],
                                               w1[:, k, m * 128:(m + 1) * 128], xT[u][:, k, :],
                                               start=(k == 0), stop=(k == 1))
                        mm.then_inc(h1_ps, 1)

                    def last_layer(t, u, nth):
                        pe.wait_ge(z_made, t + 2)
                        pe.wait_ge(wc_in[u], nth * 16 + 16)
                        pe.matmul(ps[:, 6 + u, 256:256 + D], zT[u][:, :], wC[u][:, 0:D],
                                  start=True, stop=True).then_inc(y_ps, 1)

                    turn(0, 0, 1)
                    if r > 0:
                        turn(1, 1, 1)
                    first_layer(0, 0, 1)
                    with pe.Fori(0, n) as i:
                        for u in range(2):
                            t = i * 2 + u
                            following = (t + 1, 1 - u, i + 1 + u)
                            if r == 0:
                                turn(*following)
                                last_layer(t - 1, 1 - u, i + u)
                                w2 = wB[u][:, 0:2048].rearrange("p (k n) -> p k n", k=4)
                                w3 = wB[u][:, 2048:2304].rearrange("p (k n) -> p k n", k=4)
                                pe.wait_ge(h1_made, t + 3)
                                pe.wait_ge(wb_in[u], i * 16 + 16)
                                for m in range(4):
                                    for k in range(4):
                                        mm = pe.matmul(ps[:, 4 + u, m * SLOT:(m + 1) * SLOT],
                                                       w2[:, k, m * 128:(m + 1) * 128], hid[u][:, k, :],
                                                       start=(k == 0), stop=(k == 3))
                                mm.then_inc(h2_ps, 1)
                                first_layer(*following)
                                pe.wait_ge(h2_made, t + 1)
                                pe.wait_ge(y_made, t + 1)
                                for k in range(4):
                                    mm = pe.matmul(ps[0:64, 6 + u, 0:SLOT], w3[:, k, :], hid2[u][:, k, :],
                                                   start=(k == 0), stop=(k == 3))
                                mm.then_inc(z_ps, 1)
                            else:
                                first_layer(*following)
                                turn(t + 2, u, i + 2)
                                w2 = wB[u][:, 0:FM * D].rearrange("p (k n) -> p k n", k=FM)
                                pe.wait_ge(h1_made, t + 3)
                                pe.wait_ge(wb_in[u], i * 16 + 16)
                                y = ps[:, 6 + u, 256:256 + D]
                                pe.wait_ge(y_made, t + 1)
                                for k in range(FM):
                                    mm = pe.matmul(y, hid[u][:, k, :], w2[:, k, :], start=(k == 0),
                                                   stop=(r == 2 and k == FM - 1))
                                if r == 1:
                                    pe.wait_ge(wc_in[u], i * 16 + 16)
                                    mm = pe.matmul(y, tab["ones"][0:1, 0:SLOT], wD[u][:, :], start=False, stop=True)
                                mm.then_inc(y_ps, 1)
                    if r == 0:
                        last_layer(n * 2 - 1, 1, n)

                @block.scalar
                def _(act):
                    n = steps(act)

                    def x_copied(t, u):
                        act.wait_ge(x_ps, t + 1)
                        act.activation(xT[u][:, :, :], ps[0:DH, u, 0:2 * SLOT].rearrange("p (k n) -> p k n", k=2),
                                       ACT.Copy).then_inc(xT_made, 1)

                    def first_act(t, u, nth):
                        bank = h1_bank(u)
                        act.wait_ge(h1_ps, t + 3)
                        if r < 2:
                            act.wait_ge(b_in[u], nth * 16)
                        if r == 2:
                            for b, m0, m1 in ((0, 0, 4), (1, 4, 6)):
                                ins = act.activation(hid[u][:, m0:m1, :],
                                                     ps[:, bank + b, 0:(m1 - m0) * SLOT].rearrange("p (m n) -> p m n", m=m1 - m0),
                                                     ACT.Relu)
                        else:
                            for m in range(M1):
                                ins = act.activation(hid[u][:, m, :], ps[:, bank + m // 4, (m % 4) * SLOT:(m % 4 + 1) * SLOT],
                                                     ACT.Gelu, bias=b1[u][:, m:m + 1])
                        ins.then_inc(h1_made, 1)

                    x_copied(0, 0)
                    if r > 0:
                        x_copied(1, 1)
                    first_act(0, 0, 1)
                    with act.Fori(0, n) as i:
                        for u in range(2):
                            t = i * 2 + u
                            if r > 0:
                                x_copied(t + 2, u)
                            if r == 0:
                                x_copied(t + 1, 1 - u)
                                act.wait_ge(h2_ps, t + 1)
                                for m in range(4):
                                    ins = act.activation(hid2[u][:, m, :], ps[:, 4 + u, m * SLOT:(m + 1) * SLOT],
                                                         ACT.Gelu, bias=wB[u][:, 2304 + m:2305 + m])
                                ins.then_inc(h2_made, 1)
                            first_act(t + 1, 1 - u, i + 1 + u)

                @block.vector
                def _(dve):
                    n = steps(dve)
                    dve.sem_inc(y_made, 2)
                    with dve.Fori(0, n) as i:
                        for u in range(2):
                            t = i * 2 + u
                            if r == 0:
                                dve.wait_ge(wc_in[u], i * 16 + 32)
                                dve.wait_ge(z_ps, t + 3)
                                dve.tensor_scalar(zT[u][0:64, :], ps[0:64, 6 + u, 0:SLOT], wC[u][0:64, D:D + 1], None,
                                                  ALU.add).then_inc(z_made, 1)
                            dve.wait_ge(y_left, t + 1)
                            dve.wait_ge(y_ps, t + 3)
                            dve.tensor_scalar(yo[u][:, :], ps[:, 6 + u, 256:256 + D], 1.0, None,
                                              ALU.mult).then_inc(y_made, 1)

                @block.gpsimd
                def _(pool):
                    n = steps(pool)
                    pool.sem_inc(y_left, 2)
                    with pool.Fori(0, n) as i:
                        for u in range(2):
                            t = i * 2 + u
                            hold(pool, y_made, t + 3)
                            pool.dma_start(slots_out[ds(t * SLOT, SLOT), :], yo[u][:, :]).then_inc(y_out[u], 16)
                            hold(pool, y_out[u], i * 16 + 16)
                            pool.sem_inc(y_left, 1)

        def causal_attention():
            with stage() as ctx:
                S = lane_semaphores(ctx, "b", "gathered found_used first_made stats_made rstd_made normed kept tr_ps hT_made "
                                    "qk_ps q_made k_made v_ps v_made s_ps s_taken max_made centered exped p_ps pT_made "
                                    "sums_made shares_ps shares_made y_ps y_made o_ps logits_ps logits_taken hid_ps hid_made mlp_ps")
                dve_step, pool_step = map(ctx.semaphore, "b_dve_step b_pool_step".split())
                block = ctx.block()
                qk = [x[:, :].rearrange("p (g n) -> p g n", g=6) for x in big]
                v = [x[0:TR, 0:CT * D].rearrange("p (t n) -> p t n", t=CT) for x in big2]
                scores = [x[0:TR, :] for x in sc]
                by_head = lambda x: x.rearrange("p (h n) -> p h n", h=HEADS)
                place = lambda h: (h % 4) * 3 + h // 4
                maxes = [x[0:TR, 0:HEADS] for x in small]
                sums = [x[0:TR, 16:16 + HEADS] for x in small]

                tiles = [(l, j) for j in range(CT) for l in LANES]
                yT_ps = ps[:, 7, 0:3 * TR].rearrange("p (g n) -> p g n", g=3)
                yT = [x[:, :, :].rearrange("p m n -> p (m n)")[:, 0:3 * CW].rearrange("p (g n) -> p g n", g=3) for x in hid]
                spread = [x[0:TR, 0:3 * 128] for x in wA]
                shares_ps = ps[:, 4:7, 4 * TR:5 * TR]
                shares = hid2[0][:, :, :].rearrange("p m n -> p (m n)")[:, 0:3 * TR].rearrange("p (g n) -> p g n", g=3)

                @block.tensor
                def _(pe):
                    def scores_pe(i, n):
                        l, j = tiles[n]
                        if j == 0:
                            pe.wait_ge(S[l]["q_made"], i + 1)
                            pe.wait_ge(S[l]["k_made"], i + 1)
                        if n > 0:
                            before_l, before_j = tiles[n - 1]
                            pe.wait_ge(S[before_l]["s_taken"], i * CT + before_j + 1)
                        t = slice(j * TR, (j + 1) * TR)
                        for h in range(HEADS):
                            g, r = h // 4, h % 4
                            mm = pe.matmul(ps[0:TR, r, g * TR:(g + 1) * TR], qk[l][32 * r:32 * r + HD, g, t],
                                           qk[l][32 * r:32 * r + HD, 3 + g, t], start=True, stop=True,
                                           tile_position=(32 * r, 0))
                        mm.then_inc(S[l]["s_ps"], 1)

                    def turn_pe(i, n):
                        l, j = tiles[n]
                        pe.wait_ge(S[l]["exped"], i * CT + j + 1)
                        if n > 0:
                            before_l, before_j = tiles[n - 1]
                            pe.wait_ge(S[before_l]["shares_made"], i * CT + before_j + 1)
                        for h in range(HEADS):
                            mm = pe.transpose(ps[0:TR, 4 + h // 4, (h % 4) * TR:(h % 4 + 1) * TR],
                                              scores[l][:, h * TR:(h + 1) * TR], ident[0:TR, 0:TR])
                        mm.then_inc(S[l]["p_ps"], 1)

                    def values_pe(i, n):
                        l, j = tiles[n]
                        pe.wait_ge(S[l]["pT_made"], i * CT + j + 1)
                        pe.wait_ge(S[l]["sums_made"], i * CT + j + 1)
                        for g in range(3):
                            mm = pe.matmul(shares_ps[:, g, :], spread[l][:, g * 128:(g + 1) * 128], ident[0:TR, 0:TR],
                                           start=True, stop=True)
                        mm.then_inc(S[l]["shares_ps"], 1)
                        if n > 0:
                            before_l, before_j = tiles[n - 1]
                            pe.wait_ge(S[before_l]["y_made"], i * CT + before_j + 1)
                        for h in range(HEADS):
                            g, r = h // 4, h % 4
                            o = j * D + h * HD
                            mm = pe.matmul(yT_ps[32 * r:32 * r + 32, g, :], big2[l][0:TR, o:o + 32], pT[l][:, place(h), :],
                                           start=True, stop=True)
                        mm.then_inc(S[l]["y_ps"], 1)

                    def out_pe(i, l):
                        pe.wait_ge(S[l]["y_made"], i * CT + CT)
                        project(pe, yT[l], tab["wp1"], D, lambda j: half(l, 2 + j, TR, D), 3).then_inc(S[l]["o_ps"], 1)

                    def v_pe(l):
                        project(pe, hT[l], tab["wv1"], D, lambda j: half(1, 6 * l + j, TR, D)).then_inc(S[l]["v_ps"], 1)

                    with pe.Fori(0, NSTEP) as i:
                        for l in LANES:
                            pe.wait_ge(S[l]["normed"], i * 2 + 1)
                            transpose_chunk(pe, A2[l], l, 2).then_inc(S[l]["tr_ps"], 1)
                        for l in LANES:
                            pe.wait_ge(S[l]["hT_made"], i * 2 + 1)
                            for g in range(6):
                                mm = project_wide(pe, l, 2 + g, 128, tab["wqk1"], g * 128)
                                if g % 2:
                                    mm.then_inc(S[l]["qk_ps"], 1)
                        scores_pe(i, 0)
                        v_pe(0)
                        scores_pe(i, 1)
                        v_pe(1)
                        for n in range(2, 2 * CT):
                            if n == 2:
                                pe.wait_ge(S[0]["v_made"], i + 1)
                            turn_pe(i, n - 2)
                            scores_pe(i, n)
                            if n == 2:
                                pe.wait_ge(S[1]["v_made"], i + 1)
                            values_pe(i, n - 2)
                        turn_pe(i, 2 * CT - 2)
                        values_pe(i, 2 * CT - 2)
                        turn_pe(i, 2 * CT - 1)
                        out_pe(i, 0)
                        values_pe(i, 2 * CT - 1)
                        out_pe(i, 1)
                        for l in LANES:
                            pe.wait_ge(S[l]["normed"], i * 2 + 2)
                            transpose_chunk(pe, A2[l], l, 0).then_inc(S[l]["tr_ps"], 1)
                            pe.wait_ge(S[l]["hT_made"], i * 2 + 2)
                            project(pe, hT[l], tab["gate1"], 9, lambda j: half(l, 0, TR, 18)[:, j * 9:(j + 1) * 9]).then_inc(
                                S[l]["logits_ps"], 1)
                            hidden_pe(pe, S[l], l, tab["com1"])
                        for l in LANES:
                            pe.wait_ge(S[l]["logits_taken"], i + 1)
                            mlp_out_pe(pe, S[l], l, i, tab["com2"])

                @block.scalar
                def _(act):
                    def exp_act(i, n):
                        l, j = tiles[n]
                        act.wait_ge(S[l]["centered"], i * CT + j + 1)
                        act.activation(scores[l], scores[l], ACT.Exp, scale=HD ** -0.5).then_inc(S[l]["exped"], 1)

                    def turned_act(i, n):
                        l, j = tiles[n]
                        act.wait_ge(S[l]["p_ps"], i * CT + j + 1)
                        act.activation(pT[l][:, :, :].rearrange("p (b h) n -> p b (h n)", b=3), ps[0:TR, 4:7, 0:4 * TR],
                                       ACT.Copy).then_inc(S[l]["pT_made"], 1)

                    def shares_act(i, n):
                        l, j = tiles[n]
                        if n > 0:
                            before_l, before_j = tiles[n - 1]
                            act.wait_ge(S[before_l]["y_made"], i * CT + before_j + 1)
                        act.wait_ge(S[l]["shares_ps"], i * CT + j + 1)
                        act.activation(shares, shares_ps, ACT.Copy).then_inc(S[l]["shares_made"], 1)

                    with act.Fori(0, NSTEP) as i:
                        for l in LANES:
                            turn_act(act, S[l], l, 2, i * 2)
                        for l in LANES:
                            for g in range(4):
                                act.wait_ge(S[l]["qk_ps"], i * 3 + g // 2 + 1)
                                ins = act.activation(qk[l][:, g, :], half(l, 2 + g, 128, CW), ACT.Identity,
                                                     bias=tab["bqk1"][:, g:g + 1])
                            ins.then_inc(S[l]["q_made"], 1)
                        exp_act(i, 0)
                        for n in range(1, 2 * CT - 1):
                            exp_act(i, n)
                            turned_act(i, n - 1)
                            shares_act(i, n - 1)
                        turned_act(i, 2 * CT - 2)
                        exp_act(i, 2 * CT - 1)
                        shares_act(i, 2 * CT - 2)
                        turned_act(i, 2 * CT - 1)
                        shares_act(i, 2 * CT - 1)
                        for l in LANES:
                            turn_act(act, S[l], l, 0, i * 2 + 1)
                        for l in LANES:
                            hidden_act(act, S[l], l, i, tab["bcom1"])

                @block.gpsimd
                def _(pool):
                    ch = Chain(pool, pool_step, 2 * (1 + 2))
                    ahead = Chain(pool, pool_step)
                    for l in LANES:
                        gather(pool, ahead, S[l], l, l, 2)
                    for l in LANES:
                        combine_pool(pool, S[l], l, 0, 2)
                    for l in LANES:
                        norm_pool(pool, ahead, S[l], l, 0)
                    with pool.Fori(0, NSTEP) as i:
                        ch.start(i, ahead.n)
                        for l in LANES:
                            hold(pool, S[l]["found_used"], i + 1)
                            gather(pool, ch, S[l], l, i * 2 + 2 + l, 2)
                        for l, j in tiles:
                            hold(pool, S[l]["max_made"], i * CT + j + 1)
                            x = by_head(scores[l])
                            pool.tensor_tensor(x, x, bc(maxes[l].unsqueeze(2), [TR, HEADS, TR]),
                                               ALU.subtract).then_inc(S[l]["centered"], 1)
                        for l in LANES:
                            norm_pool(pool, ch, S[l], l, i * 2 + 1)
                        for l in LANES:
                            combine_pool(pool, S[l], l, i + 1, 2)
                            keep(pool, S[l], l, i, i * 2 + 1)
                        for l in LANES:
                            norm_pool(pool, ch, S[l], l, i * 2 + 2)
                        ch.end()

                @block.vector
                def _(dve):
                    def first_norm(chain, i):
                        for l in LANES:
                            combine_dve(dve, chain, S[l], l, i, found[l][:, 1, :, :])
                            norm_dve(dve, chain, S[l], l, i * 2)

                    def mask_dve(i, n):
                        l, j = tiles[n]
                        dve.wait_ge(S[l]["s_ps"], i * CT + j + 1)
                        dve.tensor_tensor(
                            scores[l].rearrange("p (r g n) -> p r g n", r=4, g=3),
                            ps[0:TR, 0:4, 0:3 * TR].rearrange("p r (g n) -> p r g n", g=3),
                            bc(tab["causal_neg"][:, :].unsqueeze(1).unsqueeze(1), [TR, 4, 3, TR]),
                            ALU.add).then_inc(S[l]["s_taken"], 1)
                        dve.wait_ge(S[l]["s_taken"], i * CT + j + 1)
                        dve.tensor_reduce(maxes[l], by_head(scores[l]), AX, ALU.max).then_inc(S[l]["max_made"], 1)

                    def sum_dve(i, n):
                        l, j = tiles[n]
                        dve.wait_ge(S[l]["exped"], i * CT + j + 1)
                        ch.link(dve.tensor_reduce(sums[l], by_head(scores[l]), AX, ALU.add))
                        ch.link(dve.reciprocal(sums[l], sums[l]))
                        dve.tensor_copy(spread[l].rearrange("p (g r n) -> p g r n", g=3, r=4),
                                        bc(sums[l].rearrange("p (r g) -> p g r", r=4).unsqueeze(3), [TR, 3, 4, 32])).then_inc(
                            S[l]["sums_made"], 1)

                    def scale_dve(i, n):
                        l, j = tiles[n]
                        dve.wait_ge(S[l]["y_ps"], i * CT + j + 1)
                        dve.wait_ge(S[l]["shares_made"], i * CT + j + 1)
                        dve.tensor_tensor(yT[l][:, :, j * TR:(j + 1) * TR], yT_ps, shares, ALU.mult).then_inc(S[l]["y_made"], 1)

                    def k_dve(i, l):
                        dve.wait_ge(S[l]["qk_ps"], i * 3 + 3)
                        for g in (4, 5):
                            ins = dve.tensor_scalar(qk[l][:, g, :], half(l, 2 + g, 128, CW), tab["bqk1"][:, g:g + 1], None,
                                                    ALU.add)
                        ins.then_inc(S[l]["k_made"], 1)

                    def v_dve(i, l):
                        dve.wait_ge(S[l]["v_ps"], i + 1)
                        dve.tensor_tensor(v[l], span(1, 6 * l, 2, TR, D), bc(tab["bv1"][:, :].unsqueeze(1), [TR, CT, D]),
                                          ALU.add).then_inc(S[l]["v_made"], 1)

                    ch = Chain(dve, dve_step, 20)
                    ahead = Chain(dve, dve_step)
                    for l in LANES:
                        dve.memset(big2[l][0:TR, CT * D:CT * D + HD], 0.0)
                    first_norm(ahead, 0)
                    for l in LANES:
                        norm_dve_end(dve, S[l], l, 0)
                    with dve.Fori(0, NSTEP) as i:
                        ch.start(i, ahead.n)
                        for l in LANES:
                            dve.wait_ge(S[l]["normed"], i * 2 + 1)
                            ch.link(dve.tensor_tensor(A1[l][:, :, :], A2[l][:, :, :],
                                                      bc(tab["bp1"][:, :].unsqueeze(1), [TR, CT, D]), ALU.add))
                        k_dve(i, 0)
                        k_dve(i, 1)
                        mask_dve(i, 0)
                        v_dve(i, 0)
                        mask_dve(i, 1)
                        v_dve(i, 1)
                        for n in range(2, 2 * CT):
                            sum_dve(i, n - 2)
                            mask_dve(i, n)
                            scale_dve(i, n - 2)
                        for n in (2 * CT - 2, 2 * CT - 1):
                            sum_dve(i, n)
                            scale_dve(i, n)
                        for l in LANES:
                            dve.wait_ge(S[l]["o_ps"], i + 1)
                            ch.link(dve.tensor_tensor(A1[l][:, :, :], span(l, 2, 2, TR, D), A1[l][:, :, :], ALU.add))
                            norm_dve(dve, ch, S[l], l, i * 2 + 1)
                            norm_dve_end(dve, S[l], l, i * 2 + 1)
                        for l in LANES:
                            dve.wait_ge(S[l]["logits_ps"], i + 1)
                            dve.tensor_tensor(logits[:, ds((i * 2 + l) * CT, CT), 0:9],
                                              half(l, 0, TR, 18).rearrange("p (t n) -> p t n", t=CT),
                                              bc(tab["bgate1"][:, :].unsqueeze(1), [TR, CT, 9]),
                                              ALU.add).then_inc(S[l]["logits_taken"], 1)
                        first_norm(ch, i + 1)
                        for l in LANES:
                            dve.wait_ge(S[l]["kept"], i + 1)
                            norm_dve_end(dve, S[l], l, i * 2 + 2)
                        for l in LANES:
                            dve.wait_ge(S[l]["mlp_ps"], i + 1)
                            dve.tensor_tensor(common[:, ds((i * 2 + l) * CT, CT), :], span(l, 0, 2, TR, D),
                                              bc(tab["bcom2"][:, :].unsqueeze(1), [TR, CT, D]), ALU.add)
                        ch.end()

        def ffn_and_retention():
            with stage() as ctx:
                S = lane_semaphores(ctx, "c", "gathered x_used stats_made rstd_made normed kept tr_ps hT_made "
                                    "hid_ps hid_made mlp_ps v_ps v_made g_ps g_made qk_ps qk_taken rotated s_ps p_made "
                                    "pv_ps sums_made mean_ps centered squared sq_made var_ps var_made gstd_made gated o_ps "
                                    "logits_ps logits_taken")
                dve_step, pool_step = map(ctx.semaphore, "c_dve_step c_pool_step".split())
                block = ctx.block()
                v = [x[0:TR, 0:CT * RH * RV].rearrange("p (t n) -> p t n", t=CT) for x in big]
                gate = [x[:, :].rearrange("p (g n) -> p g n", g=3) for x in big2]
                og = [x[:, 0:3 * CW].rearrange("p (g n) -> p g n", g=3) for x in big]
                sq = [x[:, 3 * CW:6 * CW] for x in big]
                rot = lambda l, n: sc[l][:, n * 2 * CW:(n + 1) * 2 * CW].rearrange("p (a n) -> p a n", a=2)
                imgs = lambda x: x.rearrange("p a (b n) -> p a b n", n=L)
                probs = lambda l, h: (A0, A1)[h % 2][l][:, :, :].rearrange("p t n -> p (t n)")[:, 0:CW].rearrange(
                    "p (t n) -> p t n", t=CT)
                NG = 3 * CB
                gstat = lambda l, n: small[l][:, n * NG:(n + 1) * NG]
                by_image = lambda x: bc(x.rearrange("p (g b) -> p g b", g=3).unsqueeze(3), [128, 3, CB, L])
                og4 = [x.rearrange("p g (b n) -> p g b n", n=L) for x in og]
                o_ps = [span(l, 2, 3, 128, CW).rearrange("p g (b n) -> p g b n", n=L) for l in LANES]
                X = [f[:, 0, :, :] for f in found]
                other = [f[:, 1, :, :] for f in found]
                qb = lambda h: 6 * (h % 2)

                @block.tensor
                def _(pe):
                    def qk_of(i, l, h):
                        if h >= 2:
                            pe.wait_ge(S[l]["qk_taken"], i * RH + h - 1)
                        project_wide(pe, l, qb(h), 128, tab["wq3"], h * RQK)
                        project_wide(pe, l, qb(h) + 1, 128, tab["wk3"], h * RQK).then_inc(S[l]["qk_ps"], 1)

                    with pe.Fori(0, NSTEP) as i:
                        for l in LANES:
                            pe.wait_ge(S[l]["normed"], i * 4 + 2)
                            transpose_chunk(pe, X[l], l, 0).then_inc(S[l]["tr_ps"], 1)
                        for l in LANES:
                            pe.wait_ge(S[l]["hT_made"], i * 3 + 1)
                            pe.wait_ge(S[l]["logits_taken"], i + 1)
                            hidden_pe(pe, S[l], l, tab["ffn1"])
                        for l in LANES:
                            mlp_out_pe(pe, S[l], l, i, tab["ffn2"])
                        def turn(l):
                            pe.wait_ge(S[l]["normed"], i * 4 + 3)
                            transpose_chunk(pe, A2[l], l, 0).then_inc(S[l]["tr_ps"], 1)

                        turn(0)
                        for l in LANES:
                            pe.wait_ge(S[l]["hT_made"], i * 3 + 2)
                            for g in range(3):
                                mm = project_wide(pe, l, (6, 7, 0)[g], 128, tab["wg3"], g * 128)
                            mm.then_inc(S[l]["g_ps"], 1)
                            if l == 0:
                                turn(1)
                            project(pe, hT[l], tab["wv3"], RH * RV, lambda j: ps[0:TR, 4 * l + 1 + j, 0:RH * RV]).then_inc(
                                S[l]["v_ps"], 1)
                        for l in LANES:
                            pe.wait_ge(S[l]["g_made"], i + 1)
                            qk_of(i, l, 0)
                        for l in LANES:
                            qk_of(i, l, 1)
                        for h in range(RH):
                            for l in LANES:
                                if h == 0:
                                    pe.wait_ge(S[l]["v_made"], i + 1)
                                pe.wait_ge(S[l]["rotated"], i * RH + h + 1)
                                r = rot(l, h % 2)
                                for j in range(CT):
                                    t = slice(j * TR, (j + 1) * TR)
                                    mm = pe.matmul(half(l, 5, TR, CW)[:, t], r[:, 1, t], r[:, 0, t], start=True, stop=True)
                                mm.then_inc(S[l]["s_ps"], 1)
                            if h + 2 < RH:
                                for l in LANES:
                                    qk_of(i, l, h + 2)
                            for l in LANES:
                                pe.wait_ge(S[l]["p_made"], i * RH + h + 1)
                                o = (8 * l + 2 + h // 2) * HALF
                                for j in range(CT):
                                    mm = pe.matmul(ps_flat[(h % 2) * 64:(h % 2) * 64 + 64, o + j * TR:o + (j + 1) * TR],
                                                   v[l][:, j, h * RV:(h + 1) * RV], probs(l, h)[:, j, :], start=True, stop=True)
                                if h == RH - 1:
                                    mm.then_inc(S[l]["pv_ps"], 1)
                        for l in LANES:
                            pe.wait_ge(S[l]["sums_made"], i + 1)
                            pe.matmul(half(l, 0, 128, NG), tab["head_mean"][:, :], gstat(l, 0), start=True, stop=True).then_inc(
                                S[l]["mean_ps"], 1)
                        for l in LANES:
                            pe.wait_ge(S[l]["sq_made"], i + 1)
                            pe.matmul(half(l, 0, 128, NG), tab["head_mean"][:, :], gstat(l, 1), start=True, stop=True).then_inc(
                                S[l]["var_ps"], 1)
                        for l in LANES:
                            pe.wait_ge(S[l]["gated"], i + 1)
                            project(pe, og[l], tab["wo3"], D, lambda j: half(l, 6 + j, TR, D), 3).then_inc(S[l]["o_ps"], 1)
                        for l in LANES:
                            pe.wait_ge(S[l]["normed"], i * 4 + 6)
                            transpose_chunk(pe, A2[l], l, 0).then_inc(S[l]["tr_ps"], 1)
                            pe.wait_ge(S[l]["hT_made"], i * 3 + 3)
                            project(pe, hT[l], tab["gate3"], 8, lambda j: half(l, 2, TR, 16)[:, j * 8:(j + 1) * 8]).then_inc(
                                S[l]["logits_ps"], 1)

                @block.scalar
                def _(act):
                    with act.Fori(0, NSTEP) as i:
                        for l in LANES:
                            turn_act(act, S[l], l, 0, i * 3)
                        for l in LANES:
                            hidden_act(act, S[l], l, i, tab["bffn1"])
                        for l in LANES:
                            turn_act(act, S[l], l, 0, i * 3 + 1)
                            act.wait_ge(S[l]["g_ps"], i + 1)
                            for g in range(3):
                                ins = act.activation(gate[l][:, g, :], half(l, (6, 7, 0)[g], 128, CW), ACT.Silu)
                            ins.then_inc(S[l]["g_made"], 1)
                            act.wait_ge(S[l]["v_ps"], i + 1)
                            act.activation(v[l], ps[0:TR, 4 * l + 1:4 * l + 3, 0:RH * RV], ACT.Copy).then_inc(S[l]["v_made"], 1)
                        for l in LANES:
                            act.wait_ge(S[l]["centered"], i + 1)
                            act.activation(sq[l], og[l].rearrange("p g n -> p (g n)"), ACT.Square).then_inc(S[l]["squared"], 1)
                        for l in LANES:
                            turn_act(act, S[l], l, 0, i * 3 + 2)

                @block.gpsimd
                def _(pool):
                    ch = Chain(pool, pool_step, 2 * (1 + 4))
                    ahead = Chain(pool, pool_step)
                    for l in LANES:
                        pool.sem_inc(S[l]["kept"], 1)
                        gather(pool, ahead, S[l], l, l, 1)
                    for n in range(2):
                        for l in LANES:
                            norm_pool(pool, ahead, S[l], l, n)
                    with pool.Fori(0, NSTEP) as i:
                        ch.start(i, ahead.n)
                        for l in LANES:
                            norm_pool(pool, ch, S[l], l, i * 4 + 2)
                        for l in LANES:
                            hold(pool, S[l]["x_used"], i + 1)
                            gather(pool, ch, S[l], l, i * 2 + 2 + l, 1)
                        for n in (3, 4):
                            for l in LANES:
                                norm_pool(pool, ch, S[l], l, i * 4 + n)
                        for h in range(RH):
                            for l in LANES:
                                pool.wait_ge(S[l]["qk_taken"], i * RH + h + 1)
                                pool.tensor_tensor(rot(l, h % 2), rot(l, h % 2), rot(l, 2), ALU.add).then_inc(
                                    S[l]["rotated"], 1)
                        for l in LANES:
                            pool.wait_ge(S[l]["var_made"], i + 1)
                            pool.tensor_tensor(gstat(l, 1), gstat(l, 1), negh[:, 0:NG], ALU.pow).then_inc(S[l]["gstd_made"], 1)
                        for l in LANES:
                            norm_pool(pool, ch, S[l], l, i * 4 + 5)
                        for l in LANES:
                            keep(pool, S[l], l, i, i * 4 + 5)
                        ch.end()

                @block.vector
                def _(dve):
                    def rotate(i, l, h):
                        dve.wait_ge(S[l]["qk_ps"], i * RH + h + 1)
                        if h > 0:
                            dve.wait_ge(S[l]["rotated"], i * RH + h)
                        x, r, t = span(l, qb(h), 2, 128, CW), rot(l, h % 2), rot(l, 2)
                        dve.tensor_tensor(imgs(r), imgs(x), bc(tab["cos_qk"][:, :, :].unsqueeze(2), [128, 2, CB, L]), ALU.mult)
                        for p, o in ((0, 64), (64, 0)):
                            ins = dve.tensor_tensor(imgs(t[o:o + 64]), imgs(x[p:p + 64]),
                                                    bc(tab["sin_qk"][p:p + 64, :, :].unsqueeze(2), [64, 2, CB, L]), ALU.mult)
                        ins.then_inc(S[l]["qk_taken"], 1)

                    def weigh(i, l, h):
                        dve.wait_ge(S[l]["s_ps"], i * RH + h + 1)
                        dve.tensor_tensor(probs(l, h), half(l, 5, TR, CW).rearrange("p (t n) -> p t n", t=CT),
                                          bc(tab["decayT"][:, h, :].unsqueeze(1), [TR, CT, TR]),
                                          ALU.mult).then_inc(S[l]["p_made"], 1)

                    def first_norm(chain, l, i, n):
                        tiles = ds((i * 2 + l) * CT, CT)
                        weight = lambda k: bc(coef[:, k, tiles].unsqueeze(2), [TR, CT, D])
                        dve.wait_ge(S[l]["gathered"], (i + 1) * (16 * CT))
                        dve.tensor_tensor(X[l], X[l], weight(0), ALU.mult)
                        chain.link(dve.tensor_tensor(other[l], common[:, tiles, :], weight(1), ALU.mult))
                        chain.link(dve.tensor_tensor(X[l], X[l], H[:, tiles, :], ALU.add))
                        chain.link(dve.tensor_tensor(X[l], X[l], other[l], ALU.add))
                        norm_dve(dve, chain, S[l], l, n, src=X)

                    def second_norm(chain, l, n):
                        norm_dve_end(dve, S[l], l, n - 1, src=X, dst=X)
                        dve.wait_ge(S[l]["normed"], n)
                        chain.link(dve.tensor_tensor(X[l], X[l], bc(pbias[:, :].unsqueeze(1), [TR, CT, D]), ALU.add))
                        norm_dve(dve, chain, S[l], l, n, src=X)

                    ch = Chain(dve, dve_step, 2 * (1 + 6 + 3 + 2))
                    ahead = Chain(dve, dve_step)
                    for l in LANES:
                        dve.sem_inc(S[l]["logits_taken"], 1)
                        first_norm(ahead, l, 0, 0)
                    for l in LANES:
                        second_norm(ahead, l, 1)
                    for l in LANES:
                        norm_dve_end(dve, S[l], l, 1, src=X, dst=X)
                    with dve.Fori(0, NSTEP) as i:
                        ch.start(i, ahead.n)
                        for l in LANES:
                            dve.wait_ge(S[l]["mlp_ps"], i + 1)
                            dve.tensor_tensor(A1[l][:, :, :], span(l, 0, 2, TR, D), X[l], ALU.add).then_inc(S[l]["x_used"], 1)
                            dve.wait_ge(S[l]["x_used"], i + 1)
                            norm_dve(dve, ch, S[l], l, i * 4 + 2)
                            dve.wait_ge(S[l]["kept"], i + 1)
                            norm_dve_end(dve, S[l], l, i * 4 + 2)
                        for l in LANES:
                            first_norm(ch, l, i + 1, i * 4 + 3)
                        for l in LANES:
                            second_norm(ch, l, i * 4 + 4)
                        for h in range(RH + 1):
                            if h < RH:
                                for l in LANES:
                                    rotate(i, l, h)
                            if h > 0:
                                for l in LANES:
                                    weigh(i, l, h - 1)
                            for l in LANES:
                                if h == 1:
                                    norm_dve_end(dve, S[l], l, i * 4 + 4, src=X, dst=X)
                        for l in LANES:
                            dve.wait_ge(S[l]["pv_ps"], i + 1)
                            dve.tensor_reduce(gstat(l, 0), o_ps[l], AX, ALU.add).then_inc(S[l]["sums_made"], 1)
                        for l in LANES:
                            dve.wait_ge(S[l]["mean_ps"], i + 1)
                            ch.link(dve.tensor_copy(gstat(l, 0), half(l, 0, 128, NG)))
                            dve.tensor_tensor(og4[l], o_ps[l], by_image(gstat(l, 0)), ALU.subtract).then_inc(S[l]["centered"], 1)
                        for l in LANES:
                            dve.wait_ge(S[l]["squared"], i + 1)
                            dve.tensor_reduce(gstat(l, 1), sq[l].rearrange("p (g n) -> p g n", n=L), AX, ALU.add).then_inc(
                                S[l]["sq_made"], 1)
                        for l in LANES:
                            dve.wait_ge(S[l]["var_ps"], i + 1)
                            dve.tensor_scalar(gstat(l, 1), half(l, 0, 128, NG), EPS, None, ALU.add).then_inc(
                                S[l]["var_made"], 1)
                        for l in LANES:
                            dve.wait_ge(S[l]["gstd_made"], i + 1)
                            ch.link(dve.tensor_tensor(gstat(l, 0).rearrange("p (g b) -> p g b", g=3),
                                                      gstat(l, 1).rearrange("p (g b) -> p g b", g=3),
                                                      bc(tab["gnw"][:, :].unsqueeze(2), [128, 3, CB]), ALU.mult))
                            ch.link(dve.tensor_tensor(og4[l], og4[l], by_image(gstat(l, 0)), ALU.mult))
                            for g in range(3):
                                ins = dve.scalar_tensor_tensor(og[l][:, g, :], og[l][:, g, :], tab["gnb"][:, g:g + 1],
                                                               gate[l][:, g, :], ALU.add, ALU.mult)
                            ins.then_inc(S[l]["gated"], 1)
                        for l in LANES:
                            dve.wait_ge(S[l]["o_ps"], i + 1)
                            ch.link(dve.tensor_tensor(A0[l][:, :, :], span(l, 6, 2, TR, D), A2[l][:, :, :], ALU.add))
                            norm_dve(dve, ch, S[l], l, i * 4 + 5, src=A0)
                            norm_dve_end(dve, S[l], l, i * 4 + 5, src=A0)
                        for l in LANES:
                            dve.wait_ge(S[l]["logits_ps"], i + 1)
                            dve.tensor_scalar(logits[:, ds((i * 2 + l) * CT, CT), 0:8],
                                              half(l, 2, TR, 16).rearrange("p (t n) -> p t n", t=CT), 1.0, None,
                                              ALU.mult).then_inc(S[l]["logits_taken"], 1)
                        ch.end()

        def last_norm():
            with stage() as ctx:
                S = lane_semaphores(ctx, "d", "even_gathered odd_gathered found_used stats_made rstd_made normed stored")
                dve_step, pool_step = map(ctx.semaphore, "d_dve_step d_pool_step".split())
                block = ctx.block()
                gathered = lambda l, odd: S[l][("even_gathered", "odd_gathered")[odd]]
                rows = out.rearrange("(t p) n -> p t n", p=TR)

                @block.sync
                def _(sp):
                    for l in LANES:
                        sp.sem_inc(S[l]["stored"], 16)
                    with sp.Fori(0, NSTEP) as i:
                        for l in LANES:
                            hold(sp, S[l]["normed"], i + 1)
                            sp.dma_start(rows[:, ds((i * 2 + l) * CT, CT), :], A2[l][:, :, :]).then_inc(S[l]["stored"], 16)
                    for l in LANES:
                        sp.wait_ge(S[l]["stored"], NSTEP * 16 + 16)

                @block.gpsimd
                def _(pool):
                    def gather_step(l, i, odd):
                        ch.link(pool.tensor_copy(find[l][:, odd, :], slot_of[:, 0, ds((i * 2 + l) * CT, CT)]), alone=True)
                        for j in range(CT):
                            pool.indirect_dma_start(found[l][:, odd, j, :], None, slots_out,
                                                    bass.IndirectOffsetOnAxis(find[l][:, odd, j:j + 1], 0)).then_inc(
                                gathered(l, odd), 16)

                    ch = Chain(pool, pool_step, 8)
                    for odd in range(2):
                        for l in LANES:
                            gather_step(l, odd, odd)
                    with pool.Fori(0, NSTEP // 2 - 1) as k:
                        ch.start(k, 4)
                        for odd in range(2):
                            i = k * 2 + odd
                            for l in LANES:
                                norm_pool(pool, ch, S[l], l, i)
                            for l in LANES:
                                hold(pool, S[l]["found_used"], i + 1)
                                gather_step(l, i + 2, odd)
                        ch.end()
                    ch.start(NSTEP // 2 - 1, 4)
                    for i in (NSTEP - 2, NSTEP - 1):
                        for l in LANES:
                            norm_pool(pool, ch, S[l], l, i)

                @block.vector
                def _(dve):
                    ch = Chain(dve, dve_step, 8)
                    with dve.Fori(0, NSTEP // 2) as k:
                        ch.start(k)
                        for odd in range(2):
                            i = k * 2 + odd
                            for l in LANES:
                                tiles = ds((i * 2 + l) * CT, CT)
                                dve.wait_ge(gathered(l, odd), (k + 1) * (16 * CT))
                                dve.tensor_tensor(A1[l][:, :, :], found[l][:, odd, :, :],
                                                  bc(coef[:, 0, tiles].unsqueeze(2), [TR, CT, D]), ALU.mult).then_inc(
                                    S[l]["found_used"], 1)
                                dve.wait_ge(S[l]["found_used"], i + 1)
                                ch.link(dve.tensor_tensor(A1[l][:, :, :], A1[l][:, :, :], H[:, tiles, :], ALU.add))
                                norm_dve(dve, ch, S[l], l, i)
                            for l in LANES:
                                dve.wait_ge(S[l]["stored"], i * 16 + 16)
                                norm_dve_end(dve, S[l], l, i)
                            for l in LANES:
                                dve.wait_ge(S[l]["normed"], i + 1)
                        ch.end()

        setup()
        embed_and_rope_attention()
        route(0)
        experts(0)
        causal_attention()
        route(1)
        experts(1)
        ffn_and_retention()
        route(2)
        experts(2)
        last_norm()


def halves_k(w):
    return w.reshape(2, DH, -1).transpose(1, 0, 2)


def rows_k(w):
    return w.reshape(-1, 128, w.shape[-1]).transpose(1, 0, 2)


def lay_out(i):
    d = dict(constants())
    rep = lambda v: np.tile(np.asarray(v)[None], (TR, 1))
    x = i["x"].reshape(B, 3, 7, 16, 7, 16).transpose(1, 3, 5, 0, 2, 4).reshape(PK, 128, NCH, CW)
    d["patches"] = x.transpose(2, 1, 0, 3).reshape(NCH, 128, PK * CW)
    d["conv_w"] = rows_k(i["L0_tok_conv_w"].reshape(D, -1).T)
    d["conv_b"] = rep(i["L0_tok_conv_b"])
    bounds = np.arange(1.0 / 32, 1.0, 1.0 / 32, dtype=np.float32)
    at = np.searchsorted(bounds, np.arange(0.0, 1.0 - 1e-06, 1.0 / 7, dtype=np.float32), side="right")
    ids = (at[:, None] * 32 + at).reshape(-1)
    pos = i["L0_tok_pos_table"][ids]
    d["pos"] = np.concatenate([pos, pos], 0)
    d["wv0"] = halves_k(i["L0_attn_Wv"].T)
    d["wo0"] = i["L0_attn_Wo"].T
    d["gate0"] = halves_k(i["L0_ffn_gate_w"].T)
    w, b = i["L1_attn_W_attn"], i["L1_attn_b_attn"]
    wqk = np.zeros((D, 6, 4, 32), np.float32)
    bqk = np.zeros((6, 4, 32), np.float32)
    wqk[..., :HD] = w[:, :2 * D].reshape(D, 6, 4, HD)
    bqk[..., :HD] = b[:2 * D].reshape(6, 4, HD)
    d["wqk1"] = halves_k(wqk.reshape(D, -1))
    d["bqk1"] = bqk.reshape(6, 128).T
    d["wv1"], d["bv1"] = halves_k(w[:, 2 * D:]), rep(b[2 * D:])
    by_row = i["L1_attn_W_proj"].reshape(3, 4, HD, D).transpose(1, 2, 0, 3)
    d["wp1"] = np.concatenate([by_row, np.zeros_like(by_row)], 1).reshape(128, 3, D)
    d["bp1"] = rep(i["L1_attn_b_proj"])
    d["gate1"], d["bgate1"] = halves_k(i["L1_ffn_Ws"]), rep(i["L1_ffn_bs"])
    d["com1"], d["bcom1"] = halves_k(i["L1_ffn_W1"][0]), i["L1_ffn_b1"][0].reshape(FM, 128).T
    d["com2"], d["bcom2"] = rows_k(i["L1_ffn_W2"][0]), rep(i["L1_ffn_b2"][0])
    d["proj_w"], d["proj_b"] = halves_k(i["L2_attn_proj_w"].T), rep(i["L2_attn_proj_b"])
    d["ffn1"], d["bffn1"] = halves_k(i["L2_ffn_in_weight"].T), i["L2_ffn_in_bias"].reshape(FM, 128).T
    d["ffn2"] = rows_k(i["L2_ffn_out_weight"])
    for n, k in (("wq3", "Wq"), ("wk3", "Wk"), ("wv3", "Wv"), ("wg3", "Wg")):
        d[n] = halves_k(i["L3_attn_" + k])
    d["wo3"] = rows_k(i["L3_attn_Wo"])
    d["gnw"], d["gnb"] = (i["L3_attn_gn_" + n].reshape(3, 128).T for n in ("weight", "bias"))
    d["gate3"] = halves_k(i["L3_ffn_router_w"])
    ek = lambda w: w.reshape(w.shape[0], 2, DH, -1).transpose(0, 2, 1, 3).reshape(w.shape[0], DH, -1)
    er = lambda w: w.reshape(w.shape[0], -1, 128, w.shape[-1]).transpose(0, 2, 1, 3).reshape(w.shape[0], 128, -1)
    col = lambda b: b.reshape(b.shape[0], -1, 128).transpose(0, 2, 1)
    d["e0_a"] = ek(i["L0_ffn_W1"])
    d["e0_b1"] = col(i["L0_ffn_b1"])
    d["e0_b"] = np.concatenate([er(i["L0_ffn_W2"]), er(i["L0_ffn_W3"]), col(i["L0_ffn_b2"])], -1)
    wl = np.concatenate([i["L0_ffn_Wl"], i["L0_ffn_bl"][:, None]], 1)
    b3 = np.concatenate([i["L0_ffn_b3"], np.zeros((MOE[0][0], 1), np.float32)], 1)
    d["e0_c"] = np.concatenate([wl, b3[:, :, None]], -1)
    d["e1_a"] = ek(i["L1_ffn_W1"])
    d["e1_b1"] = col(i["L1_ffn_b1"])
    d["e1_b"] = er(i["L1_ffn_W2"])
    d["e1_d"] = i["L1_ffn_b2"][:, None]
    d["e2_a"] = ek(i["L3_ffn_wi"])
    d["e2_b"] = er(i["L3_ffn_wo"])
    return {k: np.ascontiguousarray(v) for k, v in d.items()}


def kernel(**inputs):
    import concourse.bacc as bacc
    from concourse.bass_utils import run_bass_kernel_spmd

    arrays = lay_out({k: np.asarray(v) for k, v in inputs.items()})
    nc = bacc.Bacc("TRN2", target_bir_lowering=False, num_devices=1)
    d = {k: nc.dram_tensor(k, v.shape, mybir.dt.from_np(v.dtype), kind="ExternalInput").ap()
         for k, v in arrays.items()}
    out = nc.dram_tensor("out", [NTOK, D], F32, kind="ExternalOutput").ap()
    build(nc, d, out)
    r = run_bass_kernel_spmd(nc, [arrays], core_ids=[0])
    return r.results[0]["out"].reshape(B, L, D)
```
